# Optimizing a Trainium2 kernel written in Bass

```python
import numpy as np
import jax
import jax.numpy as jnp

def _softmax(x, axis=-1):
    return jax.nn.softmax(x, axis=axis)

def _gelu(x):
    return jax.nn.gelu(x, approximate=True)

def _silu(x):
    return jax.nn.silu(x)

def _sigmoid(x):
    return jax.nn.sigmoid(x)

def _layernorm(x, axis=-1, eps=1e-05):
    m = jnp.mean(x, axis=axis, keepdims=True)
    v = jnp.var(x, axis=axis, keepdims=True)
    return (x - m) / jnp.sqrt(v + eps)

def _scatter_add(tgt, idx, src, axis=0):
    return tgt.at[idx].add(src)

def _segment_sum(src, seg, n):
    return jax.ops.segment_sum(src, seg, n)
kernel_name = 'mk_sandwich_d2_jaxref_r8_6951f2'

def setup_inputs(seed: int=0):
    np.random.seed(seed)
    _w = jnp.asarray

    def _L0_attn_setup():
        import jax, jax.numpy as jnp
        import numpy as np
        STATE_DIM = 128
        INPUT_DIM = 128
        OUTPUT_DIM = 128
        BATCH = 8
        SEQ = 256
        key = jax.random.key(seed)
        k_x, k_a, k_b, k_w, k_bias = jax.random.split(key, 5)
        x = jax.random.normal(k_x, (BATCH, SEQ, INPUT_DIM), dtype=jnp.float32)
        A = jax.random.uniform(k_a, (STATE_DIM,), dtype=jnp.float32, minval=0.0, maxval=0.99)
        B = jax.random.normal(k_b, (STATE_DIM, INPUT_DIM), dtype=jnp.float32) / np.sqrt(INPUT_DIM)
        W = jax.random.normal(k_w, (OUTPUT_DIM, STATE_DIM), dtype=jnp.float32) / np.sqrt(STATE_DIM)
        b = jax.random.normal(k_bias, (OUTPUT_DIM,), dtype=jnp.float32) * 0.01
        return {'x': x, 'A': A, 'B': B, 'W': W, 'b': b}
    _L0_attn_in = _L0_attn_setup()

    def _L0_ffn_setup():
        import jax, jax.numpy as jnp
        import numpy as np
        DIM = 128
        HEADS = 16
        HD = DIM // HEADS
        M = 32
        E = 4
        K = 2
        HID = 256
        MID = 256
        LB = 0.01
        EPS = 1.1920929e-07

        def _rms(x, w):
            return x * jax.lax.rsqrt(jnp.mean(x * x, axis=-1, keepdims=True) + EPS) * w

        def _gelu(x):
            return jax.nn.gelu(x, approximate=False)
        key = jax.random.key(seed)
        ks = jax.random.split(key, 20)
        d = DIM
        w = lambda k, s: jax.random.normal(k, s, jnp.float32) * 0.02
        return {'x': jax.random.normal(ks[0], (4, 128, d), jnp.float32), 'n1_w': jnp.ones((d,), jnp.float32), 'n2_w': jnp.ones((d,), jnp.float32), 'wq': w(ks[1], (d, d)), 'wk': w(ks[2], (d, d)), 'wv': w(ks[3], (d, d)), 'wo': w(ks[4], (d, d)), 'qn_w': jnp.ones((HD,), jnp.float32), 'kn_w': jnp.ones((HD,), jnp.float32), 'gate_w': w(ks[5], (E, d)), 'e0_up': w(ks[6], (HID, d)), 'e0_down': w(ks[7], (d, HID)), 'e1_w1': w(ks[8], (HID, d)), 'e1_w2': w(ks[9], (HID, d)), 'e1_down': w(ks[10], (d, HID)), 'e2_l1': w(ks[11], (MID, d)), 'e2_l2': w(ks[12], (HID, MID)), 'e2_l3': w(ks[13], (MID, HID)), 'e2_l4': w(ks[14], (d, MID)), 'e3_down': w(ks[15], (d, d)), 'e3_up': w(ks[16], (HID, d)), 'e3_out': w(ks[17], (d, HID))}
    _L0_ffn_in = _L0_ffn_setup()

    def _L1_attn_setup():
        import jax, jax.numpy as jnp
        import numpy as np
        B, T, D_MODEL, STATE = (4, 512, 128, 32)
        LN_EPS = 1e-05

        def _layernorm(x, w, b):
            mu = jnp.mean(x, axis=-1, keepdims=True)
            var = jnp.mean(jnp.square(x - mu), axis=-1, keepdims=True)
            return (x - mu) * jax.lax.rsqrt(var + LN_EPS) * w + b
        key = jax.random.key(seed)
        ks = jax.random.split(key, 8)
        x = jax.random.normal(ks[0], (B, T, D_MODEL), dtype=jnp.float32)
        bound_d = 1.0 / np.sqrt(D_MODEL)
        bound_n = 1.0 / np.sqrt(STATE)
        Wa_w = jax.random.normal(ks[1], (STATE, D_MODEL), dtype=jnp.float32) * 0.02
        Wa_b = jnp.zeros((STATE,), dtype=jnp.float32)
        WB_w = jax.random.normal(ks[2], (STATE, D_MODEL), dtype=jnp.float32) * 0.02
        WB_b = jax.random.uniform(ks[3], (STATE,), jnp.float32, -bound_d, bound_d)
        WC_w = jax.random.normal(ks[4], (D_MODEL, STATE), dtype=jnp.float32) * 0.02
        WC_b = jax.random.uniform(ks[5], (D_MODEL,), jnp.float32, -bound_n, bound_n)
        log_gamma = jnp.asarray(0.0, dtype=jnp.float32)
        D_skip = jax.random.normal(ks[6], (D_MODEL,), dtype=jnp.float32) * 0.01
        ln_w = jnp.ones((D_MODEL,), dtype=jnp.float32)
        ln_b = jnp.zeros((D_MODEL,), dtype=jnp.float32)
        return {'x': x, 'Wa_w': Wa_w, 'Wa_b': Wa_b, 'log_gamma': log_gamma, 'WB_w': WB_w, 'WB_b': WB_b, 'WC_w': WC_w, 'WC_b': WC_b, 'D_skip': D_skip, 'ln_w': ln_w, 'ln_b': ln_b}
    _L1_attn_in = _L1_attn_setup()

    def _L1_ffn_setup():
        import jax, jax.numpy as jnp
        import numpy as np
        DIM = 128
        HIDDEN = 384
        SCALE = 1.0 / 127.0

        def _dequant(w_int, dtype):
            return w_int.astype(dtype) * jnp.asarray(SCALE, dtype)
        key = jax.random.key(seed)
        k_x, k_g, k_u, k_d = jax.random.split(key, 4)
        x = jax.random.normal(k_x, (4, 256, DIM), dtype=jnp.float32)
        w_gate = jax.random.randint(k_g, (HIDDEN, DIM), -127, 128, dtype=jnp.int32)
        w_up = jax.random.randint(k_u, (HIDDEN, DIM), -127, 128, dtype=jnp.int32)
        w_down = jax.random.randint(k_d, (DIM, HIDDEN), -127, 128, dtype=jnp.int32)
        return {'x': x, 'w_gate': w_gate, 'w_up': w_up, 'w_down': w_down}
    _L1_ffn_in = _L1_ffn_setup()
    _d = {'L0_attn_x': _L0_attn_in['x'], 'L0_attn_A': _L0_attn_in['A'], 'L0_attn_B': _L0_attn_in['B'], 'L0_attn_W': _L0_attn_in['W'], 'L0_attn_b': _L0_attn_in['b'], 'L0_ffn_n1_w': _L0_ffn_in['n1_w'], 'L0_ffn_n2_w': _L0_ffn_in['n2_w'], 'L0_ffn_wq': _L0_ffn_in['wq'], 'L0_ffn_wk': _L0_ffn_in['wk'], 'L0_ffn_wv': _L0_ffn_in['wv'], 'L0_ffn_wo': _L0_ffn_in['wo'], 'L0_ffn_qn_w': _L0_ffn_in['qn_w'], 'L0_ffn_kn_w': _L0_ffn_in['kn_w'], 'L0_ffn_gate_w': _L0_ffn_in['gate_w'], 'L0_ffn_e0_up': _L0_ffn_in['e0_up'], 'L0_ffn_e0_down': _L0_ffn_in['e0_down'], 'L0_ffn_e1_w1': _L0_ffn_in['e1_w1'], 'L0_ffn_e1_w2': _L0_ffn_in['e1_w2'], 'L0_ffn_e1_down': _L0_ffn_in['e1_down'], 'L0_ffn_e2_l1': _L0_ffn_in['e2_l1'], 'L0_ffn_e2_l2': _L0_ffn_in['e2_l2'], 'L0_ffn_e2_l3': _L0_ffn_in['e2_l3'], 'L0_ffn_e2_l4': _L0_ffn_in['e2_l4'], 'L0_ffn_e3_down': _L0_ffn_in['e3_down'], 'L0_ffn_e3_up': _L0_ffn_in['e3_up'], 'L0_ffn_e3_out': _L0_ffn_in['e3_out'], 'L1_attn_Wa_w': _L1_attn_in['Wa_w'], 'L1_attn_Wa_b': _L1_attn_in['Wa_b'], 'L1_attn_log_gamma': _L1_attn_in['log_gamma'], 'L1_attn_WB_w': _L1_attn_in['WB_w'], 'L1_attn_WB_b': _L1_attn_in['WB_b'], 'L1_attn_WC_w': _L1_attn_in['WC_w'], 'L1_attn_WC_b': _L1_attn_in['WC_b'], 'L1_attn_D_skip': _L1_attn_in['D_skip'], 'L1_attn_ln_w': _L1_attn_in['ln_w'], 'L1_attn_ln_b': _L1_attn_in['ln_b'], 'L1_ffn_w_gate': _L1_ffn_in['w_gate'], 'L1_ffn_w_up': _L1_ffn_in['w_up'], 'L1_ffn_w_down': _L1_ffn_in['w_down']}
    _x0 = _d['L0_attn_x']
    _d['L0_attn_x'] = jax.random.normal(jax.random.fold_in(jax.random.key(seed), 1), (16, 512, 128), dtype=_x0.dtype)
    del _x0
    return _d

def reference(L0_attn_x, L0_attn_A, L0_attn_B, L0_attn_W, L0_attn_b, L0_ffn_n1_w, L0_ffn_n2_w, L0_ffn_wq, L0_ffn_wk, L0_ffn_wv, L0_ffn_wo, L0_ffn_qn_w, L0_ffn_kn_w, L0_ffn_gate_w, L0_ffn_e0_up, L0_ffn_e0_down, L0_ffn_e1_w1, L0_ffn_e1_w2, L0_ffn_e1_down, L0_ffn_e2_l1, L0_ffn_e2_l2, L0_ffn_e2_l3, L0_ffn_e2_l4, L0_ffn_e3_down, L0_ffn_e3_up, L0_ffn_e3_out, L1_attn_Wa_w, L1_attn_Wa_b, L1_attn_log_gamma, L1_attn_WB_w, L1_attn_WB_b, L1_attn_WC_w, L1_attn_WC_b, L1_attn_D_skip, L1_attn_ln_w, L1_attn_ln_b, L1_ffn_w_gate, L1_ffn_w_up, L1_ffn_w_down):

    def _L0_attn_ref(x, A, B, W, b):
        import jax, jax.numpy as jnp
        import numpy as np
        STATE_DIM = 128
        INPUT_DIM = 128
        OUTPUT_DIM = 128
        BATCH = 8
        SEQ = 256
        u = jnp.einsum('bld,nd->bln', x, B)
        aa = jnp.broadcast_to(A, u.shape)

        def combine(c1, c2):
            a1, b1 = c1
            a2, b2 = c2
            return (a1 * a2, a2 * b1 + b2)
        _, h = jax.lax.associative_scan(combine, (aa, u), axis=1)
        return jnp.einsum('bln,on->blo', h, W) + b

    def _L0_ffn_ref(x, n1_w, n2_w, wq, wk, wv, wo, qn_w, kn_w, gate_w, e0_up, e0_down, e1_w1, e1_w2, e1_down, e2_l1, e2_l2, e2_l3, e2_l4, e3_down, e3_up, e3_out):
        import jax, jax.numpy as jnp
        import numpy as np
        DIM = 128
        HEADS = 16
        HD = DIM // HEADS
        M = 32
        E = 4
        K = 2
        HID = 256
        MID = 256
        LB = 0.01
        EPS = 1.1920929e-07

        def _rms(x, w):
            return x * jax.lax.rsqrt(jnp.mean(x * x, axis=-1, keepdims=True) + EPS) * w

        def _gelu(x):
            return jax.nn.gelu(x, approximate=False)
        B, T, C = x.shape
        h = _rms(x, n1_w)
        heads = lambda w_: (h @ w_.T).reshape(B, T, HEADS, HD).transpose(0, 2, 1, 3)
        q = _rms(heads(wq), qn_w)
        k = _rms(heads(wk), kn_w)
        v = heads(wv)
        scores = jnp.einsum('bhqd,bhkd->bhqk', q, k) * HD ** (-0.5)
        causal = jnp.tril(jnp.ones((T, T), bool))
        scores = jnp.where(causal[None, None], scores, -jnp.inf)
        attn = jax.nn.softmax(scores, axis=-1)
        ao = jnp.einsum('bhqk,bhkd->bhqd', attn, v).transpose(0, 2, 1, 3).reshape(B, T, C) @ wo.T
        ao = ao.at[:, :, :M].set(0.0)
        x = x + ao
        xf = _rms(x, n2_w).reshape(-1, C)
        N = xf.shape[0]
        logits = jnp.nan_to_num(xf @ gate_w.T)
        probs = jax.nn.softmax(logits, axis=-1)
        topv, topi = jax.lax.top_k(probs, K)
        topv = topv / (topv.sum(-1, keepdims=True) + 1e-08)
        wts = jnp.zeros((N, E), x.dtype).at[jnp.arange(N)[:, None], topi].add(topv)
        o0 = _gelu(xf @ e0_up.T) @ e0_down.T
        o1 = jax.nn.silu(xf @ e1_w1.T) * (xf @ e1_w2.T) @ e1_down.T
        o2 = _gelu(_gelu(_gelu(xf @ e2_l1.T) @ e2_l2.T) @ e2_l3.T) @ e2_l4.T
        o3 = _gelu(_gelu(xf @ e3_down.T) @ e3_up.T) @ e3_out.T
        moe = wts[:, 0:1] * o0 + wts[:, 1:2] * o1 + wts[:, 2:3] * o2 + wts[:, 3:4] * o3
        moe = moe.reshape(B, T, C).at[:, :, :M].set(0.0)
        return x + moe

    def _L1_attn_ref(x, Wa_w, Wa_b, log_gamma, WB_w, WB_b, WC_w, WC_b, D_skip, ln_w, ln_b):
        import jax, jax.numpy as jnp
        import numpy as np
        B, T, D_MODEL, STATE = (4, 512, 128, 32)
        LN_EPS = 1e-05

        def _layernorm(x, w, b):
            mu = jnp.mean(x, axis=-1, keepdims=True)
            var = jnp.mean(jnp.square(x - mu), axis=-1, keepdims=True)
            return (x - mu) * jax.lax.rsqrt(var + LN_EPS) * w + b
        residual = x
        xn = _layernorm(x, ln_w, ln_b)
        gamma = jax.nn.sigmoid(log_gamma)
        a = gamma * jnp.tanh(jnp.einsum('btd,nd->btn', xn, Wa_w) + Wa_b)
        a_hat = jnp.fft.fft(a, axis=-1)
        mag = jnp.maximum(jnp.abs(a_hat), 1e-08)
        a_hat = a_hat * jax.nn.sigmoid(2.0 * (1.0 - mag))
        u = jnp.einsum('btd,nd->btn', xn, WB_w) + WB_b
        u_hat = jnp.fft.fft(u, axis=-1)

        def combine(c1, c2):
            a1, b1 = c1
            a2, b2 = c2
            return (a1 * a2, a2 * b1 + b2)
        _, h_hat = jax.lax.associative_scan(combine, (a_hat, u_hat), axis=1)
        h = jnp.real(jnp.fft.ifft(h_hat, axis=-1)).astype(x.dtype)
        y = jnp.einsum('btn,dn->btd', h, WC_w) + WC_b + D_skip * residual
        return y

    def _L1_ffn_ref(x, w_gate, w_up, w_down):
        import jax, jax.numpy as jnp
        import numpy as np
        DIM = 128
        HIDDEN = 384
        SCALE = 1.0 / 127.0

        def _dequant(w_int, dtype):
            return w_int.astype(dtype) * jnp.asarray(SCALE, dtype)
        wg = _dequant(w_gate, x.dtype)
        wu = _dequant(w_up, x.dtype)
        wd = _dequant(w_down, x.dtype)
        gate = jnp.einsum('bsd,hd->bsh', x, wg)
        up = jnp.einsum('bsd,hd->bsh', x, wu)
        h = jax.nn.silu(gate) * up
        return jnp.einsum('bsh,dh->bsd', h, wd)
    x = L0_attn_x
    x = x + _layernorm(_L0_attn_ref(_layernorm(x, axis=-1), L0_attn_A, L0_attn_B, L0_attn_W, L0_attn_b), axis=-1)
    x = x + _layernorm(_L0_ffn_ref(_layernorm(x, axis=-1), L0_ffn_n1_w, L0_ffn_n2_w, L0_ffn_wq, L0_ffn_wk, L0_ffn_wv, L0_ffn_wo, L0_ffn_qn_w, L0_ffn_kn_w, L0_ffn_gate_w, L0_ffn_e0_up, L0_ffn_e0_down, L0_ffn_e1_w1, L0_ffn_e1_w2, L0_ffn_e1_down, L0_ffn_e2_l1, L0_ffn_e2_l2, L0_ffn_e2_l3, L0_ffn_e2_l4, L0_ffn_e3_down, L0_ffn_e3_up, L0_ffn_e3_out), axis=-1)
    x = x + _layernorm(_L1_attn_ref(_layernorm(x, axis=-1), L1_attn_Wa_w, L1_attn_Wa_b, L1_attn_log_gamma, L1_attn_WB_w, L1_attn_WB_b, L1_attn_WC_w, L1_attn_WC_b, L1_attn_D_skip, L1_attn_ln_w, L1_attn_ln_b), axis=-1)
    x = x + _layernorm(_L1_ffn_ref(_layernorm(x, axis=-1), L1_ffn_w_gate, L1_ffn_w_up, L1_ffn_w_down), axis=-1)
    return x

_drawn_inputs = setup_inputs


def setup_inputs(seed=0):
    import zlib

    import numpy as np

    out = dict(_drawn_inputs(seed))
    spreads = {'L0_ffn_n1_w': (1.0, 0.6),
     'L0_ffn_n2_w': (1.0, 0.6),
     'L0_ffn_qn_w': (1.0, 0.6),
     'L0_ffn_kn_w': (1.0, 0.6),
     'L1_attn_Wa_b': (0.0, 0.511),
     'L1_attn_ln_w': (1.0, 0.6),
     'L1_attn_ln_b': (0.0, 0.663)}
    factors = {'L0_attn_b': 8.0,
     'L0_ffn_wq': 8.0,
     'L0_ffn_wk': 8.0,
     'L0_ffn_wv': 8.0,
     'L0_ffn_wo': 8.0,
     'L0_ffn_gate_w': 8.0,
     'L0_ffn_e0_up': 8.0,
     'L0_ffn_e0_down': 8.0,
     'L0_ffn_e1_w1': 8.0,
     'L0_ffn_e1_w2': 8.0,
     'L0_ffn_e1_down': 8.0,
     'L0_ffn_e2_l1': 8.0,
     'L0_ffn_e2_l2': 8.0,
     'L0_ffn_e2_l3': 8.0,
     'L0_ffn_e2_l4': 8.0,
     'L0_ffn_e3_down': 8.0,
     'L0_ffn_e3_up': 8.0,
     'L0_ffn_e3_out': 8.0}
    for name, (base, spread) in spreads.items():
        noise = np.random.default_rng([zlib.crc32(name.encode()), seed]).standard_normal(out[name].shape)
        drawn = base * np.exp(spread * noise) if base else spread * noise
        out[name] = jnp.asarray(drawn.astype(out[name].dtype))
    for name, factor in factors.items():
        out[name] = (out[name] * factor).astype(out[name].dtype)
    return out
```

```python
import math
from contextlib import ExitStack

import numpy as np

import concourse.bass as bass
from concourse import mybir

F32 = mybir.dt.float32
BF16 = mybir.dt.bfloat16
I32 = mybir.dt.int32
ALU = mybir.AluOpType
ACT = mybir.ActivationFunctionType
AX = mybir.AxisListType

P = 128
B, T, D = 16, 512, 128
NT = T // P
TILES = B * NT
LN_EPS = 1e-5
RMS_EPS = 1.1920929e-07
HEADS, HD = 16, 8
PAIRS = HEADS // 2
GROUP = 4
MASKED = 32
WIDE = D - MASKED
STATE = 32
FREQS = STATE // 2
SLOTS = 6
HIDDEN = 384
NEG = -1.0e30
FMAX = 3.4028234663852886e38

_WIDTHS = [("ident", P), ("mask", P), ("headmean", P), ("dft_re", 2 * P), ("dft_im", 2 * P), ("dft_ny", 16),
           ("inv_re", 2 * P), ("inv_im", 2 * P), ("inv_ny", 2 * P), ("earlier", 16)]
COLS, _at = {}, 0
for _name, _w in _WIDTHS:
    COLS[_name] = (_at, _at + _w)
    _at += _w
NCONST = _at


def constant_table():
    c = np.zeros((P, NCONST), np.float64)

    def put(name, a):
        c[:a.shape[0], COLS[name][0]:COLS[name][1]] = a

    put("ident", np.eye(P))
    put("mask", np.where(np.arange(P)[None, :] > np.arange(P)[:, None], NEG, 0.0))
    row = np.arange(P)
    same = (row[:, None] // 64 == row[None, :] // 64) & (row[:, None] % PAIRS == row[None, :] % PAIRS)
    put("headmean", same / HD)
    n, f = np.arange(STATE)[:, None], np.arange(FREQS)[None, :]
    turn = 2 * np.pi * ((n * f) % STATE) / STATE
    alt = (-1.0) ** np.arange(STATE)
    re, im = np.cos(turn), -np.sin(turn)
    twice = np.where(f == 0, 1.0, 2.0) / STATE
    dre, dim = np.zeros((P, 2, P)), np.zeros((P, 2, P))
    ire, iim = np.zeros((P, 2, P)), np.zeros((P, 2, P))
    dny, iny = np.zeros((P, 2, 8)), np.zeros((8, 2, P))
    for half in range(2):
        for j in range(4):
            rows, cols = slice(STATE * j, STATE * (j + 1)), slice(FREQS * (4 * half + j), FREQS * (4 * half + j + 1))
            dre[rows, half, cols], dim[rows, half, cols] = re, im
            ire[cols, half, rows], iim[cols, half, rows] = (re * twice).T, (im * twice).T
            dny[rows, half, 4 * half + j] = alt
            iny[4 * half + j, half, rows] = alt / STATE
    put("dft_re", dre.reshape(P, -1)), put("dft_im", dim.reshape(P, -1)), put("dft_ny", dny.reshape(P, -1))
    put("inv_re", ire.reshape(P, -1)), put("inv_im", iim.reshape(P, -1)), put("inv_ny", iny.reshape(8, -1))
    e = np.arange(4)
    put("earlier", np.tile((e[None, :] < e[:, None]).astype(float).reshape(1, 16), (P, 1)))
    return c.astype(np.float32)


def in_twos(eng, first, second):
    first(0, 0)
    with eng.Fori(0, B // 2 - 1) as i:
        first(i, 1)
        second(i, 0)
        first(i + 1, 0)
        second(i, 1)
    last = B // 2 - 1
    first(last, 1)
    second(last, 0)
    second(last, 1)


def tiles(buf, b):
    return buf[:, bass.ds(b * NT, NT), :]


def per_tile(stat):
    return stat.unsqueeze(2).to_broadcast([P, NT, D])


def layer_stats(nc, dve, src, stats, moments):
    for t in range(NT):
        nc.vector.bn_stats(stats[:, t, :], src[:, t, :])
    dve.drain()
    for t in range(NT):
        nc.vector.bn_aggr(moments[:, t, :], stats[:, t, :])
    dve.drain()


def build(nc, io):
    with ExitStack() as whole:
        def sb(name, shape, dt=F32, ctx=whole):
            return ctx.enter_context(nc.sbuf_tensor(name, shape, dt))

        X = sb("X", [P, TILES, D])
        XL = sb("XL", [P, TILES, D])
        const = sb("const", [P, NCONST])
        ident = const[:, COLS["ident"][0]:COLS["ident"][1]]
        minus_half = sb("minus_half", [P, 16])
        bank = [whole.enter_context(nc.psum_tensor(f"bank{n}", [P, 512], F32)) for n in range(8)]
        stack = nc.dram_tensor("qk_stack", (B, 2, 2, SLOTS, HD * PAIRS, T), BF16, kind="Internal").ap()
        values = nc.dram_tensor("v_ones", (B, P, NT * HEADS * (HD + 1)), F32, kind="Internal").ap()
        common = dict(scratch=(stack, values), nc=nc, io=io, X=X, XL=XL, const=const, ident=ident, minus_half=minus_half, bank=bank)
        for phase in PHASES:
            with ExitStack() as ctx:
                phase(ctx=ctx, sb=lambda name, shape, dt=F32, ctx=ctx: sb(name, shape, dt, ctx),
                      sem=lambda name, ctx=ctx: ctx.enter_context(nc.semaphore(name)), **common)


def const_part(const, name, rows=P):
    return const[0:rows, COLS[name][0]:COLS[name][1]]


def bcast_rows(ap, n=P):
    return ap.rearrange("(a n) -> a n", a=1).to_broadcast([n, ap.shape[0]])


def column(ap):
    return ap.rearrange("(n a) -> n a", a=1)


def first_layer(nc, io, X, XL, const, ident, minus_half, bank, ctx, sb, sem, scratch):
    BT, WT = sb("s1_BT", [P, P]), sb("s1_WT", [P, P])
    Acol, Arow = sb("s1_A", [P, 1]), sb("s1_Abc", [P, T])
    bias = sb("s1_bias", [P, D])
    stats, moments = sb("s1_stats", [P, NT, 6]), sb("s1_moments", [P, NT, 2])
    ve, rstd = sb("s1_ve", [P, 2, NT]), sb("s1_rstd", [P, 2, NT])
    xl, y, z = sb("s1_xl", [P, NT, D]), sb("s1_y", [P, NT, D]), sb("s1_z", [P, 2, NT, D])
    stats2, moments2 = sb("s1_stats2", [P, NT, 6]), sb("s1_moments2", [P, NT, 2])
    xT, h = sb("s1_xT", [P, T]), sb("s1_h", [P, T])
    loaded, x_in = sem("s1_loaded"), [sem(f"s1_x{n}") for n in range(4)]
    filled = sem("s1_filled")
    var1, rstd1, var2, rstd2 = sem("s1_var1"), sem("s1_rstd1"), sem("s1_var2"), sem("s1_rstd2")
    xl_ready, turned, xT_ready, u_ready = sem("s1_xl_ready"), sem("s1_turned"), sem("s1_xT_ready"), sem("s1_u_ready")
    h_ready, y_ready, z_ready, added = sem("s1_h_ready"), sem("s1_y_ready"), sem("s1_z_ready"), sem("s1_added")
    y_taken = sem("s1_y_taken")
    xT_bank, u_bank, y_bank = bank[0], bank[1], bank[2]
    x_dram = io["x"].rearrange("b (t p) f -> p (b t) f", p=P)
    PIECE = TILES // 4

    with nc.Block() as block:
        @block.sync
        def _(sp):
            sp.dma_start(const[:, :], io["consts"][:, :]).then_inc(loaded, 16)
            for n in range(4):
                sp.dma_start(X[:, n * PIECE:(n + 1) * PIECE, :], x_dram[:, n * PIECE:(n + 1) * PIECE, :]).then_inc(x_in[n], 16)
                if n == 0:
                    sp.dma_start(BT[:, :], io["BT"][:, :]).then_inc(loaded, 16)
                    sp.dma_start(WT[:, :], io["WT"][:, :]).then_inc(loaded, 16)
                    sp.dma_start(Acol[:, :], column(io["A"])).then_inc(loaded, 16)
                    sp.dma_start(bias[:, :], bcast_rows(io["b"])).then_inc(loaded, 16)

        @block.vector
        def _(dve):
            nc.vector.memset(minus_half[:, :], -0.5).then_inc(filled, 1)
            dve.wait_ge(loaded, 80)
            nc.vector.tensor_copy(Arow[:, :], Acol[:, :].to_broadcast([P, T]))
            dve.wait_ge(x_in[0], 16)

            def normalise(i, p):
                b = 2 * i + p
                layer_stats(nc, dve, tiles(X, b), stats, moments)
                nc.vector.tensor_scalar(ve[:, 0, :], moments[:, :, 1], LN_EPS, None, ALU.add).then_inc(var1, 1)
                dve.wait_ge(rstd1, b + 1)
                dve.wait_ge(turned, b)
                for t in range(NT):
                    last = nc.vector.tensor_scalar(xl[:, t, :], X[:, b * NT + t, :], moments[:, t, 0:1], rstd[:, 0, t:t + 1],
                                                   ALU.subtract, ALU.mult)
                last.then_inc(xl_ready, 1)
                dve.drain()

            def scan_and_add(i, p):
                b = 2 * i + p
                dve.wait_ge(u_ready, b + 1)
                nc.vector.tensor_tensor_scan(h[:, :], Arow[:, :], u_bank[:, :], 0.0, ALU.mult, ALU.add).then_inc(h_ready, 1)
                dve.wait_ge(y_ready, b + 1)
                nc.vector.tensor_tensor(y[:, :, :], y_bank[:, :].rearrange("p (t f) -> p t f", t=NT),
                                        bias[:, :].unsqueeze(1).to_broadcast([P, NT, D]), ALU.add).then_inc(y_taken, 1)
                dve.drain()
                layer_stats(nc, dve, y, stats2, moments2)
                nc.vector.tensor_scalar(ve[:, 1, :], moments2[:, :, 1], LN_EPS, None, ALU.add).then_inc(var2, 1)
                dve.wait_ge(rstd2, b + 1)
                for t in range(NT):
                    last = nc.vector.tensor_scalar(z[:, p, t, :], y[:, t, :], moments2[:, t, 0:1], rstd[:, 1, t:t + 1],
                                                   ALU.subtract, ALU.mult)
                last.then_inc(z_ready, 1)
                dve.drain()

            for n in range(1, 4):
                dve.wait_ge(x_in[n], 16)
            in_twos(dve, normalise, scan_and_add)

        @block.gpsimd
        def _(pool):
            pool.wait_ge(filled, 1)

            def invert(i, p):
                b = 2 * i + p
                pool.wait_ge(var1, b + 1)
                nc.gpsimd.tensor_tensor(rstd[:, 0, :], ve[:, 0, :], minus_half[:, 0:NT], ALU.pow).then_inc(rstd1, 1)

            def add(i, p):
                b = 2 * i + p
                pool.wait_ge(var2, b + 1)
                nc.gpsimd.tensor_tensor(rstd[:, 1, :], ve[:, 1, :], minus_half[:, 0:NT], ALU.pow).then_inc(rstd2, 1)
                pool.wait_ge(z_ready, b + 1)
                nc.gpsimd.tensor_tensor(tiles(X, b), tiles(X, b), z[:, p, :, :], ALU.add).then_inc(added, 1)

            in_twos(pool, invert, add)

        @block.scalar
        def _(act):
            def copy_xT(i, p):
                b = 2 * i + p
                act.wait_ge(turned, b + 1)
                act.wait_ge(u_ready, b)
                nc.scalar.activation(xT[:, :], xT_bank[:, :], ACT.Copy).then_inc(xT_ready, 1)

            in_twos(act, copy_xT, lambda i, p: None)

        @block.tensor
        def _(pe):
            pe.wait_ge(loaded, 80)

            def project(i, p):
                b = 2 * i + p
                pe.wait_ge(xl_ready, b + 1)
                pe.wait_ge(xT_ready, b)
                for t in range(NT):
                    last = nc.tensor.transpose(xT_bank[:, t * P:(t + 1) * P], xl[:, t, :], ident)
                last.then_inc(turned, 1)
                pe.wait_ge(xT_ready, b + 1)
                pe.wait_ge(h_ready, b)
                nc.tensor.matmul(u_bank[:, :], BT[:, :], xT[:, :], start=True, stop=True).then_inc(u_ready, 1)

            def output(i, p):
                b = 2 * i + p
                pe.wait_ge(h_ready, b + 1)
                pe.wait_ge(y_taken, b)
                for t in range(NT):
                    last = nc.tensor.matmul(y_bank[:, t * P:(t + 1) * P], h[:, t * P:(t + 1) * P], WT[:, :], start=True, stop=True)
                last.then_inc(y_ready, 1)

            in_twos(pe, project, output)


ROWS = SLOTS * HD * 2
SHIFTED = ROWS + 6
Q_PARTS = (0, 0, 0, 1, 1, 2)
K_PARTS = (0, 1, 2, 0, 1, 0)


def qkv_layer(nc, io, X, XL, const, ident, minus_half, bank, ctx, sb, sem, scratch):
    Wq, Wk, Wv = sb("q_Wq", [P, D]), sb("q_Wk", [P, D]), sb("q_Wv", [P, D])
    cols = sb("q_cols", [P, 4])
    stats, moments = sb("q_stats", [P, NT, 6]), sb("q_moments", [P, NT, 2])
    ve, rstd = sb("q_ve", [P, 2, NT]), sb("q_rstd", [P, 2, NT])
    h, hT = sb("q_h", [P, NT, D]), sb("q_hT", [P, T])
    sq, rr, qn, rest = sb("q_sq", [P, 2, T]), sb("q_rr", [P, 2, T]), sb("q_qn", [P, 2, T]), sb("q_rest", [P, 2, T])
    parts = sb("q_parts", [P, 2, 3, 2, T], BF16)
    v1 = sb("q_v1", [P, 2, NT, HEADS, HD + 1])
    loaded, filled = sem("q_loaded"), sem("q_filled")
    names = "var rstd h_ready turned hT_ready qk_ready v_ready sq_ready mean_ready rr_ready qn_ready high_ready rest_ready mid_ready low_ready v1_ready"
    var1, rstd1, h_ready, turned, hT_ready, qk_ready, v_ready, sq_ready, mean_ready, rr_ready, qn_ready, high_ready, rest_ready, \
        mid_ready, low_ready, v1_ready = (sem("q_" + x) for x in names.split())
    stored = [sem("q_stored0"), sem("q_stored1")]
    hT_bank, q_bank, k_bank, v_bank, mean_bank = bank[0], bank[1], bank[2], bank[3], bank[4:6]
    headmean = const_part(const, "headmean")
    stack, values = scratch
    PER_BATCH = 13 * 16

    with nc.Block() as block:
        @block.sync
        def _(sp):
            for dst, name in ((Wq, "WqT"), (Wk, "WkT"), (Wv, "WvT")):
                sp.dma_start(dst[:, :], io[name][:, :]).then_inc(loaded, 16)
            for n, name in enumerate(("n1_w", "qn_w", "kn_w")):
                sp.dma_start(cols[:, n:n + 1], column(io[name])).then_inc(loaded, 16)

            def store(i, p):
                b = 2 * i + p
                sp.wait_ge(low_ready, b + 1)
                sp.wait_ge(mid_ready, b + 1)
                for par in range(2):
                    rows = slice(par * 64, par * 64 + 64)
                    for qk, slots in ((0, ((0, 3, None), (3, 2, None), (5, 1, None))), (1, ((0, 3, 0), (3, 2, 0), (5, 1, 0)))):
                        for s0, n, _ in slots:
                            if qk == 0:
                                part = Q_PARTS[s0]
                                src = parts[rows, p, part:part + 1, 0, :].to_broadcast([64, n, T])
                            else:
                                src = parts[rows, p, 0:n, 1, :]
                            dst = stack[bass.ds(b, 1), qk, par, s0:s0 + n, :, :].rearrange("a s r n -> (a r) s n")
                            sp.dma_start(dst, src).then_inc(stored[p], 16)
                sp.wait_ge(v1_ready, b + 1)
                sp.dma_start(values[bass.ds(b, 1), :, :].rearrange("a p n -> (a p) n"),
                             v1[:, p, :, :, :].rearrange("p t h d -> p (t h d)")).then_inc(stored[p], 16)

            in_twos(sp, store, lambda i, p: None)
            for s in stored:
                sp.wait_ge(s, B // 2 * PER_BATCH)

        @block.vector
        def _(dve):
            nc.vector.memset(cols[:, 3:4], RMS_EPS)
            nc.vector.memset(v1[:, :, :, :, HD:HD + 1].rearrange("p a t h d -> p (a t h) d"), 1.0).then_inc(filled, 1)
            dve.wait_ge(loaded, 96)

            def normalise(i, p):
                b = 2 * i + p
                layer_stats(nc, dve, tiles(X, b), stats, moments)
                nc.vector.tensor_scalar(ve[:, 0, :], moments[:, :, 1], LN_EPS, None, ALU.add)
                nc.vector.tensor_scalar(ve[:, 1, :], moments[:, :, 1], 1.0 + RMS_EPS, LN_EPS * RMS_EPS, ALU.mult,
                                        ALU.add).then_inc(var1, 1)
                dve.wait_ge(rstd1, b + 1)
                dve.wait_ge(turned, b)
                for t in range(NT):
                    nc.vector.tensor_scalar(XL[:, b * NT + t, :], X[:, b * NT + t, :], moments[:, t, 0:1], rstd[:, 0, t:t + 1],
                                            ALU.subtract, ALU.mult)
                    last = nc.vector.tensor_scalar(h[:, t, :], X[:, b * NT + t, :], moments[:, t, 0:1], rstd[:, 1, t:t + 1],
                                                   ALU.subtract, ALU.mult)
                last.then_inc(h_ready, 1)
                dve.drain()

            def split(i, p):
                b = 2 * i + p
                dve.wait_ge(v_ready, b + 1)
                dve.wait_ge(stored[p], i * PER_BATCH)
                nc.vector.tensor_copy(v1[:, p, :, :, 0:HD], v_bank[:, :].rearrange("p (t h d) -> p t h d", t=NT, h=HEADS)).then_inc(v1_ready, 1)
                dve.wait_ge(rr_ready, b + 1)
                nc.vector.scalar_tensor_tensor(qn[:, 0, :], q_bank[:, :], cols[:, 1:2], rr[:, 0, :], ALU.mult, ALU.mult)
                nc.vector.scalar_tensor_tensor(qn[:, 1, :], k_bank[:, :], cols[:, 2:3], rr[:, 1, :], ALU.mult,
                                               ALU.mult).then_inc(qn_ready, 1)
                dve.wait_ge(high_ready, b + 1)
                nc.vector.tensor_tensor(rest[:, :, :], qn[:, :, :], parts[:, p, 0, :, :], ALU.subtract).then_inc(rest_ready, 1)
                dve.wait_ge(mid_ready, b + 1)
                nc.vector.tensor_tensor(parts[:, p, 2, :, :], rest[:, :, :], parts[:, p, 1, :, :], ALU.subtract).then_inc(low_ready, 1)
                dve.drain()

            in_twos(dve, normalise, split)

        @block.gpsimd
        def _(pool):
            def invert(i, p):
                b = 2 * i + p
                pool.wait_ge(var1, b + 1)
                nc.gpsimd.tensor_tensor(rstd[:, :, :], ve[:, :, :], minus_half[:, 0:2 * NT].rearrange("p (a t) -> p a t", a=2),
                                        ALU.pow).then_inc(rstd1, 1)

            in_twos(pool, invert, lambda i, p: None)

        @block.scalar
        def _(act):
            act.wait_ge(loaded, 96)
            act.wait_ge(filled, 1)

            def copy_hT(i, p):
                b = 2 * i + p
                act.wait_ge(turned, b + 1)
                act.wait_ge(v_ready, b)
                nc.scalar.activation(hT[:, :], hT_bank[:, :], ACT.Copy, scale=cols[:, 0:1]).then_inc(hT_ready, 1)

            def norms(i, p):
                b = 2 * i + p
                act.wait_ge(qk_ready, b + 1)
                nc.scalar.activation(sq[:, 0, :], q_bank[:, :], ACT.Square)
                nc.scalar.activation(sq[:, 1, :], k_bank[:, :], ACT.Square).then_inc(sq_ready, 1)
                act.wait_ge(mean_ready, b + 1)
                for n in range(2):
                    nc.scalar.activation(rr[:, n, :], mean_bank[n][:, :], ACT.Ln, bias=cols[:, 3:4])
                act.drain()
                nc.scalar.activation(rr[:, :, :], rr[:, :, :], ACT.Exp, scale=-0.5).then_inc(rr_ready, 1)
                act.wait_ge(qn_ready, b + 1)
                nc.scalar.activation(parts[:, p, 0, :, :], qn[:, :, :], ACT.Copy).then_inc(high_ready, 1)
                act.wait_ge(rest_ready, b + 1)
                nc.scalar.activation(parts[:, p, 1, :, :], rest[:, :, :], ACT.Copy).then_inc(mid_ready, 1)

            in_twos(act, copy_hT, norms)

        @block.tensor
        def _(pe):
            pe.wait_ge(loaded, 96)

            def turn(i, p):
                b = 2 * i + p
                pe.wait_ge(h_ready, b + 1)
                pe.wait_ge(hT_ready, b)
                for t in range(NT):
                    last = nc.tensor.transpose(hT_bank[:, t * P:(t + 1) * P], h[:, t, :], ident)
                last.then_inc(turned, 1)

            def project(i, p):
                b = 2 * i + p
                pe.wait_ge(hT_ready, b + 1)
                pe.wait_ge(qn_ready, b)
                nc.tensor.matmul(q_bank[:, :], Wq[:, :], hT[:, :], start=True, stop=True)
                nc.tensor.matmul(k_bank[:, :], Wk[:, :], hT[:, :], start=True, stop=True).then_inc(qk_ready, 1)
                pe.wait_ge(v1_ready, b)
                for t in range(NT):
                    last = nc.tensor.matmul(v_bank[:, t * P:(t + 1) * P], hT[:, t * P:(t + 1) * P], Wv[:, :], start=True, stop=True)
                last.then_inc(v_ready, 1)
                pe.wait_ge(sq_ready, b + 1)
                pe.wait_ge(rr_ready, b)
                for n in range(2):
                    last = nc.tensor.matmul(mean_bank[n][:, :], headmean, sq[:, n, :], start=True, stop=True)
                last.then_inc(mean_ready, 1)

            in_twos(pe, turn, project)


SCORE_UNITS = [(0, (h,)) for h in range(4)] + [(1, (h,)) for h in range(4)] + [(2, (0, 1)), (2, (2, 3)), (3, (0, 1, 2, 3))]
MAX_UNITS = [(0, (0, 1, 2, 3)), (1, (0, 1)), (1, (2, 3))] + [(2, (h,)) for h in range(4)] + [(3, (h,)) for h in range(4)]
UNITS = len(SCORE_UNITS)
GROUPS = HEADS // GROUP
SCORES = UNITS * GROUPS
LAST_OF_TILE = {max(k for k, u in enumerate(SCORE_UNITS) if u[0] == kt): kt for kt in range(NT)}


def order_of_work():
    for g in range(GROUPS):
        for k in range(UNITS):
            yield "score", g, k
            yield "max", g, k
            if g and k == 1:
                yield "values", g - 1, 2
            if g and k == 4:
                yield "values", g - 1, 3
            if g and k == 8:
                yield "turn", g - 1, 0
            if k == 7:
                yield "values", g, 0
            if k == 10:
                yield "values", g, 1
            if g == 2 and k == 6:
                yield "shift", 0, 0
    yield "values", 3, 2
    yield "values", 3, 3
    yield "turn", 3, 0
    yield "project", 0, 0
    yield "shift", 1, 0


def attention_layer(nc, io, X, XL, const, ident, minus_half, bank, ctx, sb, sem, scratch):
    stack, values = scratch
    Q, K = sb("a_Q", [P, 2, PAIRS, T], BF16), sb("a_K", [P, 2, HEADS, T], BF16)
    V = sb("a_V", [P, 2, NT, HEADS, HD + 1])
    Wo = sb("a_Wo", [P, WIDE])
    identb, maskb = sb("a_identb", [P, P], BF16), sb("a_maskb", [P, P], BF16)
    E = [sb(f"a_E{kt}", [P, GROUP, T - P * kt]) for kt in range(NT)]
    neg = sb("a_neg", [P, NT, 2, PAIRS])
    nb, nr = sb("a_nb", [P, 2, NT, 2, 4], BF16), sb("a_nr", [P, NT, 2, 4])
    nparts = sb("a_nparts", [P, NT, 3, 2, 4])
    shiftT = sb("a_shiftT", [24, T], BF16)
    outT, inv = sb("a_outT", [P, T]), sb("a_inv", [P, NT * GROUP])
    ao, aoT = sb("a_ao", [P, NT, D]), sb("a_aoT", [P, T])
    loaded, prepared = sem("a_loaded"), sem("a_prepared")
    stacked = [[sem(f"a_stacked{p}{hf}") for hf in range(2)] for p in range(2)]
    v_in = [sem("a_v_in0"), sem("a_v_in1")]
    score_ready, exp_done, kept = sem("a_score_ready"), sem("a_exp_done"), sem("a_kept")
    max_ready, max_taken, nparts_ready, shift_turned = sem("a_max_ready"), sem("a_max_taken"), sem("a_nparts"), sem("a_shift_turned")
    shift_copied, shift_in = sem("a_shift_copied"), [sem("a_shift_in0"), sem("a_shift_in1")]
    pv_done, outT_ready, turned, ao_ready = sem("a_pv_done"), sem("a_outT_ready"), sem("a_turned"), sem("a_ao_ready")
    ao_turned, aoT_ready, wo_ready, wo_taken = sem("a_ao_turned"), sem("a_aoT_ready"), sem("a_wo_ready"), sem("a_wo_taken")
    pool_tick = sem("a_pool_tick")
    score_bank, max_bank, pv_bank, turn_bank, misc_bank = bank[0:3], bank[3:5], bank[5], bank[6], bank[7]
    SCALE = float(HD) ** -0.5
    n_pv = GROUPS * NT

    def stack_count(b, p):
        return ((b + p) // 2 + 1) * 64 if isinstance(b, int) else (b - p) * 32 + 64 * (p + 1)

    def v_count(b, p):
        return (b // 2 + 1) * 16 if isinstance(b, int) else (b - p) * 8 + 16

    def run(eng, step):
        for g in range(GROUPS):
            for k in range(UNITS):
                step("max", g, k, -1, 1)
            if g == 1:
                step("shift", 0, 0, -1, 1)
        step("shift", 1, 0, -1, 1)
        with eng.Fori(0, B // 2 - 1) as i:
            for p in range(2):
                for kind, g, k in order_of_work():
                    step(kind, g, k, 2 * i + p, p)
        for b in (B - 2, B - 1):
            for kind, g, k in order_of_work():
                if b < B - 1 or kind not in ("max", "shift"):
                    step(kind, g, k, b, b % 2)

    with nc.Block() as block:
        @block.sync
        def _(sp):
            sp.dma_start(Wo[:, :], io["WoT"][:, :]).then_inc(loaded, 16)
            sp.wait_ge(prepared, 3)

            def load(b, p):
                for hf in range(2):
                    pairs = slice(4 * hf, 4 * hf + 4)
                    if not (isinstance(b, int) and b < 2):
                        sp.wait_ge(score_ready, (b - 2) * SCORES + (hf + 1) * SCORES // 2)
                    for par in range(2):
                        rows = slice(par * SLOTS * HD, (par + 1) * SLOTS * HD)
                        src = stack[bass.ds(b, 1), :, par, :, :, :].rearrange("a c s (d r) n -> c (a s d) r n", r=PAIRS)
                        sp.dma_start(Q[rows, p, pairs, :], src[0, :, pairs, :]).then_inc(stacked[p][hf], 16)
                        sp.dma_start(K[rows, p, 8 * hf + par:8 * hf + 8:2, :], src[1, :, pairs, :]).then_inc(stacked[p][hf], 16)
                if not (isinstance(b, int) and b < 2):
                    sp.wait_ge(pv_done, (b - 1) * n_pv)
                sp.dma_start(V[:, p, :, :, :].rearrange("p t h d -> p (t h d)"),
                             values[bass.ds(b, 1), :, :].rearrange("a p n -> (a p) n")).then_inc(v_in[p], 16)

            load(0, 0)
            load(1, 1)
            with sp.Fori(0, B // 2 - 1) as i:
                for p in range(2):
                    load(2 * i + p + 2, p)

        @block.tensor
        def _(pe):
            pe.wait_ge(loaded, 16)
            pe.wait_ge(prepared, 5)

            def step(kind, g, k, b, p):
                m, mp = b + 1, 1 - p
                im = (m - mp) // 2 if isinstance(m, int) else None
                if kind == "score":
                    n = g * UNITS + k
                    kt, heads = SCORE_UNITS[k]
                    if k == 0 and g % 2 == 0:
                        pe.wait_ge(shift_in[g // 2], (b + 1) * 96)
                    if n >= 3:
                        pe.wait_ge(exp_done, b * SCORES + n - 2)
                    wide = T - P * kt
                    for x, j in enumerate(heads):
                        h = GROUP * g + j
                        last = nc.tensor.matmul(score_bank[n % 3][:, x * wide:(x + 1) * wide], K[0:SHIFTED, p, h, kt * P:(kt + 1) * P],
                                                Q[0:SHIFTED, p, h // 2, kt * P:T], start=True, stop=True)
                    last.then_inc(score_ready, 1)
                if kind == "max":
                    n = g * UNITS + k
                    qt, heads = MAX_UNITS[k]
                    if k == 0 and g % 2 == 0:
                        pe.wait_ge(stacked[mp][g // 2], stack_count(b, p))
                    pe.wait_ge(max_taken, m * SCORES + max(n - 1, 0))
                    wide = P * (qt + 1)
                    for x, j in enumerate(heads):
                        h = GROUP * g + j
                        at = x * wide
                        nc.tensor.matmul(max_bank[n % 2][:, at:at + wide], Q[0:ROWS, mp, h // 2, qt * P:(qt + 1) * P],
                                         K[0:ROWS, mp, h, 0:wide], start=True, stop=False)
                        last = nc.tensor.matmul(max_bank[n % 2][:, at + wide - P:at + wide], identb[:, :], maskb[:, :],
                                                start=False, stop=True)
                    last.then_inc(max_ready, 1)
                if kind == "values":
                    kt = k
                    pe.wait_ge(kept, b * n_pv + g * NT + kt + 1)
                    if kt == 0:
                        pe.wait_ge(outT_ready, b * GROUPS + g)
                        if g == 0:
                            pe.wait_ge(v_in[p], v_count(b, p))
                    for j in range(GROUP):
                        last = nc.tensor.matmul(pv_bank[32 * j:32 * j + HD + 1, kt * P:T], V[:, p, kt, GROUP * g + j, :], E[kt][:, j, :],
                                                start=(kt == 0), stop=(kt == NT - 1))
                    last.then_inc(pv_done, 1)
                if kind == "turn":
                    pe.wait_ge(outT_ready, b * GROUPS + g + 1)
                    if g:
                        pe.wait_ge(ao_ready, b * GROUPS + g)
                    else:
                        pe.wait_ge(aoT_ready, b)
                    for t in range(NT):
                        last = nc.tensor.transpose(turn_bank[:, t * P:(t + 1) * P], outT[:, t * P:(t + 1) * P], ident)
                    last.then_inc(turned, 1)
                if kind == "project":
                    pe.wait_ge(ao_ready, (b + 1) * GROUPS)
                    for t in range(NT):
                        last = nc.tensor.transpose(turn_bank[:, t * P:(t + 1) * P], ao[:, t, :], ident)
                    last.then_inc(ao_turned, 1)
                    pe.wait_ge(aoT_ready, b + 1)
                    pe.wait_ge(shift_copied, 2 * m if isinstance(b, int) and m == B else 2 * m + 1)
                    for t in range(NT):
                        last = nc.tensor.matmul(misc_bank[:, t * WIDE:(t + 1) * WIDE], aoT[:, t * P:(t + 1) * P], Wo[:, :],
                                                start=True, stop=True)
                    last.then_inc(wo_ready, 1)
                if kind == "shift":
                    pe.wait_ge(nparts_ready, 2 * m + g + 1)
                    if g == 0:
                        pe.wait_ge(shift_copied, 2 * m)
                    elif isinstance(b, int) and b < 0:
                        pe.wait_ge(shift_copied, 1)
                    else:
                        pe.wait_ge(wo_taken, b + 1)
                    for t in range(NT):
                        last = nc.tensor.transpose(misc_bank[0:24, t * P:(t + 1) * P], nparts[:, t, :, :, :].rearrange("p a r c -> p (a r c)"), ident)
                    last.then_inc(shift_turned, 1)

            run(pe, step)

        @block.scalar
        def _(act):
            act.wait_ge(prepared, 5)

            def step(kind, g, k, b, p):
                m, mp = b + 1, 1 - p
                if kind == "score":
                    n = g * UNITS + k
                    kt, heads = SCORE_UNITS[k]
                    act.wait_ge(score_ready, b * SCORES + n + 1)
                    if g:
                        act.wait_ge(pv_done, b * n_pv + (g - 1) * NT + kt + 1)
                    wide = T - P * kt
                    nc.scalar.activation(E[kt][:, heads[0]:heads[-1] + 1, :],
                                         score_bank[n % 3][:, 0:len(heads) * wide].rearrange("p (h q) -> p h q", q=wide),
                                         ACT.Exp, scale=SCALE).then_inc(exp_done, 1)
                if kind == "values" and k == NT - 1:
                    act.wait_ge(pv_done, b * n_pv + g * NT + NT)
                    act.wait_ge(turned, b * GROUPS + g)
                    nc.scalar.activation(outT[:, :], pv_bank[:, :], ACT.Copy).then_inc(outT_ready, 1)
                if kind == "project":
                    act.wait_ge(ao_turned, b + 1)
                    nc.scalar.activation(aoT[:, :], turn_bank[:, :], ACT.Copy).then_inc(aoT_ready, 1)
                if kind == "shift":
                    act.wait_ge(shift_turned, 2 * m + g + 1)
                    act.wait_ge(shift_in[1 - g], m * 96 if g == 0 else (m + 1) * 96)
                    nc.scalar.activation(shiftT[:, :], misc_bank[0:24, :], ACT.Copy).then_inc(shift_copied, 1)
                    act.wait_ge(shift_copied, 2 * m + g + 1)
                    for part in range(3):
                        for par in range(2):
                            row = ROWS + 3 * par + part
                            act.dma_start(Q[row:row + 1, mp, 4 * g:4 * g + 4, :],
                                          shiftT[part * 8 + par * 4:part * 8 + par * 4 + 4, :]).then_inc(shift_in[g], 16)

            run(act, step)

        @block.vector
        def _(dve):
            nc.vector.memset(K[:, :, :, :].bitcast(F32), 0.0)
            nc.vector.memset(pv_bank[:, :], 0.0).then_inc(prepared, 1)
            dve.drain()
            for par in range(2):
                heads = K[:, :, par:HEADS:2, :]
                if par == 0:
                    nc.vector.memset(heads[ROWS:ROWS + 3], 1.0).then_inc(prepared, 1)
                else:
                    nc.vector.memset(heads[ROWS:ROWS + 6], 1.0)
                    dve.drain()
                    nc.vector.memset(heads[ROWS:ROWS + 3], 0.0).then_inc(prepared, 1)
            nc.vector.tensor_copy(identb[:, :], ident).then_inc(prepared, 1)
            nc.vector.tensor_copy(maskb[:, :], const_part(const, "mask")).then_inc(prepared, 1)
            dve.drain()

            def step(kind, g, k, b, p):
                m = b + 1
                if kind == "max":
                    n = g * UNITS + k
                    qt, heads = MAX_UNITS[k]
                    dve.wait_ge(max_ready, m * SCORES + n + 1)
                    if k == 0:
                        dve.wait_ge(nparts_ready, 2 * m)
                    wide, h0, nh = P * (qt + 1), GROUP * g + heads[0], len(heads)
                    src = max_bank[n % 2][:, 0:nh * wide].rearrange("p (h q) -> p h q", q=wide)
                    if nh == 1:
                        dst = neg[:, qt, h0 % 2, h0 // 2:h0 // 2 + 1]
                    elif nh == 2:
                        dst = neg[:, qt, 0:2, h0 // 2]
                    else:
                        dst = neg[:, qt, :, h0 // 2:h0 // 2 + 2].rearrange("p r a -> p a r")
                        src = src.rearrange("p (a r) q -> p a r q", r=2)
                    nc.vector.tensor_reduce(out=dst, in_=src, axis=AX.X, op=ALU.max, negate=True).then_inc(max_taken, 1)
                if kind == "turn":
                    dve.wait_ge(turned, b * GROUPS + g + 1)
                    o = turn_bank[:, :].rearrange("p (n c) -> p n c", c=32)
                    nc.vector.reciprocal(inv[:, :], o[:, :, HD])
                    dve.drain()
                    nc.vector.tensor_tensor(ao[:, :, 32 * g:32 * g + 32].rearrange("p t (j d) -> p t j d", d=HD),
                                            o[:, :, 0:HD].rearrange("p (t j) d -> p t j d", t=NT),
                                            inv[:, :].rearrange("p (t j) -> p t j", t=NT).unsqueeze(3).to_broadcast([P, NT, GROUP, HD]),
                                            ALU.mult).then_inc(ao_ready, 1)
                    dve.drain()
                if kind == "project":
                    dve.wait_ge(wo_ready, b + 1)
                    dst = XL[:, bass.ds(b * NT, NT), MASKED:D]
                    nc.vector.tensor_tensor(dst, misc_bank[:, 0:NT * WIDE].rearrange("p (t f) -> p t f", t=NT), dst, ALU.add).then_inc(wo_taken, 1)

            run(dve, step)

        @block.gpsimd
        def _(pool):
            pool.wait_ge(prepared, 5)

            def step(kind, g, k, b, p):
                m = b + 1
                if kind == "score" and k in LAST_OF_TILE:
                    kt = LAST_OF_TILE[k]
                    pool.wait_ge(exp_done, b * SCORES + g * UNITS + k + 1)
                    pool.sem_inc(pool_tick, 1)
                    nc.gpsimd.affine_select(out=E[kt][:, :, 0:P], in_=E[kt][:, :, 0:P], compare_op=ALU.is_ge, fill=0.0, base=0,
                                            pattern=[[0, GROUP], [1, P]], channel_multiplier=-1).then_inc(kept, 1)
                if kind == "max" and g % 2 == 1 and k == UNITS - 1:
                    hf = g // 2
                    pool.wait_ge(max_taken, m * SCORES + (g + 1) * UNITS)
                    pool.wait_ge(shift_turned, 2 * m + hf)
                    pool.sem_inc(pool_tick, 1)
                    src = neg[:, :, :, 4 * hf:4 * hf + 4]
                    nc.gpsimd.tensor_copy(nb[:, 0, :, :, :], src)
                    pool.drain()
                    nc.gpsimd.tensor_copy(nparts[:, :, 0, :, :], nb[:, 0, :, :, :])
                    nc.gpsimd.tensor_tensor(nr[:, :, :, :], src, nb[:, 0, :, :, :], ALU.subtract)
                    pool.drain()
                    nc.gpsimd.tensor_copy(nb[:, 1, :, :, :], nr[:, :, :, :])
                    pool.drain()
                    nc.gpsimd.tensor_copy(nparts[:, :, 1, :, :], nb[:, 1, :, :, :])
                    nc.gpsimd.tensor_tensor(nparts[:, :, 2, :, :], nr[:, :, :, :], nb[:, 1, :, :, :], ALU.subtract).then_inc(nparts_ready, 1)
                    pool.drain()

            run(pool, step)


EXPERTS = 4
HC2 = 2
MOE_ORDER = [("up", "e0u", "x", 1, 2), ("up", "e1a", "x", 1, 2), ("up", "e1b", "x", 1, 2), ("up", "e2a", "x", 1, 2),
             ("out", 0), ("up", "e3a", "x", 1, 1), ("up", "e2b", "G1", 2, 2), ("out", 1), ("up", "e3b", "G3", 1, 2),
             ("up", "e2c", "G2", 2, 2), ("out", 3), ("out", 2)]
MOE_UPS = [s for s in MOE_ORDER if s[0] == "up"]
MOE_OUTS = [s[1] for s in MOE_ORDER if s[0] == "out"]
MOE_TO = {"e0u": "H0", "e1a": "S1", "e1b": "H1", "e2a": "G1", "e3a": "G3", "e2b": "G2", "e3b": "H3", "e2c": "G4"}
MOE_LAST = {0: "H0", 1: "H1", 2: "G4", 3: "H3"}


def expert_layer(nc, io, X, XL, const, ident, minus_half, bank, ctx, sb, sem, scratch):
    W = {name: sb(f"e_{name}", [P, n, HC2 * P if name != "e3a" else P]) for name, n in
         (("e0u", 1), ("e1a", 1), ("e1b", 1), ("e2a", 1), ("e2b", 2), ("e2c", 2), ("e3a", 1), ("e3b", 1))}
    down = sb("e_down", [P, EXPERTS, HC2, WIDE])
    gate = sb("e_gate", [P, EXPERTS])
    n2w = sb("e_n2w", [P, 1])
    stats, moments = sb("e_stats", [P, NT, 6]), sb("e_moments", [P, NT, 2])
    stats2, moments2 = sb("e_stats2", [P, NT, 6]), sb("e_moments2", [P, NT, 2])
    ve, rstd = sb("e_ve", [P, 2, NT]), sb("e_rstd", [P, 2, NT])
    xf, z = sb("e_xf", [P, NT, D]), sb("e_z", [P, 2, NT, D])
    xfT = sb("e_xfT", [P, 2, T])
    hid = {name: sb(f"e_{name}", [P, 1 if name == "G3" else HC2, T]) for name in ("H0", "S1", "H1", "G1", "G2", "G3", "G4", "H3")}
    euler = sb("e_euler", [P, NT * EXPERTS])
    lg, part, pr, tv = (sb(f"e_{x}", [P, NT, EXPERTS]) for x in ("lg", "part", "pr", "tv"))
    top, cmp1, cmp2 = sb("e_top", [P, NT]), sb("e_cmp1", [P, NT, EXPERTS, EXPERTS]), sb("e_cmp2", [P, NT, EXPERTS, EXPERTS])
    wts = sb("e_wts", [P, 2, NT, EXPERTS])
    loaded, filled = sem("e_loaded"), sem("e_filled")
    names = "var1 rstd1 var2 rstd2 xf_ready turned xfT_ready logits_ready logits_taken diff_ready exp_ready up_ready act_done mul_done out_ready out_taken z_ready added"
    (var1, rstd1, var2, rstd2, xf_ready, turned, xfT_ready, logits_ready, logits_taken, diff_ready, exp_ready, up_ready, act_done,
     mul_done, out_ready, out_taken, z_ready, added) = (sem("e_" + x) for x in names.split())
    xT_bank, logit_bank, out_bank = bank[0], bank[1], bank[6:8]
    up_banks = (bank[2:4], bank[4:6])
    n_up, n_act = len(MOE_UPS), len(MOE_UPS) - 1
    up_at = {s[1]: n for n, s in enumerate(MOE_UPS)}
    act_at = {s[1]: n for n, s in enumerate(s for s in MOE_UPS if s[1] != "e1b")}
    LOADS = len(W) + 4 + 2 + 1

    def up_free(eng, n, b):
        if n < 2:
            return
        name = MOE_UPS[n - 2][1]
        if name == "e1b":
            eng.wait_ge(mul_done, b + 1)
        else:
            eng.wait_ge(act_done, b * n_act + act_at[name] + 1)

    def made(eng, name, b):
        if name == "H1":
            eng.wait_ge(mul_done, b + 1)
        elif name != "x":
            src = [k for k, v in MOE_TO.items() if v == name][0]
            eng.wait_ge(act_done, b * n_act + act_at[src] + 1)

    with nc.Block() as block:
        @block.sync
        def _(sp):
            for name, w in W.items():
                sp.dma_start(w[:, :, :], io[name + "T"].rearrange("(c p) f -> p c f", p=P)).then_inc(loaded, 16)
            for e in range(EXPERTS):
                n = 1 if io[f"d{e}T"].shape[0] == P else 2
                sp.dma_start(down[:, e, 0:n, :], io[f"d{e}T"].rearrange("(c p) f -> p c f", p=P)).then_inc(loaded, 16)
            sp.dma_start(gate[:, :], io["gateT"][:, :]).then_inc(loaded, 16)
            sp.dma_start(n2w[:, :], column(io["n2_w"])).then_inc(loaded, 16)

        @block.tensor
        def _(pe):
            pe.wait_ge(loaded, 16 * (len(W) + EXPERTS + 2))

            def turn(i, p):
                b = 2 * i + p
                pe.wait_ge(xf_ready, b + 1)
                pe.wait_ge(xfT_ready, b)
                for t in range(NT):
                    last = nc.tensor.transpose(xT_bank[:, t * P:(t + 1) * P], xf[:, t, :], ident)
                last.then_inc(turned, 1)
                pe.wait_ge(xfT_ready, b + 1)
                pe.wait_ge(logits_taken, b)
                for t in range(NT):
                    last = nc.tensor.matmul(logit_bank[:, t * EXPERTS:(t + 1) * EXPERTS], xfT[:, p, t * P:(t + 1) * P], gate[:, :],
                                            start=True, stop=True)
                last.then_inc(logits_ready, 1)

            def experts(i, p):
                b = 2 * i + p
                n_out = 0
                for step in MOE_ORDER:
                    if step[0] == "up":
                        _, name, src, n_in, n_chunks = step
                        n = up_at[name]
                        up_free(pe, n, b)
                        made(pe, src, b)
                        for c in range(n_chunks):
                            for k in range(n_in):
                                rhs = xfT[:, p, :] if src == "x" else hid[src][:, k, :]
                                last = nc.tensor.matmul(up_banks[n % 2][c][:, :], W[name][:, k, c * P:(c + 1) * P], rhs,
                                                        start=(k == 0), stop=(k == n_in - 1))
                        last.then_inc(up_ready, 1)
                    else:
                        e = step[1]
                        made(pe, MOE_LAST[e], b)
                        pe.wait_ge(out_taken, b * EXPERTS + max(n_out - 1, 0))
                        for t in range(NT):
                            for k in range(HC2):
                                last = nc.tensor.matmul(out_bank[n_out % 2][:, t * WIDE:(t + 1) * WIDE],
                                                        hid[MOE_LAST[e]][:, k, t * P:(t + 1) * P], down[:, e, k, :],
                                                        start=(k == 0), stop=(k == HC2 - 1))
                        last.then_inc(out_ready, 1)
                        n_out += 1

            in_twos(pe, turn, experts)

        @block.scalar
        def _(act):
            act.wait_ge(loaded, 16 * (len(W) + EXPERTS + 2))

            def copy_xfT(i, p):
                b = 2 * i + p
                act.wait_ge(turned, b + 1)
                nc.scalar.activation(xfT[:, p, :], xT_bank[:, :], ACT.Copy, scale=n2w[:, 0:1]).then_inc(xfT_ready, 1)

            def functions(i, p):
                b = 2 * i + p
                for n, (_, name, _, _, n_chunks) in enumerate(MOE_UPS):
                    if name == "e1b":
                        continue
                    act.wait_ge(up_ready, b * n_up + n + 1)
                    dst = hid[MOE_TO[name]]
                    if name == "e0u":
                        act.wait_ge(out_ready, b * EXPERTS)
                    if name == "e1a":
                        act.wait_ge(mul_done, b)
                    for c in range(n_chunks):
                        last = nc.scalar.activation(dst[:, c, :], up_banks[n % 2][c][:, :], ACT.Silu if name == "e1a" else ACT.Gelu)
                    last.then_inc(act_done, 1)

            in_twos(act, copy_xfT, functions)

        @block.gpsimd
        def _(pool):
            nc.gpsimd.memset(euler[:, :], math.e)
            pool.drain()

            def front(i, p):
                b = 2 * i + p
                pool.wait_ge(var1, b + 1)
                nc.gpsimd.tensor_tensor(rstd[:, 0, :], ve[:, 0, :], minus_half[:, 0:NT], ALU.pow).then_inc(rstd1, 1)
                pool.wait_ge(diff_ready, b + 1)
                nc.gpsimd.tensor_tensor(pr[:, :, :].rearrange("p t e -> p (t e)"), euler[:, :],
                                        part[:, :, :].rearrange("p t e -> p (t e)"), ALU.pow).then_inc(exp_ready, 1)

            def add(i, p):
                b = 2 * i + p
                pool.wait_ge(var2, b + 1)
                nc.gpsimd.tensor_tensor(rstd[:, 1, :], ve[:, 1, :], minus_half[:, 0:NT], ALU.pow).then_inc(rstd2, 1)
                pool.wait_ge(z_ready, b + 1)
                nc.gpsimd.tensor_tensor(tiles(X, b), tiles(X, b), z[:, p, :, :], ALU.add).then_inc(added, 1)

            in_twos(pool, front, add)

        @block.vector
        def _(dve):
            earlier = const_part(const, "earlier").rearrange("p (i j) -> p i j", i=EXPERTS)

            def front(i, p):
                b = 2 * i + p
                layer_stats(nc, dve, tiles(XL, b), stats, moments)
                nc.vector.tensor_tensor(top[:, :], moments[:, :, 0], moments[:, :, 0], ALU.mult)
                dve.drain()
                nc.vector.scalar_tensor_tensor(ve[:, 0, :], moments[:, :, 1], RMS_EPS, top[:, :], ALU.add, ALU.add).then_inc(var1, 1)
                dve.wait_ge(rstd1, b + 1)
                dve.wait_ge(turned, b)
                for t in range(NT):
                    last = nc.vector.tensor_scalar(xf[:, t, :], XL[:, b * NT + t, :], rstd[:, 0, t:t + 1], None, ALU.mult)
                last.then_inc(xf_ready, 1)
                dve.drain()

            def gating(i, p):
                b = 2 * i + p
                dve.wait_ge(logits_ready, b + 1)
                raw = logit_bank[:, 0:NT * EXPERTS].rearrange("p (t e) -> p t e", e=EXPERTS)
                nc.vector.tensor_scalar(lg[:, :, :], raw, 0.0, FMAX, ALU.max, ALU.min)
                nc.vector.tensor_scalar(part[:, :, :], raw, 0.0, -FMAX, ALU.min, ALU.max).then_inc(logits_taken, 1)
                dve.drain()
                nc.vector.tensor_tensor(lg[:, :, :], lg[:, :, :], part[:, :, :], ALU.add)
                dve.drain()
                nc.vector.tensor_reduce(out=top[:, :], in_=lg[:, :, :], axis=AX.X, op=ALU.max)
                dve.drain()
                nc.vector.tensor_tensor(part[:, :, :], lg[:, :, :], top[:, :].unsqueeze(2).to_broadcast([P, NT, EXPERTS]),
                                        ALU.subtract).then_inc(diff_ready, 1)
                dve.wait_ge(exp_ready, b + 1)
                nc.vector.tensor_reduce(out=top[:, :], in_=pr[:, :, :], axis=AX.X, op=ALU.add)
                dve.drain()
                nc.vector.reciprocal(top[:, :], top[:, :])
                dve.drain()
                nc.vector.tensor_tensor(pr[:, :, :], pr[:, :, :], top[:, :].unsqueeze(2).to_broadcast([P, NT, EXPERTS]), ALU.mult)
                dve.drain()
                full = [P, NT, EXPERTS, EXPERTS]
                mine, other = pr[:, :, :].unsqueeze(3).to_broadcast(full), pr[:, :, :].unsqueeze(2).to_broadcast(full)
                nc.vector.tensor_tensor(cmp1[:, :, :, :], other, mine, ALU.is_equal)
                nc.vector.tensor_tensor(cmp2[:, :, :, :], other, mine, ALU.is_gt)
                dve.drain()
                nc.vector.tensor_tensor(cmp1[:, :, :, :], cmp1[:, :, :, :], earlier.unsqueeze(1).to_broadcast(full), ALU.mult)
                dve.drain()
                nc.vector.tensor_tensor(cmp1[:, :, :, :], cmp1[:, :, :, :], cmp2[:, :, :, :], ALU.add)
                dve.drain()
                nc.vector.tensor_reduce(out=tv[:, :, :], in_=cmp1[:, :, :, :], axis=AX.X, op=ALU.add)
                dve.drain()
                nc.vector.scalar_tensor_tensor(tv[:, :, :], tv[:, :, :], 1.5, pr[:, :, :], ALU.is_lt, ALU.mult)
                dve.drain()
                nc.vector.tensor_reduce(out=top[:, :], in_=tv[:, :, :], axis=AX.X, op=ALU.add)
                dve.drain()
                nc.vector.tensor_scalar(top[:, :], top[:, :], 1e-8, None, ALU.add)
                dve.drain()
                nc.vector.reciprocal(top[:, :], top[:, :])
                dve.drain()
                nc.vector.tensor_tensor(wts[:, p, :, :], tv[:, :, :], top[:, :].unsqueeze(2).to_broadcast([P, NT, EXPERTS]), ALU.mult)
                dve.drain()

            def combine(i, p):
                b = 2 * i + p
                n_out = 0
                for step in MOE_ORDER:
                    if step[0] == "up" and step[1] == "e1b":
                        dve.wait_ge(up_ready, b * n_up + up_at["e1b"] + 1)
                        dve.wait_ge(act_done, b * n_act + act_at["e1a"] + 1)
                        for c in range(HC2):
                            last = nc.vector.tensor_tensor(hid["H1"][:, c, :], hid["S1"][:, c, :], up_banks[up_at["e1b"] % 2][c][:, :], ALU.mult)
                        last.then_inc(mul_done, 1)
                    if step[0] == "out":
                        e = step[1]
                        dve.wait_ge(out_ready, b * EXPERTS + n_out + 1)
                        for t in range(NT):
                            acc = XL[:, b * NT + t, MASKED:D]
                            last = nc.vector.scalar_tensor_tensor(acc, out_bank[n_out % 2][:, t * WIDE:(t + 1) * WIDE],
                                                                  wts[:, p, t, e:e + 1], acc, ALU.mult, ALU.add)
                        last.then_inc(out_taken, 1)
                        dve.drain()
                        n_out += 1
                layer_stats(nc, dve, tiles(XL, b), stats2, moments2)
                nc.vector.tensor_scalar(ve[:, 1, :], moments2[:, :, 1], LN_EPS, None, ALU.add).then_inc(var2, 1)
                dve.wait_ge(rstd2, b + 1)
                for t in range(NT):
                    last = nc.vector.tensor_scalar(z[:, p, t, :], XL[:, b * NT + t, :], moments2[:, t, 0:1], rstd[:, 1, t:t + 1],
                                                   ALU.subtract, ALU.mult)
                last.then_inc(z_ready, 1)
                dve.drain()

            def first(i, p):
                front(i, p)
                gating(i, p)

            in_twos(dve, first, combine)


def staged(eng, first, second, count, unroll):
    def after(i, p):
        return (i, p + 1) if p + 1 < unroll else (i + 1, 0)

    trips = count // unroll
    first(0, 0)
    if trips > 1:
        with eng.Fori(0, trips - 1) as i:
            for p in range(unroll):
                first(*after(i, p))
                second(i, p)
    for p in range(unroll):
        if p + 1 < unroll:
            first(trips - 1, p + 1)
        second(trips - 1, p)


CHUNK = 16
CHUNKS = T // CHUNK
SETS = 2


def spectral_layer(nc, io, X, XL, const, ident, minus_half, bank, ctx, sb, sem, scratch):
    WaT, WBT, WCT = sb("s3_WaT", [P, STATE]), sb("s3_WBT", [P, STATE]), sb("s3_WCT", [P, D])
    cols = sb("s3_cols", [P, 6])
    skip_w, out_b = sb("s3_skip_w", [P, D]), sb("s3_out_b", [P, D])
    stats, moments = sb("s3_stats", [P, NT, 6]), sb("s3_moments", [P, NT, 2])
    ve, rstd = sb("s3_ve", [P, 2, NT]), sb("s3_rstd", [P, 2, NT])
    xn, xnT = sb("s3_xn", [P, NT, D]), sb("s3_xnT", [P, T])
    a_in, u_in = sb("s3_a", [P, 4, T]), sb("s3_u", [P, 4, T])
    A = sb("s3_A", [P, 2, SETS, T])
    HP = sb("s3_HP", [P, 4, SETS * CHUNKS, CHUNK])
    squares, mag = sb("s3_squares", [P, 2, SETS, T]), sb("s3_mag", [P, SETS, T])
    An, Un, Hn, gn = (sb(f"s3_{x}", [8, SETS, T]) for x in ("An", "Un", "Hn", "gn"))
    two = sb("s3_two", [P, 1])
    by, ends = sb("s3_by", [P, 3, 4, SETS * CHUNKS]), sb("s3_ends", [P, 2, 4, SETS * CHUNKS])
    loaded, gamma_ready = sem("s3_loaded"), sem("s3_gamma")
    var1, rstd1 = sem("s3_var1"), sem("s3_rstd1")
    xn_ready, turned, xnT_ready, au_ready, au_taken = (sem(f"s3_{x}") for x in ("xn_ready", "turned", "xnT_ready", "au_ready", "au_taken"))
    xnT_bank, a_bank, u_bank = bank[0], bank[1], bank[2]

    with nc.Block() as block:
        @block.sync
        def _(sp):
            sp.dma_start(WaT[:, :], io["WaT"][:, :]).then_inc(loaded, 16)
            sp.dma_start(WBT[:, :], io["WBT"][:, :]).then_inc(loaded, 16)
            sp.dma_start(WCT[:, :], io["WCT4"][:, :]).then_inc(loaded, 16)
            for n, name in enumerate(("ln_w", "ln_b", "Wa_b4", "WB_b4")):
                sp.dma_start(cols[:, n:n + 1], column(io[name])).then_inc(loaded, 16)
            sp.dma_start(cols[:, 4:5], io["log_gamma"].rearrange("(a n) -> a n", a=1).to_broadcast([P, 1])).then_inc(loaded, 16)
            sp.dma_start(skip_w[:, :], bcast_rows(io["D_skip"])).then_inc(loaded, 16)
            sp.dma_start(out_b[:, :], bcast_rows(io["WC_b"])).then_inc(loaded, 16)

        @block.vector
        def _(dve):
            def moments_of(i, p):
                b = 4 * i + p
                layer_stats(nc, dve, tiles(X, b), stats, moments)
                nc.vector.tensor_scalar(ve[:, 0, :], moments[:, :, 1], LN_EPS, None, ALU.add)
                nc.vector.tensor_scalar(ve[:, 1, :], moments[:, :, 1], 1.0 + LN_EPS, LN_EPS * LN_EPS, ALU.mult,
                                        ALU.add).then_inc(var1, 1)
                dve.wait_ge(rstd1, b + 1)
                dve.wait_ge(turned, b)
                for t in range(NT):
                    nc.vector.tensor_scalar(XL[:, b * NT + t, :], X[:, b * NT + t, :], moments[:, t, 0:1], rstd[:, 0, t:t + 1],
                                            ALU.subtract, ALU.mult)
                    last = nc.vector.tensor_scalar(xn[:, t, :], X[:, b * NT + t, :], moments[:, t, 0:1], rstd[:, 1, t:t + 1],
                                                   ALU.subtract, ALU.mult)
                last.then_inc(xn_ready, 1)
                dve.drain()

            def times_gamma(i, p):
                if p == 3:
                    dve.wait_ge(au_taken, i + 1)
                    if isinstance(i, int):
                        dve.wait_ge(gamma_ready, 1)
                    nc.vector.tensor_scalar(a_in[:, i, :], a_in[:, i, :], cols[:, 5:6], None, ALU.mult)

            dve.wait_ge(gamma_ready, 1)
            staged(dve, moments_of, times_gamma, B, 4)

        @block.gpsimd
        def _(pool):
            def invert(i, p):
                b = 4 * i + p
                pool.wait_ge(var1, b + 1)
                nc.gpsimd.tensor_tensor(rstd[:, :, :], ve[:, :, :], minus_half[:, 0:2 * NT].rearrange("p (a t) -> p a t", a=2),
                                        ALU.pow).then_inc(rstd1, 1)

            staged(pool, invert, lambda i, p: None, B, 4)

        @block.scalar
        def _(act):
            act.wait_ge(loaded, 160)
            nc.scalar.activation(cols[:, 5:6], cols[:, 4:5], ACT.Sigmoid).then_inc(gamma_ready, 1)

            def copy_xnT(i, p):
                b = 4 * i + p
                act.wait_ge(turned, b + 1)
                act.wait_ge(au_ready, b)
                nc.scalar.activation(xnT[:, :], xnT_bank[:, :], ACT.Identity, scale=cols[:, 0:1], bias=cols[:, 1:2]).then_inc(xnT_ready, 1)

            def take(i, p):
                if p == 3:
                    act.wait_ge(au_ready, 4 * i + 4)
                    nc.scalar.activation(u_in[:, i, :], u_bank[:, :], ACT.Identity, bias=cols[:, 3:4])
                    nc.scalar.activation(a_in[:, i, :], a_bank[:, :], ACT.Tanh, bias=cols[:, 2:3]).then_inc(au_taken, 1)

            staged(act, copy_xnT, take, B, 4)

        @block.tensor
        def _(pe):
            pe.wait_ge(loaded, 160)

            def turn(i, p):
                b = 4 * i + p
                pe.wait_ge(xn_ready, b + 1)
                pe.wait_ge(xnT_ready, b)
                for t in range(NT):
                    last = nc.tensor.transpose(xnT_bank[:, t * P:(t + 1) * P], xn[:, t, :], ident)
                last.then_inc(turned, 1)

            def project(i, p):
                b = 4 * i + p
                pe.wait_ge(xnT_ready, b + 1)
                pe.wait_ge(au_taken, i)
                rows = slice(STATE * p, STATE * (p + 1))
                nc.tensor.matmul(a_bank[rows, :], WaT[:, :], xnT[:, :], start=True, stop=True)
                nc.tensor.matmul(u_bank[rows, :], WBT[:, :], xnT[:, :], start=True, stop=True).then_inc(au_ready, 1)

            staged(pe, turn, project, B, 4)

    spec_ready, spec_taken, squared, mag2_ready = sem("s3_spec_ready"), sem("s3_spec_taken"), sem("s3_squared"), sem("s3_mag2")
    mag_ready, clamped, gate_ready = sem("s3_mag_ready"), sem("s3_clamped"), sem("s3_gate")
    re, im = const_part(const, "dft_re"), const_part(const, "dft_im")
    ny = const_part(const, "dft_ny")
    hp_h = HP[:, :, :, :].rearrange("p (c k) m s -> p c k (m s)", c=2)
    with nc.Block() as block:
        @block.tensor
        def _(pe):
            for n, (src, mat) in enumerate(((a_in, re), (a_in, im), (u_in, re), (u_in, im))):
                for s in range(SETS):
                    for half in range(2):
                        last = nc.tensor.matmul(bank[2 * n + s][:, :], mat[:, half * P:(half + 1) * P], src[:, 2 * s + half, :],
                                                start=(half == 0), stop=(half == 1))
                    last.then_inc(spec_ready, 1)
            for n, src in enumerate((a_in, u_in)):
                for s in range(SETS):
                    pe.wait_ge(spec_taken, 2 * n + s + 1)
                    for half in range(2):
                        last = nc.tensor.matmul(bank[2 * n + s][0:8, :], ny[:, half * 8:half * 8 + 8], src[:, 2 * s + half, :],
                                                start=(half == 0), stop=(half == 1))
                    last.then_inc(spec_ready, 1)

        @block.scalar
        def _(act):
            for n in range(4):
                for s in range(SETS):
                    act.wait_ge(spec_ready, 2 * n + s + 1)
                    dst = A[:, n % 2, s, :] if n < 2 else hp_h[:, n % 2, 0, s * T:(s + 1) * T]
                    nc.scalar.activation(dst, bank[2 * n + s][:, :], ACT.Copy).then_inc(spec_taken, 1)
                if n == 1:
                    act.drain()
                    nc.scalar.activation(squares[:, :, :, :], A[:, :, :, :], ACT.Square).then_inc(squared, 1)
            for n, dst in enumerate((An, Un)):
                for s in range(SETS):
                    act.wait_ge(spec_ready, 8 + 2 * n + s + 1)
                    nc.scalar.activation(dst[:, s, :], bank[2 * n + s][0:8, :], ACT.Copy)
            act.drain()
            nc.scalar.activation(gn[:, :, :], An[:, :, :], ACT.Abs)
            act.wait_ge(mag2_ready, 1)
            nc.scalar.activation(mag[:, :, :], squares[:, 0, :, :], ACT.Sqrt).then_inc(mag_ready, 1)
            act.wait_ge(clamped, 1)
            nc.scalar.activation(mag[:, :, :], mag[:, :, :], ACT.Sigmoid, scale=-2.0, bias=two[:, :])
            nc.scalar.activation(gn[:, :, :], gn[:, :, :], ACT.Sigmoid, scale=-2.0, bias=two[0:8, :]).then_inc(gate_ready, 1)


        @block.vector
        def _(dve):
            nc.vector.memset(two[:, :], 2.0)
            nc.vector.memset(HP[:, :, :, :].rearrange("p (c k) m s -> p c k (m s)", c=2)[:, :, 1, :], 0.0)
            dve.wait_ge(squared, 1)
            nc.vector.tensor_tensor(squares[:, 0, :, :], squares[:, 0, :, :], squares[:, 1, :, :], ALU.add).then_inc(mag2_ready, 1)
            dve.wait_ge(mag_ready, 1)
            nc.vector.tensor_scalar(mag[:, :, :], mag[:, :, :], 1e-8, None, ALU.max)
            nc.vector.tensor_scalar(gn[:, :, :], gn[:, :, :], 1e-8, None, ALU.max).then_inc(clamped, 1)
            dve.wait_ge(gate_ready, 1)
            dve.wait_ge(spec_taken, 8)
            for c in range(2):
                nc.vector.tensor_tensor(A[:, c, :, :], A[:, c, :, :], mag[:, :, :], ALU.mult)
            nc.vector.tensor_tensor(An[:, :, :], An[:, :, :], gn[:, :, :], ALU.mult)
            dve.drain()
            for s in range(SETS):
                nc.vector.tensor_tensor_scan(Hn[:, s, :], An[:, s, :], Un[:, s, :], 0.0, ALU.mult, ALU.add)
            Am = A[:, :, :, :].rearrange("p c s (k t) -> p c (s k) t", t=CHUNK)
            M = SETS * CHUNKS
            by_re, by_im, step = by[:, 0, :, :], by[:, 1, :, :], by[:, 2, :, :]

            def times(dst, left_re, left_im, right):
                nc.vector.tensor_tensor(dst[0], left_re, right, ALU.mult)
                nc.vector.tensor_tensor(dst[1], left_im, right, ALU.mult)
                dve.drain()
                nc.vector.tensor_tensor(dst[2][:, 0:2], dst[0][:, 0:2], dst[1][:, 2:4], ALU.subtract)
                nc.vector.tensor_tensor(dst[2][:, 2:4], dst[0][:, 2:4], dst[1][:, 0:2], ALU.add)
                dve.drain()

            for c in range(2):
                nc.vector.tensor_copy(HP[:, 2 * c + 1, :, 0], Am[:, c, :, 0])
            dve.drain()
            for s in range(1, CHUNK):
                times((by_re, by_im, step), Am[:, 0, :, s].unsqueeze(1).to_broadcast([P, 4, M]),
                      Am[:, 1, :, s].unsqueeze(1).to_broadcast([P, 4, M]), HP[:, :, :, s - 1])
                nc.vector.tensor_tensor(HP[:, :, :, s], HP[:, :, :, s], step, ALU.add)
                dve.drain()
            nc.vector.tensor_copy(ends[:, 0, :, :], HP[:, :, :, CHUNK - 1])
            dve.drain()
            now, d = 0, 1
            while d < CHUNKS:
                cur, new = (ends[:, n, :, :].rearrange("p q (s k) -> p q s k", s=SETS) for n in (now, 1 - now))
                n = CHUNKS - d
                v = [by[:, m, :, :].rearrange("p q (s k) -> p q s k", s=SETS)[:, :, :, 0:n] for m in range(3)]
                for s in range(SETS):
                    w = [x[:, :, s, :] for x in v]
                    times(w, cur[:, 1, s, d:].unsqueeze(1).to_broadcast([P, 4, n]),
                          cur[:, 3, s, d:].unsqueeze(1).to_broadcast([P, 4, n]), cur[:, :, s, 0:n])
                for c in range(2):
                    nc.vector.tensor_tensor(new[:, 2 * c, :, d:], cur[:, 2 * c, :, d:], v[2][:, 2 * c], ALU.add)
                    nc.vector.tensor_copy(new[:, 2 * c + 1, :, d:], v[2][:, 2 * c + 1])
                nc.vector.tensor_copy(new[:, :, :, 0:d], cur[:, :, :, 0:d])
                dve.drain()
                now, d = 1 - now, 2 * d
            flat = squares[:, :, :, :].rearrange("p c s (k t) -> p c s k t", t=CHUNK)
            hp5 = HP[:, :, :, :].rearrange("p q (s k) t -> p q s k t", s=SETS)
            carry = ends[:, now, :, :].rearrange("p q (s k) -> p q s k", s=SETS)
            n = CHUNKS - 1
            for c in range(2):
                for half, (x, y) in enumerate(((1, 2 * c), (3, 2 - 2 * c))):
                    nc.vector.tensor_tensor(flat[:, half, :, 1:, :], hp5[:, x, :, 1:, :],
                                            carry[:, y, :, 0:n].unsqueeze(3).to_broadcast([P, SETS, n, CHUNK]), ALU.mult)
                dve.drain()
                nc.vector.tensor_tensor(flat[:, 0, :, 1:, :], flat[:, 0, :, 1:, :], flat[:, 1, :, 1:, :],
                                        ALU.subtract if c == 0 else ALU.add)
                dve.drain()
                nc.vector.tensor_tensor(hp5[:, 2 * c, :, 1:, :], hp5[:, 2 * c, :, 1:, :], flat[:, 0, :, 1:, :], ALU.add)
                dve.drain()


    hT = sb("s3_hT", [P, 2, T])
    y, z, skip = sb("s3_y", [P, NT, D]), sb("s3_z", [P, 2, NT, D]), sb("s3_skip", [P, 2, NT, D])
    stats2, moments2 = sb("s3_stats2", [P, NT, 6]), sb("s3_moments2", [P, NT, 2])
    h_ready, h_taken, y_ready, y_taken = (sem(f"s3_{x}") for x in ("h_ready", "h_taken", "y_ready", "y_taken"))
    skip_ready, var2, rstd2, z_ready, added = (sem(f"s3_{x}") for x in ("skip_ready", "var2", "rstd2", "z_ready", "added"))
    ire, iim, iny = const_part(const, "inv_re"), const_part(const, "inv_im"), const_part(const, "inv_ny", 8)
    h_bank = bank[0:2]
    y_bank = bank[2:4]
    none = lambda i, p: None
    with nc.Block() as block:
        @block.tensor
        def _(pe):
            def states(i, p):
                if p % 4:
                    return
                half = p // 4
                lhs = slice(half * P, (half + 1) * P)
                pe.wait_ge(h_taken, 2 * i + half)
                nc.tensor.matmul(h_bank[half][:, :], ire[:, lhs], hp_h[:, 0, 0, bass.ds(i * T, T)], start=True, stop=False)
                nc.tensor.matmul(h_bank[half][:, :], iim[:, lhs], hp_h[:, 1, 0, bass.ds(i * T, T)], start=False, stop=False)
                nc.tensor.matmul(h_bank[half][:, :], iny[:, lhs], Hn[:, i, :], start=False, stop=True).then_inc(h_ready, 1)

            def output(i, p):
                b, j, half = 8 * i + p, p % 4, p // 4
                if j == 0:
                    pe.wait_ge(h_taken, 2 * i + half + 1)
                pe.wait_ge(y_taken, b)
                rows = slice(STATE * j, STATE * (j + 1))
                for t in range(NT):
                    last = nc.tensor.matmul(y_bank[0][:, t * P:(t + 1) * P], hT[rows, half, t * P:(t + 1) * P], WCT[rows, :],
                                            start=True, stop=True)
                last.then_inc(y_ready, 1)

            staged(pe, states, output, B, 8)

        @block.scalar
        def _(act):
            def take(i, p):
                if p % 4:
                    return
                half = p // 4
                act.wait_ge(h_ready, 2 * i + half + 1)
                act.wait_ge(y_ready, 8 * i + 4 * half)
                nc.scalar.activation(hT[:, half, :], h_bank[half][:, :], ACT.Copy).then_inc(h_taken, 1)

            staged(act, take, none, B, 8)

        @block.gpsimd
        def _(pool):
            def skips(i, p):
                b = 8 * i + p
                if not (isinstance(b, int) and b == 0):
                    pool.wait_ge(y_taken, b - 1)
                nc.gpsimd.tensor_tensor(skip[:, p % 2, :, :], tiles(XL, b), skip_w[:, :].unsqueeze(1).to_broadcast([P, NT, D]), ALU.mult)
                pool.drain()
                nc.gpsimd.tensor_tensor(skip[:, p % 2, :, :], skip[:, p % 2, :, :], out_b[:, :].unsqueeze(1).to_broadcast([P, NT, D]),
                                        ALU.add).then_inc(skip_ready, 1)

            def add(i, p):
                b = 8 * i + p
                pool.wait_ge(var2, b + 1)
                nc.gpsimd.tensor_tensor(rstd[:, 1, :], ve[:, 1, :], minus_half[:, 0:NT], ALU.pow).then_inc(rstd2, 1)
                pool.wait_ge(z_ready, b + 1)
                nc.gpsimd.tensor_tensor(tiles(X, b), tiles(X, b), z[:, p % 2, :, :], ALU.add).then_inc(added, 1)

            staged(pool, skips, add, B, 8)

        @block.vector
        def _(dve):
            def tail(i, p):
                b = 8 * i + p
                dve.wait_ge(y_ready, b + 1)
                dve.wait_ge(skip_ready, b + 1)
                nc.vector.tensor_tensor(y[:, :, :], y_bank[0][:, :].rearrange("p (t f) -> p t f", t=NT), skip[:, p % 2, :, :],
                                        ALU.add).then_inc(y_taken, 1)
                dve.drain()
                layer_stats(nc, dve, y, stats2, moments2)
                nc.vector.tensor_scalar(ve[:, 1, :], moments2[:, :, 1], LN_EPS, None, ALU.add).then_inc(var2, 1)
                dve.wait_ge(rstd2, b + 1)
                for t in range(NT):
                    last = nc.vector.tensor_scalar(z[:, p % 2, t, :], y[:, t, :], moments2[:, t, 0:1], rstd[:, 1, t:t + 1],
                                                   ALU.subtract, ALU.mult)
                last.then_inc(z_ready, 1)
                dve.drain()

            staged(dve, none, tail, B, 8)


def swiglu_layer(nc, io, X, XL, const, ident, minus_half, bank, ctx, sb, sem, scratch):
    HC = HIDDEN // P
    raw = sb("s4_raw", [P, 3, HIDDEN], I32)
    wg, wu, wd = sb("s4_wg", [P, HIDDEN]), sb("s4_wu", [P, HIDDEN]), sb("s4_wd", [P, HC, D])
    stats, moments = sb("s4_stats", [P, NT, 6]), sb("s4_moments", [P, NT, 2])
    stats2, moments2 = sb("s4_stats2", [P, NT, 6]), sb("s4_moments2", [P, NT, 2])
    ve, rstd = sb("s4_ve", [P, 2, NT]), sb("s4_rstd", [P, 2, NT])
    xl, z = sb("s4_xl", [P, NT, D]), sb("s4_z", [P, 2, NT, D])
    xT = sb("s4_xT", [P, 2, T])
    silu, hid = sb("s4_silu", [P, HC, T]), sb("s4_hid", [P, 2, HC, T])
    loaded, scaled = sem("s4_loaded"), sem("s4_scaled")
    var1, rstd1, var2, rstd2 = sem("s4_var1"), sem("s4_rstd1"), sem("s4_var2"), sem("s4_rstd2")
    xl_ready, turned, xT_ready = sem("s4_xl_ready"), sem("s4_turned"), sem("s4_xT_ready")
    gate_ready, up_ready, silu_ready = sem("s4_gate_ready"), sem("s4_up_ready"), sem("s4_silu_ready")
    hid_ready, y_ready, y_taken = sem("s4_hid_ready"), sem("s4_y_ready"), sem("s4_y_taken")
    z_ready, added, stored = sem("s4_z_ready"), sem("s4_added"), sem("s4_stored")
    xT_bank, y_bank = bank[0], bank[1]
    gate_bank, up_bank = bank[2:5], bank[5:8]
    out_dram = io["out"].rearrange("b (t p) f -> p (b t) f", p=P)

    with nc.Block() as block:
        @block.sync
        def _(sp):
            sp.dma_start(raw[:, 0, :], io["w_gateT"][:, :]).then_inc(loaded, 16)
            sp.dma_start(raw[:, 1, :], io["w_upT"][:, :]).then_inc(loaded, 16)
            sp.dma_start(raw[:, 2, :].rearrange("p (c f) -> p c f", c=HC),
                         io["w_downT"].rearrange("(c p) f -> p c f", p=P)).then_inc(loaded, 16)
            with sp.Fori(0, B) as b:
                sp.wait_ge(added, b + 1)
                sp.dma_start(out_dram[:, bass.ds(b * NT, NT), :], tiles(X, b)).then_inc(stored, 16)
            sp.wait_ge(stored, 16 * B)

        @block.vector
        def _(dve):
            dve.wait_ge(loaded, 48)
            scale = float(np.float32(1.0 / 127.0))
            nc.vector.tensor_scalar(wg[:, :], raw[:, 0, :], scale, None, ALU.mult)
            nc.vector.tensor_scalar(wu[:, :], raw[:, 1, :], scale, None, ALU.mult)
            nc.vector.tensor_scalar(wd[:, :, :], raw[:, 2, :].rearrange("p (c f) -> p c f", c=HC), scale, None,
                                    ALU.mult).then_inc(scaled, 1)

            def normalise(i, p):
                b = 2 * i + p
                layer_stats(nc, dve, tiles(X, b), stats, moments)
                nc.vector.tensor_scalar(ve[:, 0, :], moments[:, :, 1], LN_EPS, None, ALU.add).then_inc(var1, 1)
                dve.wait_ge(rstd1, b + 1)
                dve.wait_ge(turned, b)
                for t in range(NT):
                    last = nc.vector.tensor_scalar(xl[:, t, :], X[:, b * NT + t, :], moments[:, t, 0:1], rstd[:, 0, t:t + 1],
                                                   ALU.subtract, ALU.mult)
                last.then_inc(xl_ready, 1)
                dve.drain()

            def gate_and_add(i, p):
                b = 2 * i + p
                for c in range(HC):
                    dve.wait_ge(silu_ready, HC * b + c + 1)
                    dve.wait_ge(up_ready, HC * b + c + 1)
                    nc.vector.tensor_tensor(hid[:, p, c, :], silu[:, c, :], up_bank[c][:, :], ALU.mult).then_inc(hid_ready, 1)
                dve.wait_ge(y_ready, b + 1)
                y = y_bank[:, :].rearrange("p (t f) -> p t f", t=NT)
                layer_stats(nc, dve, y, stats2, moments2)
                nc.vector.tensor_scalar(ve[:, 1, :], moments2[:, :, 1], LN_EPS, None, ALU.add).then_inc(var2, 1)
                dve.wait_ge(rstd2, b + 1)
                for t in range(NT):
                    last = nc.vector.tensor_scalar(z[:, p, t, :], y[:, t, :], moments2[:, t, 0:1], rstd[:, 1, t:t + 1],
                                                   ALU.subtract, ALU.mult)
                last.then_inc(z_ready, 1)
                dve.drain()

            in_twos(dve, normalise, gate_and_add)

        @block.gpsimd
        def _(pool):
            def invert(i, p):
                b = 2 * i + p
                pool.wait_ge(var1, b + 1)
                nc.gpsimd.tensor_tensor(rstd[:, 0, :], ve[:, 0, :], minus_half[:, 0:NT], ALU.pow).then_inc(rstd1, 1)

            def add(i, p):
                b = 2 * i + p
                pool.wait_ge(var2, b + 1)
                nc.gpsimd.tensor_tensor(rstd[:, 1, :], ve[:, 1, :], minus_half[:, 0:NT], ALU.pow).then_inc(rstd2, 1)
                pool.wait_ge(z_ready, b + 1)
                nc.gpsimd.tensor_tensor(tiles(X, b), tiles(X, b), z[:, p, :, :], ALU.add).then_inc(added, 1)

            in_twos(pool, invert, add)

        @block.scalar
        def _(act):
            def copy_xT(i, p):
                b = 2 * i + p
                act.wait_ge(turned, b + 1)
                nc.scalar.activation(xT[:, p, :], xT_bank[:, :], ACT.Copy).then_inc(xT_ready, 1)

            def silus(i, p):
                b = 2 * i + p
                for c in range(HC):
                    act.wait_ge(gate_ready, HC * b + c + 1)
                    act.wait_ge(hid_ready, HC * b)
                    nc.scalar.activation(silu[:, c, :], gate_bank[c][:, :], ACT.Silu).then_inc(silu_ready, 1)

            in_twos(act, copy_xT, silus)

        @block.tensor
        def _(pe):
            pe.wait_ge(scaled, 1)

            def turn(i, p):
                b = 2 * i + p
                pe.wait_ge(xl_ready, b + 1)
                pe.wait_ge(xT_ready, b)
                for t in range(NT):
                    last = nc.tensor.transpose(xT_bank[:, t * P:(t + 1) * P], xl[:, t, :], ident)
                last.then_inc(turned, 1)

            def mlp(i, p):
                b = 2 * i + p
                pe.wait_ge(xT_ready, b + 1)
                for c in range(HC):
                    pe.wait_ge(silu_ready, HC * b)
                    nc.tensor.matmul(gate_bank[c][:, :], wg[:, c * P:(c + 1) * P], xT[:, p, :], start=True,
                                     stop=True).then_inc(gate_ready, 1)
                    pe.wait_ge(hid_ready, HC * b)
                    nc.tensor.matmul(up_bank[c][:, :], wu[:, c * P:(c + 1) * P], xT[:, p, :], start=True,
                                     stop=True).then_inc(up_ready, 1)
                pe.wait_ge(hid_ready, HC * (b + 1))
                pe.wait_ge(z_ready, b)
                for t in range(NT):
                    for c in range(HC):
                        last = nc.tensor.matmul(y_bank[:, t * P:(t + 1) * P], hid[:, p, c, t * P:(t + 1) * P], wd[:, c, :],
                                                start=(c == 0), stop=(c == HC - 1))
                last.then_inc(y_ready, 1)

            in_twos(pe, turn, mlp)


def load_only(nc, io, X, XL, const, ident, minus_half, bank, ctx, sb, sem, scratch):
    l = sem("lo_in")
    with nc.Block() as block:
        @block.sync
        def _(sp):
            sp.dma_start(const[:, :], io["consts"][:, :]).then_inc(l, 16)
            sp.dma_start(X[:, :, :], io["x"].rearrange("b (t p) f -> p (b t) f", p=P)).then_inc(l, 16)
            sp.wait_ge(l, 32)
        @block.vector
        def _(dve):
            nc.vector.memset(minus_half[:, :], -0.5)


def store_only(nc, io, X, XL, const, ident, minus_half, bank, ctx, sb, sem, scratch):
    out_done = sem("so_out")
    with nc.Block() as block:
        @block.sync
        def _(sp):
            sp.dma_start(io["out"].rearrange("b (t p) f -> p (b t) f", p=P), X[:, :, :]).then_inc(out_done, 16)
            sp.wait_ge(out_done, 16)


PHASES = [first_layer, qkv_layer, attention_layer, expert_layer, spectral_layer, swiglu_layer]


def laid_out(v):
    col = np.ascontiguousarray
    t = lambda a: col(np.asarray(a).T)
    a = {k: np.asarray(x) for k, x in v.items()}
    perm = np.array([(2 * pair + par) * HD + d for par in range(2) for d in range(HD) for pair in range(PAIRS)])
    dims = np.array([d for par in range(2) for d in range(HD) for pair in range(PAIRS)])
    return {
        "WqT": t(a["L0_ffn_wq"])[:, perm], "WkT": t(a["L0_ffn_wk"])[:, perm], "WvT": t(a["L0_ffn_wv"]),
        "WoT": t(a["L0_ffn_wo"])[:, MASKED:], "n1_w": a["L0_ffn_n1_w"], "qn_w": a["L0_ffn_qn_w"][dims],
        "kn_w": a["L0_ffn_kn_w"][dims], "n2_w": a["L0_ffn_n2_w"], "gateT": t(a["L0_ffn_gate_w"]),
        "e0uT": t(a["L0_ffn_e0_up"]), "e1aT": t(a["L0_ffn_e1_w1"]), "e1bT": t(a["L0_ffn_e1_w2"]),
        "e2aT": t(a["L0_ffn_e2_l1"]), "e2bT": t(a["L0_ffn_e2_l2"]), "e2cT": t(a["L0_ffn_e2_l3"]),
        "e3aT": t(a["L0_ffn_e3_down"]), "e3bT": t(a["L0_ffn_e3_up"]),
        "d0T": t(a["L0_ffn_e0_down"])[:, MASKED:], "d1T": t(a["L0_ffn_e1_down"])[:, MASKED:],
        "d2T": t(a["L0_ffn_e2_l4"])[:, MASKED:], "d3T": t(a["L0_ffn_e3_out"])[:, MASKED:],
        "x": a["L0_attn_x"], "A": a["L0_attn_A"], "BT": t(a["L0_attn_B"]), "WT": t(a["L0_attn_W"]), "b": a["L0_attn_b"],
        "WaT": t(a["L1_attn_Wa_w"]), "WBT": t(a["L1_attn_WB_w"]), "WCT4": np.tile(t(a["L1_attn_WC_w"]), (4, 1)),
        "ln_w": a["L1_attn_ln_w"], "ln_b": a["L1_attn_ln_b"], "Wa_b4": np.tile(a["L1_attn_Wa_b"], 4),
        "WB_b4": np.tile(a["L1_attn_WB_b"], 4), "log_gamma": a["L1_attn_log_gamma"].reshape(1),
        "D_skip": a["L1_attn_D_skip"], "WC_b": a["L1_attn_WC_b"],
        "w_gateT": t(a["L1_ffn_w_gate"]), "w_upT": t(a["L1_ffn_w_up"]), "w_downT": t(a["L1_ffn_w_down"]),
    }


def kernel(**inputs):
    import numpy as _np
    import concourse.bacc as _bacc
    from concourse import mybir as _mybir
    from concourse.bass_utils import run_bass_kernel_spmd as _run

    nc = _bacc.Bacc("TRN2", target_bir_lowering=False, num_devices=1)
    arrays, io = {}, {}
    for name, a in {**laid_out(inputs), "consts": constant_table()}.items():
        a = _np.ascontiguousarray(a)
        arrays[f"in_{name}"] = a
        io[name] = nc.dram_tensor(f"in_{name}", a.shape, _mybir.dt.from_np(a.dtype), kind="ExternalInput").ap()
    io["out"] = nc.dram_tensor("out_0", (B, T, D), _mybir.dt.float32, kind="ExternalOutput").ap()
    build(nc, io)
    r = _run(nc, [arrays], core_ids=[0])
    return r.results[0]["out_0"]
```

```python
import math
from contextlib import ExitStack

import numpy as np

import concourse.bass as bass
from concourse import mybir

F32 = mybir.dt.float32
BF16 = mybir.dt.bfloat16
I32 = mybir.dt.int32
ALU = mybir.AluOpType
ACT = mybir.ActivationFunctionType
AX = mybir.AxisListType

P = 128
B, T, D = 16, 512, 128
NT = T // P
TILES = B * NT
LN_EPS = 1e-5
RMS_EPS = 1.1920929e-07
HEADS, HD = 16, 8
PAIRS = HEADS // 2
GROUP = 4
MASKED = 32
WIDE = D - MASKED
STATE = 32
FREQS = STATE // 2
SLOTS = 6
HIDDEN = 384
NEG = -1.0e30
FMAX = 3.4028234663852886e38

_WIDTHS = [("ident", P), ("mask", P), ("headmean", P), ("dft_re", 2 * P), ("dft_im", 2 * P), ("dft_ny", 16),
           ("inv_re", 2 * P), ("inv_im", 2 * P), ("inv_ny", 2 * P), ("earlier", 16)]
COLS, _at = {}, 0
for _name, _w in _WIDTHS:
    COLS[_name] = (_at, _at + _w)
    _at += _w
NCONST = _at


def constant_table():
    c = np.zeros((P, NCONST), np.float64)

    def put(name, a):
        c[:a.shape[0], COLS[name][0]:COLS[name][1]] = a

    put("ident", np.eye(P))
    put("mask", np.where(np.arange(P)[None, :] > np.arange(P)[:, None], NEG, 0.0))
    row = np.arange(P)
    same = (row[:, None] // 64 == row[None, :] // 64) & (row[:, None] % PAIRS == row[None, :] % PAIRS)
    put("headmean", same / HD)
    n, f = np.arange(STATE)[:, None], np.arange(FREQS)[None, :]
    turn = 2 * np.pi * ((n * f) % STATE) / STATE
    alt = (-1.0) ** np.arange(STATE)
    re, im = np.cos(turn), -np.sin(turn)
    twice = np.where(f == 0, 1.0, 2.0) / STATE
    dre, dim = np.zeros((P, 2, P)), np.zeros((P, 2, P))
    ire, iim = np.zeros((P, 2, P)), np.zeros((P, 2, P))
    dny, iny = np.zeros((P, 2, 8)), np.zeros((8, 2, P))
    for half in range(2):
        for j in range(4):
            rows, cols = slice(STATE * j, STATE * (j + 1)), slice(FREQS * (4 * half + j), FREQS * (4 * half + j + 1))
            dre[rows, half, cols], dim[rows, half, cols] = re, im
            ire[cols, half, rows], iim[cols, half, rows] = (re * twice).T, (im * twice).T
            dny[rows, half, 4 * half + j] = alt
            iny[4 * half + j, half, rows] = alt / STATE
    put("dft_re", dre.reshape(P, -1)), put("dft_im", dim.reshape(P, -1)), put("dft_ny", dny.reshape(P, -1))
    put("inv_re", ire.reshape(P, -1)), put("inv_im", iim.reshape(P, -1)), put("inv_ny", iny.reshape(8, -1))
    e = np.arange(4)
    put("earlier", np.tile((e[None, :] < e[:, None]).astype(float).reshape(1, 16), (P, 1)))
    return c.astype(np.float32)


def pipeline(eng, depth, *stages, unroll=2):
    lead = -(-(depth + 1) // unroll) * unroll
    def peeled(step):
        for s, work in stages:
            if 0 <= step - s < B:
                work((step - s) // unroll, (step - s) % unroll)
    for step in range(lead):
        peeled(step)
    with eng.Fori(0, (B - lead) // unroll) as i:
        for n in range(unroll):
            for s, work in stages:
                p = (n - s) % unroll
                work(i + (lead + n - s - p) // unroll, p)
    for step in range(B, B + depth - 1):
        peeled(step)


def counted(n):
    return max(n, 0) if isinstance(n, int) else n


def in_twos(eng, first, second):
    first(0, 0)
    with eng.Fori(0, B // 2 - 1) as i:
        first(i, 1)
        second(i, 0)
        first(i + 1, 0)
        second(i, 1)
    last = B // 2 - 1
    first(last, 1)
    second(last, 0)
    second(last, 1)


def tiles(buf, b):
    return buf[:, bass.ds(b * NT, NT), :]


def per_tile(stat):
    return stat.unsqueeze(2).to_broadcast([P, NT, D])


def layer_stats(nc, dve, src, stats, moments):
    for t in range(NT):
        nc.vector.bn_stats(stats[:, t, :], src[:, t, :])
    dve.drain()
    for t in range(NT):
        nc.vector.bn_aggr(moments[:, t, :], stats[:, t, :])
    dve.drain()


def build(nc, io):
    with ExitStack() as whole:
        def sb(name, shape, dt=F32, ctx=whole):
            return ctx.enter_context(nc.sbuf_tensor(name, shape, dt))

        X = sb("X", [P, TILES, D])
        XL = sb("XL", [P, TILES, D])
        const = sb("const", [P, NCONST])
        ident = const[:, COLS["ident"][0]:COLS["ident"][1]]
        minus_half = sb("minus_half", [P, 16])
        bank = [whole.enter_context(nc.psum_tensor(f"bank{n}", [P, 512], F32)) for n in range(8)]
        stack = nc.dram_tensor("qk_parts", (B, 3, 2, P, T), BF16, kind="Internal").ap()
        values = nc.dram_tensor("v_ones", (B, P, NT * HEADS * (HD + 1)), F32, kind="Internal").ap()
        common = dict(scratch=(stack, values), nc=nc, io=io, X=X, XL=XL, const=const, ident=ident, minus_half=minus_half, bank=bank)
        for phase in PHASES:
            with ExitStack() as ctx:
                phase(ctx=ctx, sb=lambda name, shape, dt=F32, ctx=ctx: sb(name, shape, dt, ctx),
                      sem=lambda name, ctx=ctx: ctx.enter_context(nc.semaphore(name)), **common)


def const_part(const, name, rows=P):
    return const[0:rows, COLS[name][0]:COLS[name][1]]


def bcast_rows(ap, n=P):
    return ap.rearrange("(a n) -> a n", a=1).to_broadcast([n, ap.shape[0]])


def column(ap):
    return ap.rearrange("(n a) -> n a", a=1)


def first_layer(nc, io, X, XL, const, ident, minus_half, bank, ctx, sb, sem, scratch):
    BT, WT = sb("s1_BT", [P, P]), sb("s1_WT", [P, P])
    Acol, Arow = sb("s1_A", [P, 1]), sb("s1_Abc", [P, T])
    bias, ones = sb("s1_bias", [1, NT * D]), sb("s1_ones", [1, P])
    stats, moments = sb("s1_stats", [P, NT, 6]), sb("s1_moments", [P, 2, 2, NT, 2])
    ve, rstd = sb("s1_ve", [P, 2, 2, NT]), sb("s1_rstd", [P, 2, 2, NT])
    xl, z = sb("s1_xl", [P, 2, NT, D]), sb("s1_z", [P, 2, NT, D])
    stats2 = sb("s1_stats2", [P, NT, 6])
    xT, h = sb("s1_xT", [P, 2, T]), sb("s1_h", [P, 2, T])
    loaded, x_in = sem("s1_loaded"), [sem(f"s1_x{n}") for n in range(4)]
    filled = sem("s1_filled")
    var1, rstd1, var2, rstd2 = sem("s1_var1"), sem("s1_rstd1"), sem("s1_var2"), sem("s1_rstd2")
    xl_ready, turned, xT_ready, u_ready = sem("s1_xl_ready"), sem("s1_turned"), sem("s1_xT_ready"), sem("s1_u_ready")
    h_ready, y_ready, z_ready, added = sem("s1_h_ready"), sem("s1_y_ready"), sem("s1_z_ready"), sem("s1_added")
    xT_bank, u_bank, y_bank = bank[0:2], bank[2:4], bank[4:6]
    x_dram = io["x"].rearrange("b (t p) f -> p (b t) f", p=P)
    PIECE, LOADS = TILES // 4, 8 * 16
    STAGES, PEELED = 5, 6

    with nc.Block() as block:
        @block.sync
        def _(sp):
            sp.dma_start(const[:, :], io["consts"][:, :]).then_inc(loaded, 16)
            for n in range(4):
                sp.dma_start(X[:, n * PIECE:(n + 1) * PIECE, :], x_dram[:, n * PIECE:(n + 1) * PIECE, :]).then_inc(x_in[n], 16)
                if n == 0:
                    sp.dma_start(BT[:, :], io["BT"][:, :]).then_inc(loaded, 16)
                    sp.dma_start(WT[:, :], io["WT"][:, :]).then_inc(loaded, 16)
                    sp.dma_start(Acol[:, :], column(io["A"])).then_inc(loaded, 16)
                    for t in range(NT):
                        sp.dma_start(bias[:, t * D:(t + 1) * D], io["b"].rearrange("(a f) -> a f", a=1)).then_inc(loaded, 16)

        @block.vector
        def _(dve):
            nc.vector.memset(ones[:, :], 1.0)
            nc.vector.memset(minus_half[:, :], -0.5).then_inc(filled, 1)
            dve.wait_ge(loaded, LOADS)
            nc.vector.tensor_copy(Arow[:, :], Acol[:, :].to_broadcast([P, T]))

            def x_stats(i, p):
                b = 2 * i + p
                if isinstance(b, int):
                    dve.wait_ge(x_in[b * NT // PIECE], 16)
                    if b == PEELED - 1:
                        for n in range(4):
                            dve.wait_ge(x_in[n], 16)
                layer_stats(nc, dve, tiles(X, b), stats, moments[:, p, 0, :, :])
                nc.vector.tensor_scalar(ve[:, p, 0, :], moments[:, p, 0, :, 1], LN_EPS, None, ALU.add).then_inc(var1, 1)
                dve.drain()

            def normalise(i, p):
                b = 2 * i + p
                dve.wait_ge(rstd1, b + 1)
                dve.wait_ge(turned, counted(b - 1))
                for t in range(NT):
                    last = nc.vector.tensor_scalar(xl[:, p, t, :], X[:, b * NT + t, :], moments[:, p, 0, t, 0:1],
                                                   rstd[:, p, 0, t:t + 1], ALU.subtract, ALU.mult)
                last.then_inc(xl_ready, 1)
                dve.drain()

            def scan(i, p):
                b = 2 * i + p
                dve.wait_ge(u_ready, b + 1)
                dve.wait_ge(y_ready, counted(b - 1))
                nc.vector.tensor_tensor_scan(h[:, p, :], Arow[:, :], u_bank[p][:, :], 0.0, ALU.mult, ALU.add).then_inc(h_ready, 1)

            def y_stats(i, p):
                b = 2 * i + p
                dve.wait_ge(y_ready, b + 1)
                layer_stats(nc, dve, y_bank[p][:, :].rearrange("p (t f) -> p t f", t=NT), stats2, moments[:, p, 1, :, :])
                nc.vector.tensor_scalar(ve[:, p, 1, :], moments[:, p, 1, :, 1], LN_EPS, None, ALU.add).then_inc(var2, 1)
                dve.drain()

            def normalise_y(i, p):
                b = 2 * i + p
                dve.wait_ge(rstd2, b + 1)
                dve.wait_ge(added, counted(b - 1))
                for t in range(NT):
                    last = nc.vector.tensor_scalar(z[:, p, t, :], y_bank[p][:, t * P:(t + 1) * P], moments[:, p, 1, t, 0:1],
                                                   rstd[:, p, 1, t:t + 1], ALU.subtract, ALU.mult)
                last.then_inc(z_ready, 1)
                dve.drain()

            pipeline(dve, STAGES, (4, normalise_y), (0, x_stats), (1, normalise), (3, y_stats), (2, scan))

        @block.gpsimd
        def _(pool):
            pool.wait_ge(filled, 1)

            def invert_x(i, p):
                pool.wait_ge(var1, 2 * i + p + 1)
                nc.gpsimd.tensor_tensor(rstd[:, p, 0, :], ve[:, p, 0, :], minus_half[:, 0:NT], ALU.pow).then_inc(rstd1, 1)

            def invert_y(i, p):
                pool.wait_ge(var2, 2 * i + p + 1)
                nc.gpsimd.tensor_tensor(rstd[:, p, 1, :], ve[:, p, 1, :], minus_half[:, 0:NT], ALU.pow).then_inc(rstd2, 1)

            def add(i, p):
                b = 2 * i + p
                pool.wait_ge(z_ready, b + 1)
                nc.gpsimd.tensor_tensor(tiles(X, b), tiles(X, b), z[:, p, :, :], ALU.add).then_inc(added, 1)

            pipeline(pool, STAGES, (4, add), (0, invert_x), (3, invert_y))

        @block.scalar
        def _(act):
            def copy_xT(i, p):
                b = 2 * i + p
                act.wait_ge(turned, b + 1)
                act.wait_ge(u_ready, counted(b - 1))
                nc.scalar.activation(xT[:, p, :], xT_bank[p][:, :], ACT.Copy).then_inc(xT_ready, 1)

            pipeline(act, STAGES, (1, copy_xT))

        @block.tensor
        def _(pe):
            pe.wait_ge(loaded, LOADS)
            pe.wait_ge(filled, 1)

            def turn(i, p):
                b = 2 * i + p
                pe.wait_ge(xl_ready, b + 1)
                pe.wait_ge(xT_ready, counted(b - 1))
                for t in range(NT):
                    last = nc.tensor.transpose(xT_bank[p][:, t * P:(t + 1) * P], xl[:, p, t, :], ident)
                last.then_inc(turned, 1)

            def project(i, p):
                b = 2 * i + p
                pe.wait_ge(xT_ready, b + 1)
                pe.wait_ge(h_ready, counted(b - 1))
                nc.tensor.matmul(u_bank[p][:, :], BT[:, :], xT[:, p, :], start=True, stop=True).then_inc(u_ready, 1)

            def output(i, p):
                b = 2 * i + p
                pe.wait_ge(h_ready, b + 1)
                pe.wait_ge(z_ready, counted(b - 1))
                nc.tensor.matmul(y_bank[p][:, :], ones[:, :], bias[:, :], start=True, stop=False)
                for t in range(NT):
                    last = nc.tensor.matmul(y_bank[p][:, t * P:(t + 1) * P], h[:, p, t * P:(t + 1) * P], WT[:, :],
                                            start=False, stop=(t == NT - 1))
                last.then_inc(y_ready, 1)

            pipeline(pe, STAGES, (3, output), (2, project), (1, turn))


ROWS = SLOTS * HD * 2
SHIFTED = ROWS + 6


def qkv_layer(nc, io, X, XL, const, ident, minus_half, bank, ctx, sb, sem, scratch):
    STAGES = 7
    Wq, Wk, Wv = sb("q_Wq", [P, D]), sb("q_Wk", [P, D]), sb("q_Wv", [P, D])
    cols = sb("q_cols", [P, 4])
    stats, moments = sb("q_stats", [P, NT, 6]), sb("q_moments", [P, 2, NT, 2])
    ve, rstd = sb("q_ve", [P, 2, 2, NT]), sb("q_rstd", [P, 2, 2, NT])
    h, hT = sb("q_h", [P, 2, NT, D]), sb("q_hT", [P, 2, T])
    sq, rroot, qn, rest = sb("q_sq", [P, 2, 2, T]), sb("q_rroot", [P, 2, 2, T]), sb("q_qn", [P, 2, 2, T]), sb("q_rest", [P, 2, 2, T])
    parts = sb("q_parts", [P, 2, 3, 2, T], BF16)
    v1 = sb("q_v1", [P, 2, NT, HEADS, HD + 1])
    loaded, filled = sem("q_loaded"), sem("q_filled")
    var1, rstd1, h_ready, turned, hT_ready = sem("q_var"), sem("q_rstd"), sem("q_h_ready"), sem("q_turned"), sem("q_hT_ready")
    qk_ready, v_ready, sq_ready, mean_ready = sem("q_qk_ready"), sem("q_v_ready"), sem("q_sq_ready"), sem("q_mean_ready")
    rroot_ready, qn_ready, v1_ready = sem("q_rroot_ready"), sem("q_qn_ready"), sem("q_v1_ready")
    high_ready, rest_ready, mid_ready, low_ready = sem("q_high_ready"), sem("q_rest_ready"), sem("q_mid_ready"), sem("q_low_ready")
    stored, v_stored = [sem("q_stored0"), sem("q_stored1")], [sem("q_v_stored0"), sem("q_v_stored1")]
    q_bank, k_bank, mean_bank, hT_bank, v_bank = bank[0:2], bank[2:4], bank[4:6], bank[6], bank[7]
    headmean = const_part(const, "headmean")
    stack, values = scratch

    with nc.Block() as block:
        @block.sync
        def _(sp):
            for dst, name in ((Wq, "WqT"), (Wk, "WkT"), (Wv, "WvT")):
                sp.dma_start(dst[:, :], io[name][:, :]).then_inc(loaded, 16)
            for n, name in enumerate(("n1_w", "qn_w", "kn_w")):
                sp.dma_start(cols[:, n:n + 1], column(io[name])).then_inc(loaded, 16)

            def store_v(i, p):
                b = 2 * i + p
                sp.wait_ge(v1_ready, b + 1)
                sp.dma_start(values[bass.ds(b, 1), :, :].rearrange("a p n -> (a p) n"),
                             v1[:, p, :, :, :].rearrange("p t h d -> p (t h d)")).then_inc(v_stored[p], 16)

            def store(i, p):
                b = 2 * i + p
                sp.wait_ge(low_ready, b + 1)
                sp.dma_start(stack[bass.ds(b, 1), :, :, :, :].rearrange("a c k r n -> (a r) c k n"),
                             parts[:, p, :, :, :]).then_inc(stored[p], 16)

            pipeline(sp, STAGES, (6, store), (4, store_v))
            for s in stored + v_stored:
                sp.wait_ge(s, B // 2 * 16)

        @block.vector
        def _(dve):
            nc.vector.memset(cols[:, 3:4], RMS_EPS)
            nc.vector.memset(v1[:, :, :, :, HD:HD + 1].rearrange("p a t h d -> p (a t h) d"), 1.0).then_inc(filled, 1)
            dve.wait_ge(loaded, 96)

            def x_stats(i, p):
                layer_stats(nc, dve, tiles(X, 2 * i + p), stats, moments[:, p, :, :])
                nc.vector.tensor_scalar(ve[:, p, 0, :], moments[:, p, :, 1], LN_EPS, None, ALU.add)
                nc.vector.tensor_scalar(ve[:, p, 1, :], moments[:, p, :, 1], 1.0 + RMS_EPS, LN_EPS * RMS_EPS, ALU.mult,
                                        ALU.add).then_inc(var1, 1)
                dve.drain()

            def normalise(i, p):
                b = 2 * i + p
                dve.wait_ge(rstd1, b + 1)
                dve.wait_ge(turned, counted(b - 1))
                for t in range(NT):
                    nc.vector.tensor_scalar(XL[:, b * NT + t, :], X[:, b * NT + t, :], moments[:, p, t, 0:1], rstd[:, p, 0, t:t + 1],
                                            ALU.subtract, ALU.mult)
                    last = nc.vector.tensor_scalar(h[:, p, t, :], X[:, b * NT + t, :], moments[:, p, t, 0:1], rstd[:, p, 1, t:t + 1],
                                                   ALU.subtract, ALU.mult)
                last.then_inc(h_ready, 1)
                dve.drain()

            def norm(i, p):
                b = 2 * i + p
                dve.wait_ge(rroot_ready, b + 1)
                nc.vector.scalar_tensor_tensor(qn[:, p, 0, :], q_bank[p][:, :], cols[:, 1:2], rroot[:, p, 0, :], ALU.mult, ALU.mult)
                nc.vector.scalar_tensor_tensor(qn[:, p, 1, :], k_bank[p][:, :], cols[:, 2:3], rroot[:, p, 1, :], ALU.mult,
                                               ALU.mult).then_inc(qn_ready, 1)

            def leave(i, p):
                b = 2 * i + p
                dve.wait_ge(high_ready, b + 1)
                dve.wait_ge(low_ready, counted(b - 1))
                nc.vector.tensor_tensor(rest[:, p, :, :], qn[:, p, :, :], parts[:, p, 0, :, :], ALU.subtract).then_inc(rest_ready, 1)

            pipeline(dve, STAGES, (2, normalise), (4, norm), (0, x_stats), (5, leave))

        @block.gpsimd
        def _(pool):
            def invert(i, p):
                pool.wait_ge(var1, 2 * i + p + 1)
                nc.gpsimd.tensor_tensor(rstd[:, p, :, :], ve[:, p, :, :], minus_half[:, 0:2 * NT].rearrange("p (a t) -> p a t", a=2),
                                        ALU.pow).then_inc(rstd1, 1)

            def low(i, p):
                b = 2 * i + p
                pool.wait_ge(mid_ready, b + 1)
                nc.gpsimd.tensor_tensor(parts[:, p, 2, :, :], rest[:, p, :, :], parts[:, p, 1, :, :], ALU.subtract).then_inc(low_ready, 1)

            pipeline(pool, STAGES, (6, low), (0, invert))

        @block.scalar
        def _(act):
            act.wait_ge(loaded, 96)
            act.wait_ge(filled, 1)

            def copy_hT(i, p):
                b = 2 * i + p
                act.wait_ge(turned, b + 1)
                act.wait_ge(v_ready, counted(b - 1))
                nc.scalar.activation(hT[:, p, :], hT_bank[:, :], ACT.Copy, scale=cols[:, 0:1]).then_inc(hT_ready, 1)

            def squares(i, p):
                b = 2 * i + p
                act.wait_ge(qk_ready, b + 1)
                act.wait_ge(mean_ready, counted(b - 1))
                nc.scalar.activation(sq[:, p, 0, :], q_bank[p][:, :], ACT.Square)
                nc.scalar.activation(sq[:, p, 1, :], k_bank[p][:, :], ACT.Square).then_inc(sq_ready, 1)
                act.wait_ge(v_ready, b + 1)
                act.wait_ge(v_stored[p], 16 * i)
                nc.scalar.activation(v1[:, p, :, :, 0:HD], v_bank[:, :].rearrange("p (t h d) -> p t h d", t=NT, h=HEADS),
                                     ACT.Copy).then_inc(v1_ready, 1)

            def roots(i, p):
                b = 2 * i + p
                act.wait_ge(mean_ready, b + 1)
                act.wait_ge(qn_ready, counted(b - 1))
                nc.scalar.activation(rroot[:, p, 0, :], mean_bank[0][:, :], ACT.Ln, bias=cols[:, 3:4])
                nc.scalar.activation(rroot[:, p, 1, :], mean_bank[1][:, :], ACT.Ln, bias=cols[:, 3:4])
                act.drain()
                nc.scalar.activation(rroot[:, p, :, :], rroot[:, p, :, :], ACT.Exp, scale=-0.5).then_inc(rroot_ready, 1)

            def high(i, p):
                act.wait_ge(qn_ready, 2 * i + p + 1)
                act.wait_ge(stored[p], 16 * i)
                nc.scalar.activation(parts[:, p, 0, :, :], qn[:, p, :, :], ACT.Copy).then_inc(high_ready, 1)

            def mid(i, p):
                act.wait_ge(rest_ready, 2 * i + p + 1)
                nc.scalar.activation(parts[:, p, 1, :, :], rest[:, p, :, :], ACT.Copy).then_inc(mid_ready, 1)

            pipeline(act, STAGES, (6, mid), (4, roots), (3, squares), (5, high), (2, copy_hT))

        @block.tensor
        def _(pe):
            pe.wait_ge(loaded, 96)

            def turn(i, p):
                b = 2 * i + p
                pe.wait_ge(h_ready, b + 1)
                pe.wait_ge(hT_ready, b)
                for t in range(NT):
                    last = nc.tensor.transpose(hT_bank[:, t * P:(t + 1) * P], h[:, p, t, :], ident)
                last.then_inc(turned, 1)

            def project(i, p):
                b = 2 * i + p
                pe.wait_ge(hT_ready, b + 1)
                pe.wait_ge(qn_ready, counted(b - 1))
                nc.tensor.matmul(q_bank[p][:, :], Wq[:, :], hT[:, p, :], start=True, stop=True)
                nc.tensor.matmul(k_bank[p][:, :], Wk[:, :], hT[:, p, :], start=True, stop=True).then_inc(qk_ready, 1)
                pe.wait_ge(v1_ready, b)
                for t in range(NT):
                    last = nc.tensor.matmul(v_bank[:, t * P:(t + 1) * P], hT[:, p, t * P:(t + 1) * P], Wv[:, :], start=True, stop=True)
                last.then_inc(v_ready, 1)

            def means(i, p):
                b = 2 * i + p
                pe.wait_ge(sq_ready, b + 1)
                pe.wait_ge(rroot_ready, b)
                for n in range(2):
                    last = nc.tensor.matmul(mean_bank[n][:, :], headmean, sq[:, p, n, :], start=True, stop=True)
                last.then_inc(mean_ready, 1)

            pipeline(pe, STAGES, (4, means), (3, project), (2, turn))


SCORE_UNITS = [(0, (h,)) for h in range(4)] + [(1, (h,)) for h in range(4)] + [(2, (0, 1)), (2, (2, 3)), (3, (0, 1, 2, 3))]
MAX_UNITS = [(0, (0, 1, 2, 3)), (1, (0, 1)), (1, (2, 3))] + [(2, (h,)) for h in range(4)] + [(3, (h,)) for h in range(4)]
UNITS = len(SCORE_UNITS)
GROUPS = HEADS // GROUP
SCORES = UNITS * GROUPS
LAST_OF_TILE = {max(k for k, u in enumerate(SCORE_UNITS) if u[0] == kt): kt for kt in range(NT)}


def order_of_work():
    for g in range(GROUPS):
        for k in range(UNITS):
            yield "score", g, k
            yield "max", g, k
            if g and k == 1:
                yield "values", g - 1, 2
            if g and k == 4:
                yield "values", g - 1, 3
            if g and k == 8:
                yield "turn", g - 1, 0
            if k == 7:
                yield "values", g, 0
            if k == 10:
                yield "values", g, 1
            if g == 2 and k == 6:
                yield "shift", 0, 0
    yield "values", 3, 2
    yield "values", 3, 3
    yield "turn", 3, 0
    yield "project", 0, 0
    yield "shift", 1, 0


def attention_layer(nc, io, X, XL, const, ident, minus_half, bank, ctx, sb, sem, scratch):
    stack, values = scratch
    Q, K = sb("a_Q", [P, 2, PAIRS, T], BF16), sb("a_K", [P, 2, 2, PAIRS, T], BF16)
    V = sb("a_V", [P, 2, NT, HEADS, HD + 1])
    Wo = sb("a_Wo", [P, WIDE])
    identb, maskb = sb("a_identb", [P, P], BF16), sb("a_maskb", [P, P], BF16)
    E = [sb(f"a_E{kt}", [P, GROUP, T - P * kt]) for kt in range(NT)]
    neg = sb("a_neg", [P, NT, 2, PAIRS])
    nb, nr = sb("a_nb", [P, 2, NT, 2, 4], BF16), sb("a_nr", [P, NT, 2, 4])
    nparts = sb("a_nparts", [P, NT, 2, 3, 4])
    shiftT = sb("a_shiftT", [24, T], BF16)
    outT, inv = sb("a_outT", [P, T]), sb("a_inv", [P, NT * GROUP])
    ao, aoT = sb("a_ao", [P, NT, D]), sb("a_aoT", [P, T])
    loaded, prepared, ones_ready = sem("a_loaded"), sem("a_prepared"), sem("a_ones_ready")
    zeroed, pool_zeroed = sem("a_zeroed"), sem("a_pool_zeroed")
    stacked = [[sem(f"a_stacked{p}{hf}") for hf in range(2)] for p in range(2)]
    v_in = [sem("a_v_in0"), sem("a_v_in1")]
    score_ready, exp_done, kept = sem("a_score_ready"), sem("a_exp_done"), sem("a_kept")
    max_ready, max_taken, nparts_ready, shift_turned = sem("a_max_ready"), sem("a_max_taken"), sem("a_nparts"), sem("a_shift_turned")
    shift_copied, shift_in = sem("a_shift_copied"), [sem("a_shift_in0"), sem("a_shift_in1")]
    pv_done, outT_ready, turned, ao_ready = sem("a_pv_done"), sem("a_outT_ready"), sem("a_turned"), sem("a_ao_ready")
    ao_turned, aoT_ready, wo_ready, wo_taken = sem("a_ao_turned"), sem("a_aoT_ready"), sem("a_wo_ready"), sem("a_wo_taken")
    pool_tick = sem("a_pool_tick")
    score_bank, max_bank, pv_bank, turn_bank, misc_bank = bank[0:3], bank[3:5], bank[5], bank[6], bank[7]
    SCALE = float(HD) ** -0.5
    n_pv = GROUPS * NT

    def stack_count(b, p):
        return ((b + p) // 2 + 1) * 192 if isinstance(b, int) else (b - p) * 96 + 192 * (p + 1)

    def v_count(b, p):
        return (b // 2 + 1) * 16 if isinstance(b, int) else (b - p) * 8 + 16

    def run(eng, step):
        for g in range(GROUPS):
            for k in range(UNITS):
                step("max", g, k, -1, 1)
            if g == 1:
                step("shift", 0, 0, -1, 1)
        step("shift", 1, 0, -1, 1)
        with eng.Fori(0, B // 2 - 1) as i:
            for p in range(2):
                for kind, g, k in order_of_work():
                    step(kind, g, k, 2 * i + p, p)
        for b in (B - 2, B - 1):
            for kind, g, k in order_of_work():
                if b < B - 1 or kind not in ("max", "shift"):
                    step(kind, g, k, b, b % 2)

    def shift_rows(ops, eng, p):
        eng.drain()
        ops.memset(K[ROWS:ROWS + 3, p, 0, :, :], 1.0)
        ops.memset(K[ROWS:SHIFTED, p, 1, :, :], 1.0)
        eng.drain()
        return ops.memset(K[ROWS:ROWS + 3, p, 1, :, :], 0.0)

    with nc.Block() as block:
        @block.sync
        def _(sp):
            sp.dma_start(Wo[:, :], io["WoT"][:, :]).then_inc(loaded, 16)
            def load(b, p, hf):
                pairs = slice(4 * hf, 4 * hf + 4)
                if not (isinstance(b, int) and b < 2):
                    sp.wait_ge(score_ready, (b - 2) * SCORES + (hf + 1) * SCORES // 2)
                for par in range(2):
                    src = stack[bass.ds(b, 1), :, :, par * 64:par * 64 + 64, :].rearrange("a c k (d r) n -> (a c) k d r n", r=PAIRS)
                    slot = 0
                    for c in range(3):
                        rows = slice((par * SLOTS + slot) * HD, (par * SLOTS + slot + 3 - c) * HD)
                        sp.dma_start(Q[rows, p, pairs, :],
                                     src[c:c + 1, 0, :, pairs, :].to_broadcast([3 - c, HD, 4, T])).then_inc(stacked[p][hf], 16)
                        sp.dma_start(K[rows, p, par, pairs, :],
                                     src[0:3 - c, 1, :, pairs, :]).then_inc(stacked[p][hf], 16)
                        slot += 3 - c

            def load_v(b, p):
                if not (isinstance(b, int) and b < 2):
                    sp.wait_ge(pv_done, (b - 1) * n_pv)
                sp.dma_start(V[:, p, :, :, :].rearrange("p t h d -> p (t h d)"),
                             values[bass.ds(b, 1), :, :].rearrange("a p n -> (a p) n")).then_inc(v_in[p], 16)

            def shift(m, p, hf):
                sp.wait_ge(shift_copied, 2 * m + hf + 1)
                sp.dma_start(Q[ROWS:SHIFTED, p, 4 * hf:4 * hf + 4, :], shiftT[:, :]).then_inc(shift_in[hf], 16)

            sp.wait_ge(zeroed, 1)
            load(0, 0, 0)
            load(0, 0, 1)
            load_v(0, 0)
            sp.wait_ge(pool_zeroed, 1)
            load(1, 1, 0)
            shift(0, 0, 0)
            load(1, 1, 1)
            load_v(1, 1)
            shift(0, 0, 1)
            with sp.Fori(0, B // 2 - 1) as i:
                for p in range(2):
                    load(2 * i + p + 2, p, 0)
                    shift(2 * i + p + 1, 1 - p, 0)
                    shift(2 * i + p + 1, 1 - p, 1)
                    load(2 * i + p + 2, p, 1)
                    load_v(2 * i + p + 2, p)
            shift(B - 1, 1, 0)
            shift(B - 1, 1, 1)

        @block.tensor
        def _(pe):
            pe.wait_ge(loaded, 16)
            pe.wait_ge(prepared, 1)

            def step(kind, g, k, b, p):
                m, mp = b + 1, 1 - p
                im = (m - mp) // 2 if isinstance(m, int) else None
                if kind == "score":
                    n = g * UNITS + k
                    kt, heads = SCORE_UNITS[k]
                    if k == 0 and g % 2 == 0:
                        pe.wait_ge(shift_in[g // 2], 16 * (b + 1))
                    if n >= 3:
                        pe.wait_ge(exp_done, b * SCORES + n - 2)
                    wide = T - P * kt
                    for x, j in enumerate(heads):
                        h = GROUP * g + j
                        last = nc.tensor.matmul(score_bank[n % 3][:, x * wide:(x + 1) * wide], K[0:SHIFTED, p, h % 2, h // 2, kt * P:(kt + 1) * P],
                                                Q[0:SHIFTED, p, h // 2, kt * P:T], start=True, stop=True)
                    last.then_inc(score_ready, 1)
                if kind == "max":
                    n = g * UNITS + k
                    qt, heads = MAX_UNITS[k]
                    if k == 0 and g % 2 == 0:
                        pe.wait_ge(stacked[mp][g // 2], stack_count(b, p))
                    pe.wait_ge(max_taken, m * SCORES + max(n - 1, 0))
                    wide = P * (qt + 1)
                    for x, j in enumerate(heads):
                        h = GROUP * g + j
                        at = x * wide
                        nc.tensor.matmul(max_bank[n % 2][:, at:at + wide], Q[0:ROWS, mp, h // 2, qt * P:(qt + 1) * P],
                                         K[0:ROWS, mp, h % 2, h // 2, 0:wide], start=True, stop=False)
                        last = nc.tensor.matmul(max_bank[n % 2][:, at + wide - P:at + wide], identb[:, :], maskb[:, :],
                                                start=False, stop=True)
                    last.then_inc(max_ready, 1)
                if kind == "values":
                    kt = k
                    pe.wait_ge(kept, b * n_pv + g * NT + kt + 1)
                    if kt == 0:
                        pe.wait_ge(outT_ready, b * GROUPS + g)
                        if g == 0:
                            pe.wait_ge(v_in[p], v_count(b, p))
                    for j in range(GROUP):
                        last = nc.tensor.matmul(pv_bank[32 * j:32 * j + HD + 1, kt * P:T], V[:, p, kt, GROUP * g + j, :], E[kt][:, j, :],
                                                start=(kt == 0), stop=(kt == NT - 1))
                    last.then_inc(pv_done, 1)
                if kind == "turn":
                    pe.wait_ge(outT_ready, b * GROUPS + g + 1)
                    if g:
                        pe.wait_ge(ao_ready, b * GROUPS + g)
                    else:
                        pe.wait_ge(aoT_ready, b)
                    for t in range(NT):
                        last = nc.tensor.transpose(turn_bank[:, t * P:(t + 1) * P], outT[:, t * P:(t + 1) * P], ident)
                    last.then_inc(turned, 1)
                if kind == "project":
                    pe.wait_ge(ao_ready, (b + 1) * GROUPS)
                    for t in range(NT):
                        last = nc.tensor.transpose(turn_bank[:, t * P:(t + 1) * P], ao[:, t, :], ident)
                    last.then_inc(ao_turned, 1)
                    pe.wait_ge(aoT_ready, b + 1)
                    pe.wait_ge(shift_copied, 2 * m if isinstance(b, int) and m == B else 2 * m + 1)
                    for t in range(NT):
                        last = nc.tensor.matmul(misc_bank[:, t * WIDE:(t + 1) * WIDE], aoT[:, t * P:(t + 1) * P], Wo[:, :],
                                                start=True, stop=True)
                    last.then_inc(wo_ready, 1)
                if kind == "shift":
                    pe.wait_ge(nparts_ready, 2 * m + g + 1)
                    if g == 0:
                        pe.wait_ge(shift_copied, 2 * m)
                    elif isinstance(b, int) and b < 0:
                        pe.wait_ge(shift_copied, 1)
                    else:
                        pe.wait_ge(wo_taken, b + 1)
                    for t in range(NT):
                        last = nc.tensor.transpose(misc_bank[0:24, t * P:(t + 1) * P], nparts[:, t, :, :, :].rearrange("p a r c -> p (a r c)"), ident)
                    last.then_inc(shift_turned, 1)
                    if isinstance(b, int) and b < 0 and g == 1:
                        pe.wait_ge(ones_ready, 2)

            run(pe, step)

        @block.scalar
        def _(act):
            def step(kind, g, k, b, p):
                m, mp = b + 1, 1 - p
                if kind == "score":
                    n = g * UNITS + k
                    kt, heads = SCORE_UNITS[k]
                    act.wait_ge(score_ready, b * SCORES + n + 1)
                    if g:
                        act.wait_ge(pv_done, b * n_pv + (g - 1) * NT + kt + 1)
                    wide = T - P * kt
                    nc.scalar.activation(E[kt][:, heads[0]:heads[-1] + 1, :],
                                         score_bank[n % 3][:, 0:len(heads) * wide].rearrange("p (h q) -> p h q", q=wide),
                                         ACT.Exp, scale=SCALE).then_inc(exp_done, 1)
                if kind == "values" and k == NT - 1:
                    act.wait_ge(pv_done, b * n_pv + g * NT + NT)
                    act.wait_ge(turned, b * GROUPS + g)
                    nc.scalar.activation(outT[:, :], pv_bank[:, :], ACT.Copy).then_inc(outT_ready, 1)
                if kind == "project":
                    act.wait_ge(ao_turned, b + 1)
                    nc.scalar.activation(aoT[:, :], turn_bank[:, :], ACT.Copy).then_inc(aoT_ready, 1)
                if kind == "shift":
                    act.wait_ge(shift_turned, 2 * m + g + 1)
                    act.wait_ge(shift_in[1 - g], 16 * m if g == 0 else 16 * (m + 1))
                    nc.scalar.activation(shiftT[:, :], misc_bank[0:24, :], ACT.Copy).then_inc(shift_copied, 1)

            run(act, step)

        @block.vector
        def _(dve):
            nc.vector.memset(K[:, 0, :, :, :].bitcast(F32), 0.0).then_inc(zeroed, 1)
            nc.vector.memset(pv_bank[:, :], 0.0)
            nc.vector.tensor_copy(identb[:, :], ident)
            nc.vector.tensor_copy(maskb[:, :], const_part(const, "mask")).then_inc(prepared, 1)
            shift_rows(nc.vector, dve, 0).then_inc(ones_ready, 1)
            dve.drain()

            def step(kind, g, k, b, p):
                m = b + 1
                if kind == "max":
                    n = g * UNITS + k
                    qt, heads = MAX_UNITS[k]
                    dve.wait_ge(max_ready, m * SCORES + n + 1)
                    if k == 0:
                        dve.wait_ge(nparts_ready, 2 * m)
                    wide, h0, nh = P * (qt + 1), GROUP * g + heads[0], len(heads)
                    src = max_bank[n % 2][:, 0:nh * wide].rearrange("p (h q) -> p h q", q=wide)
                    if nh == 1:
                        dst = neg[:, qt, h0 % 2, h0 // 2:h0 // 2 + 1]
                    elif nh == 2:
                        dst = neg[:, qt, 0:2, h0 // 2]
                    else:
                        dst = neg[:, qt, :, h0 // 2:h0 // 2 + 2].rearrange("p r a -> p a r")
                        src = src.rearrange("p (a r) q -> p a r q", r=2)
                    nc.vector.tensor_reduce(out=dst, in_=src, axis=AX.X, op=ALU.max, negate=True).then_inc(max_taken, 1)
                if kind == "turn":
                    dve.wait_ge(turned, b * GROUPS + g + 1)
                    o = turn_bank[:, :].rearrange("p (n c) -> p n c", c=32)
                    nc.vector.reciprocal(inv[:, :], o[:, :, HD])
                    dve.drain()
                    nc.vector.tensor_tensor(ao[:, :, 32 * g:32 * g + 32].rearrange("p t (j d) -> p t j d", d=HD),
                                            o[:, :, 0:HD].rearrange("p (t j) d -> p t j d", t=NT),
                                            inv[:, :].rearrange("p (t j) -> p t j", t=NT).unsqueeze(3).to_broadcast([P, NT, GROUP, HD]),
                                            ALU.mult).then_inc(ao_ready, 1)
                    dve.drain()
                if kind == "project":
                    dve.wait_ge(wo_ready, b + 1)
                    dst = XL[:, bass.ds(b * NT, NT), MASKED:D]
                    nc.vector.tensor_tensor(dst, misc_bank[:, 0:NT * WIDE].rearrange("p (t f) -> p t f", t=NT), dst, ALU.add).then_inc(wo_taken, 1)

            run(dve, step)

        @block.gpsimd
        def _(pool):
            nc.gpsimd.memset(K[:, 1, :, :, :].bitcast(F32), 0.0).then_inc(pool_zeroed, 1)
            shift_rows(nc.gpsimd, pool, 1).then_inc(ones_ready, 1)
            pool.drain()

            def step(kind, g, k, b, p):
                m = b + 1
                if kind == "score" and k in LAST_OF_TILE:
                    kt = LAST_OF_TILE[k]
                    pool.wait_ge(exp_done, b * SCORES + g * UNITS + k + 1)
                    pool.sem_inc(pool_tick, 1)
                    nc.gpsimd.affine_select(out=E[kt][:, :, 0:P], in_=E[kt][:, :, 0:P], compare_op=ALU.is_ge, fill=0.0, base=0,
                                            pattern=[[0, GROUP], [1, P]], channel_multiplier=-1).then_inc(kept, 1)
                if kind == "max" and g % 2 == 1 and k == UNITS - 1:
                    hf = g // 2
                    pool.wait_ge(max_taken, m * SCORES + (g + 1) * UNITS)
                    pool.wait_ge(shift_turned, 2 * m + hf)
                    pool.sem_inc(pool_tick, 1)
                    src = neg[:, :, :, 4 * hf:4 * hf + 4]
                    nc.gpsimd.tensor_copy(nb[:, 0, :, :, :], src)
                    pool.drain()
                    nc.gpsimd.tensor_copy(nparts[:, :, :, 0, :], nb[:, 0, :, :, :])
                    nc.gpsimd.tensor_tensor(nr[:, :, :, :], src, nb[:, 0, :, :, :], ALU.subtract)
                    pool.drain()
                    nc.gpsimd.tensor_copy(nb[:, 1, :, :, :], nr[:, :, :, :])
                    pool.drain()
                    nc.gpsimd.tensor_copy(nparts[:, :, :, 1, :], nb[:, 1, :, :, :])
                    nc.gpsimd.tensor_tensor(nparts[:, :, :, 2, :], nr[:, :, :, :], nb[:, 1, :, :, :], ALU.subtract).then_inc(nparts_ready, 1)
                    pool.drain()

            run(pool, step)


EXPERTS = 4
HC2 = 2
MOE_ORDER = [("up", "e0u", "x", 1, 2), ("up", "e1a", "x", 1, 2), ("up", "e1b", "x", 1, 2), ("up", "e2a", "x", 1, 2),
             ("out", 0), ("up", "e3a", "x", 1, 1), ("up", "e2b", "G1", 2, 2), ("out", 1), ("up", "e3b", "G3", 1, 2),
             ("up", "e2c", "G2", 2, 2), ("out", 3), ("out", 2)]
MOE_UPS = [s for s in MOE_ORDER if s[0] == "up"]
MOE_OUTS = [s[1] for s in MOE_ORDER if s[0] == "out"]
MOE_TO = {"e0u": "H0", "e1a": "S1", "e1b": "H1", "e2a": "G1", "e3a": "G3", "e2b": "G2", "e3b": "H3", "e2c": "G4"}
MOE_LAST = {0: "H0", 1: "H1", 2: "G4", 3: "H3"}


def expert_layer(nc, io, X, XL, const, ident, minus_half, bank, ctx, sb, sem, scratch):
    STAGES = 6
    W = {name: sb(f"e_{name}", [P, n, HC2 * P if name != "e3a" else P]) for name, n in
         (("e0u", 1), ("e1a", 1), ("e1b", 1), ("e2a", 1), ("e2b", 2), ("e2c", 2), ("e3a", 1), ("e3b", 1))}
    down = sb("e_down", [P, EXPERTS, HC2, WIDE])
    gate = sb("e_gate", [P, EXPERTS])
    n2w = sb("e_n2w", [P, 1])
    stats, moments = sb("e_stats", [P, NT, 6]), sb("e_moments", [P, NT, 2])
    stats2, moments2 = sb("e_stats2", [P, NT, 6]), sb("e_moments2", [P, 2, NT, 2])
    ve, rstd = sb("e_ve", [P, 2, 2, NT]), sb("e_rstd", [P, 2, 2, NT])
    xf, z = sb("e_xf", [P, 2, NT, D]), sb("e_z", [P, 2, NT, D])
    xfT = sb("e_xfT", [P, 2, T])
    hid = {name: sb(f"e_{name}", [P, 1 if name == "G3" else HC2, T]) for name in ("H0", "S1", "H1", "G1", "G2", "G3", "G4", "H3")}
    euler = sb("e_euler", [P, NT * EXPERTS])
    lg, part, pr, tv = (sb(f"e_{x}", [P, NT, EXPERTS]) for x in ("lg", "part", "pr", "tv"))
    top, cmp1, cmp2 = sb("e_top", [P, NT]), sb("e_cmp1", [P, NT, EXPERTS, EXPERTS]), sb("e_cmp2", [P, NT, EXPERTS, EXPERTS])
    wts = sb("e_wts", [P, NT, EXPERTS])
    loaded, filled = sem("e_loaded"), sem("e_filled")
    names = "var1 rstd1 var2 rstd2 xf_ready turned xfT_ready logits_ready logits_taken diff_ready exp_ready up_ready act_done mul_done out_ready out_taken z_ready added"
    (var1, rstd1, var2, rstd2, xf_ready, turned, xfT_ready, logits_ready, logits_taken, diff_ready, exp_ready, up_ready, act_done,
     mul_done, out_ready, out_taken, z_ready, added) = (sem("e_" + x) for x in names.split())
    xT_bank, logit_bank, out_bank = bank[0], bank[1], bank[6:8]
    up_banks = (bank[2:4], bank[4:6])
    n_up, n_act = len(MOE_UPS), len(MOE_UPS) - 1
    up_at = {s[1]: n for n, s in enumerate(MOE_UPS)}
    act_at = {s[1]: n for n, s in enumerate(s for s in MOE_UPS if s[1] != "e1b")}
    LOADS = 16 * (len(W) + EXPERTS + 2)

    def up_free(eng, n, b):
        if n < 2:
            return
        name = MOE_UPS[n - 2][1]
        if name == "e1b":
            eng.wait_ge(mul_done, b + 1)
        else:
            eng.wait_ge(act_done, b * n_act + act_at[name] + 1)

    def made(eng, name, b):
        if name == "H1":
            eng.wait_ge(mul_done, b + 1)
        elif name != "x":
            src = [k for k, v in MOE_TO.items() if v == name][0]
            eng.wait_ge(act_done, b * n_act + act_at[src] + 1)

    with nc.Block() as block:
        @block.sync
        def _(sp):
            for name, w in W.items():
                sp.dma_start(w[:, :, :], io[name + "T"].rearrange("(c p) f -> p c f", p=P)).then_inc(loaded, 16)
            for e in range(EXPERTS):
                n = 1 if io[f"d{e}T"].shape[0] == P else 2
                sp.dma_start(down[:, e, 0:n, :], io[f"d{e}T"].rearrange("(c p) f -> p c f", p=P)).then_inc(loaded, 16)
            sp.dma_start(gate[:, :], io["gateT"][:, :]).then_inc(loaded, 16)
            sp.dma_start(n2w[:, :], column(io["n2_w"])).then_inc(loaded, 16)

        @block.tensor
        def _(pe):
            pe.wait_ge(loaded, LOADS)

            def turn(i, p):
                b = 2 * i + p
                pe.wait_ge(xf_ready, b + 1)
                pe.wait_ge(xfT_ready, b)
                for t in range(NT):
                    last = nc.tensor.transpose(xT_bank[:, t * P:(t + 1) * P], xf[:, p, t, :], ident)
                last.then_inc(turned, 1)

            def score(i, p):
                b = 2 * i + p
                pe.wait_ge(xfT_ready, b + 1)
                pe.wait_ge(logits_taken, b)
                for t in range(NT):
                    last = nc.tensor.matmul(logit_bank[:, t * EXPERTS:(t + 1) * EXPERTS], xfT[:, p, t * P:(t + 1) * P], gate[:, :],
                                            start=True, stop=True)
                last.then_inc(logits_ready, 1)

            def experts(i, p, steps):
                b = 2 * i + p
                for step in steps:
                    if step[0] == "up":
                        _, name, src, n_in, n_chunks = step
                        n = up_at[name]
                        up_free(pe, n, b)
                        made(pe, src, b)
                        for c in range(n_chunks):
                            for k in range(n_in):
                                rhs = xfT[:, p, :] if src == "x" else hid[src][:, k, :]
                                last = nc.tensor.matmul(up_banks[n % 2][c][:, :], W[name][:, k, c * P:(c + 1) * P], rhs,
                                                        start=(k == 0), stop=(k == n_in - 1))
                        last.then_inc(up_ready, 1)
                    else:
                        e = step[1]
                        n_out = MOE_OUTS.index(e)
                        made(pe, MOE_LAST[e], b)
                        pe.wait_ge(out_taken, b * EXPERTS + max(n_out - 1, 0))
                        for t in range(NT):
                            for k in range(HC2):
                                last = nc.tensor.matmul(out_bank[n_out % 2][:, t * WIDE:(t + 1) * WIDE],
                                                        hid[MOE_LAST[e]][:, k, t * P:(t + 1) * P], down[:, e, k, :],
                                                        start=(k == 0), stop=(k == HC2 - 1))
                        last.then_inc(out_ready, 1)

            half = MOE_ORDER.index(("out", 1)) + 1
            pipeline(pe, STAGES, (3, lambda i, p: experts(i, p, MOE_ORDER[:half])), (2, score),
                     (3, lambda i, p: experts(i, p, MOE_ORDER[half:])), (1, turn))

        @block.scalar
        def _(act):
            act.wait_ge(loaded, LOADS)

            def copy_xfT(i, p):
                b = 2 * i + p
                act.wait_ge(turned, b + 1)
                nc.scalar.activation(xfT[:, p, :], xT_bank[:, :], ACT.Copy, scale=n2w[:, 0:1]).then_inc(xfT_ready, 1)

            def functions(i, p):
                b = 2 * i + p
                for n, (_, name, _, _, n_chunks) in enumerate(MOE_UPS):
                    if name == "e1b":
                        continue
                    act.wait_ge(up_ready, b * n_up + n + 1)
                    dst = hid[MOE_TO[name]]
                    if name == "e0u":
                        act.wait_ge(out_ready, b * EXPERTS)
                    if name == "e1a":
                        act.wait_ge(mul_done, b)
                    for c in range(n_chunks):
                        last = nc.scalar.activation(dst[:, c, :], up_banks[n % 2][c][:, :], ACT.Silu if name == "e1a" else ACT.Gelu)
                    last.then_inc(act_done, 1)

            pipeline(act, STAGES, (3, functions), (1, copy_xfT))

        @block.gpsimd
        def _(pool):
            nc.gpsimd.memset(euler[:, :], math.e)
            pool.drain()

            def invert_x(i, p):
                pool.wait_ge(var1, 2 * i + p + 1)
                nc.gpsimd.tensor_tensor(rstd[:, p, 0, :], ve[:, p, 0, :], minus_half[:, 0:NT], ALU.pow).then_inc(rstd1, 1)

            def exponentials(i, p):
                pool.wait_ge(diff_ready, 2 * i + p + 1)
                nc.gpsimd.tensor_tensor(pr[:, :, :].rearrange("p t e -> p (t e)"), euler[:, :],
                                        part[:, :, :].rearrange("p t e -> p (t e)"), ALU.pow).then_inc(exp_ready, 1)

            def invert_y(i, p):
                pool.wait_ge(var2, 2 * i + p + 1)
                nc.gpsimd.tensor_tensor(rstd[:, p, 1, :], ve[:, p, 1, :], minus_half[:, 0:NT], ALU.pow).then_inc(rstd2, 1)

            def add(i, p):
                b = 2 * i + p
                pool.wait_ge(z_ready, b + 1)
                nc.gpsimd.tensor_tensor(tiles(X, b), tiles(X, b), z[:, p, :, :], ALU.add).then_inc(added, 1)

            pipeline(pool, STAGES, (5, add), (0, invert_x), (2, exponentials), (4, invert_y))

        @block.vector
        def _(dve):
            earlier = const_part(const, "earlier").rearrange("p (i j) -> p i j", i=EXPERTS)

            def f_stats(i, p):
                layer_stats(nc, dve, tiles(XL, 2 * i + p), stats, moments)
                nc.vector.tensor_tensor(top[:, :], moments[:, :, 0], moments[:, :, 0], ALU.mult)
                dve.drain()
                nc.vector.scalar_tensor_tensor(ve[:, p, 0, :], moments[:, :, 1], RMS_EPS, top[:, :], ALU.add, ALU.add).then_inc(var1, 1)
                dve.drain()

            def scale(i, p):
                b = 2 * i + p
                dve.wait_ge(rstd1, b + 1)
                dve.wait_ge(turned, counted(b - 1))
                for t in range(NT):
                    last = nc.vector.tensor_scalar(xf[:, p, t, :], XL[:, b * NT + t, :], rstd[:, p, 0, t:t + 1], None, ALU.mult)
                last.then_inc(xf_ready, 1)
                dve.drain()

            def differences(i, p):
                b = 2 * i + p
                dve.wait_ge(logits_ready, b + 1)
                raw = logit_bank[:, 0:NT * EXPERTS].rearrange("p (t e) -> p t e", e=EXPERTS)
                nc.vector.tensor_scalar(lg[:, :, :], raw, 0.0, FMAX, ALU.max, ALU.min)
                nc.vector.tensor_scalar(part[:, :, :], raw, 0.0, -FMAX, ALU.min, ALU.max).then_inc(logits_taken, 1)
                dve.drain()
                nc.vector.tensor_tensor(lg[:, :, :], lg[:, :, :], part[:, :, :], ALU.add)
                dve.drain()
                nc.vector.tensor_reduce(out=top[:, :], in_=lg[:, :, :], axis=AX.X, op=ALU.max)
                dve.drain()
                nc.vector.tensor_tensor(part[:, :, :], lg[:, :, :], top[:, :].unsqueeze(2).to_broadcast([P, NT, EXPERTS]),
                                        ALU.subtract).then_inc(diff_ready, 1)
                dve.drain()

            def weights(i, p):
                dve.wait_ge(exp_ready, 2 * i + p + 1)
                nc.vector.tensor_reduce(out=top[:, :], in_=pr[:, :, :], axis=AX.X, op=ALU.add)
                dve.drain()
                nc.vector.reciprocal(top[:, :], top[:, :])
                dve.drain()
                nc.vector.tensor_tensor(pr[:, :, :], pr[:, :, :], top[:, :].unsqueeze(2).to_broadcast([P, NT, EXPERTS]), ALU.mult)
                dve.drain()
                full = [P, NT, EXPERTS, EXPERTS]
                mine, other = pr[:, :, :].unsqueeze(3).to_broadcast(full), pr[:, :, :].unsqueeze(2).to_broadcast(full)
                nc.vector.tensor_tensor(cmp1[:, :, :, :], other, mine, ALU.is_equal)
                nc.vector.tensor_tensor(cmp2[:, :, :, :], other, mine, ALU.is_gt)
                dve.drain()
                nc.vector.tensor_tensor(cmp1[:, :, :, :], cmp1[:, :, :, :], earlier.unsqueeze(1).to_broadcast(full), ALU.mult)
                dve.drain()
                nc.vector.tensor_tensor(cmp1[:, :, :, :], cmp1[:, :, :, :], cmp2[:, :, :, :], ALU.add)
                dve.drain()
                nc.vector.tensor_reduce(out=tv[:, :, :], in_=cmp1[:, :, :, :], axis=AX.X, op=ALU.add)
                dve.drain()
                nc.vector.scalar_tensor_tensor(tv[:, :, :], tv[:, :, :], 1.5, pr[:, :, :], ALU.is_lt, ALU.mult)
                dve.drain()
                nc.vector.tensor_reduce(out=top[:, :], in_=tv[:, :, :], axis=AX.X, op=ALU.add)
                dve.drain()
                nc.vector.tensor_scalar(top[:, :], top[:, :], 1e-8, None, ALU.add)
                dve.drain()
                nc.vector.reciprocal(top[:, :], top[:, :])
                dve.drain()
                nc.vector.tensor_tensor(wts[:, :, :], tv[:, :, :], top[:, :].unsqueeze(2).to_broadcast([P, NT, EXPERTS]), ALU.mult)
                dve.drain()

            def multiply(i, p):
                b = 2 * i + p
                dve.wait_ge(up_ready, b * n_up + up_at["e1b"] + 1)
                dve.wait_ge(act_done, b * n_act + act_at["e1a"] + 1)
                for c in range(HC2):
                    last = nc.vector.tensor_tensor(hid["H1"][:, c, :], hid["S1"][:, c, :], up_banks[up_at["e1b"] % 2][c][:, :], ALU.mult)
                last.then_inc(mul_done, 1)

            def combine(i, p, n_out):
                b, e = 2 * i + p, MOE_OUTS[n_out]
                dve.wait_ge(out_ready, b * EXPERTS + n_out + 1)
                for t in range(NT):
                    acc = XL[:, b * NT + t, MASKED:D]
                    last = nc.vector.scalar_tensor_tensor(acc, out_bank[n_out % 2][:, t * WIDE:(t + 1) * WIDE],
                                                          wts[:, t, e:e + 1], acc, ALU.mult, ALU.add)
                last.then_inc(out_taken, 1)
                dve.drain()

            def y_stats(i, p):
                layer_stats(nc, dve, tiles(XL, 2 * i + p), stats2, moments2[:, p, :, :])
                nc.vector.tensor_scalar(ve[:, p, 1, :], moments2[:, p, :, 1], LN_EPS, None, ALU.add).then_inc(var2, 1)
                dve.drain()

            def normalise_y(i, p):
                b = 2 * i + p
                dve.wait_ge(rstd2, b + 1)
                dve.wait_ge(added, counted(b - 1))
                for t in range(NT):
                    last = nc.vector.tensor_scalar(z[:, p, t, :], XL[:, b * NT + t, :], moments2[:, p, t, 0:1], rstd[:, p, 1, t:t + 1],
                                                   ALU.subtract, ALU.mult)
                last.then_inc(z_ready, 1)
                dve.drain()

            pipeline(dve, STAGES, (3, weights), (3, multiply), (3, lambda i, p: combine(i, p, 0)), (5, normalise_y), (0, f_stats),
                     (1, scale), (3, lambda i, p: combine(i, p, 1)), (2, differences), (4, y_stats),
                     (3, lambda i, p: combine(i, p, 2)), (3, lambda i, p: combine(i, p, 3)))


CHUNK = 16
CHUNKS = T // CHUNK
SETS = 2


def spectral_layer(nc, io, X, XL, const, ident, minus_half, bank, ctx, sb, sem, scratch):
    WaT, WBT, WCT = sb("s3_WaT", [P, STATE]), sb("s3_WBT", [P, STATE]), sb("s3_WCT", [P, D])
    cols = sb("s3_cols", [P, 6])
    skip_w, out_b, ones = sb("s3_skip_w", [P, D]), sb("s3_out_b", [P, NT * D]), sb("s3_ones", [P, P])
    stats, moments = sb("s3_stats", [P, NT, 6]), sb("s3_moments", [P, 2, NT, 2])
    ve, rstd = sb("s3_ve", [P, 2, 2, NT]), sb("s3_rstd", [P, 2, 2, NT])
    xn, xnT = sb("s3_xn", [P, 2, NT, D]), sb("s3_xnT", [P, 2, T])
    a_in, u_in = sb("s3_a", [P, 4, T]), sb("s3_u", [P, 4, T])
    A = sb("s3_A", [P, 2, SETS, T])
    HP = sb("s3_HP", [P, 4, SETS * CHUNKS, CHUNK])
    squares, mag = sb("s3_squares", [P, 2, SETS, T]), sb("s3_mag", [P, SETS, T])
    An, Un, Hn, gn = (sb(f"s3_{x}", [8, SETS, T]) for x in ("An", "Un", "Hn", "gn"))
    two = sb("s3_two", [P, 1])
    by, ends = sb("s3_by", [P, 3, 4, SETS * CHUNKS]), sb("s3_ends", [P, 2, 4, SETS * CHUNKS])
    loaded, gamma_ready = sem("s3_loaded"), sem("s3_gamma")
    var1, rstd1 = sem("s3_var1"), sem("s3_rstd1")
    xn_ready, turned, xnT_ready, au_ready, au_taken = (sem(f"s3_{x}") for x in ("xn_ready", "turned", "xnT_ready", "au_ready", "au_taken"))
    xnT_bank, a_bank, u_bank = bank[0], bank[1], bank[2]
    LOADS = 16 * (9 + NT)

    with nc.Block() as block:
        @block.sync
        def _(sp):
            sp.dma_start(WaT[:, :], io["WaT"][:, :]).then_inc(loaded, 16)
            sp.dma_start(WBT[:, :], io["WBT"][:, :]).then_inc(loaded, 16)
            sp.dma_start(WCT[:, :], io["WCT4"][:, :]).then_inc(loaded, 16)
            for n, name in enumerate(("ln_w", "ln_b", "Wa_b4", "WB_b4")):
                sp.dma_start(cols[:, n:n + 1], column(io[name])).then_inc(loaded, 16)
            sp.dma_start(cols[:, 4:5], io["log_gamma"].rearrange("(a n) -> a n", a=1).to_broadcast([P, 1])).then_inc(loaded, 16)
            sp.dma_start(skip_w[:, :], bcast_rows(io["D_skip"])).then_inc(loaded, 16)
            for t in range(NT):
                sp.dma_start(out_b[:, t * D:(t + 1) * D], bcast_rows(io["WC_b"])).then_inc(loaded, 16)

        @block.vector
        def _(dve):
            dve.wait_ge(gamma_ready, 1)

            def x_stats(i, p):
                q = p % 2
                layer_stats(nc, dve, tiles(X, 4 * i + p), stats, moments[:, q, :, :])
                nc.vector.tensor_scalar(ve[:, q, 0, :], moments[:, q, :, 1], LN_EPS, None, ALU.add)
                nc.vector.tensor_scalar(ve[:, q, 1, :], moments[:, q, :, 1], 1.0 + LN_EPS, LN_EPS * LN_EPS, ALU.mult,
                                        ALU.add).then_inc(var1, 1)
                dve.drain()

            def normalise(i, p):
                b, q = 4 * i + p, p % 2
                dve.wait_ge(rstd1, b + 1)
                dve.wait_ge(turned, counted(b - 1))
                for t in range(NT):
                    nc.vector.tensor_scalar(XL[:, b * NT + t, :], X[:, b * NT + t, :], moments[:, q, t, 0:1], rstd[:, q, 0, t:t + 1],
                                            ALU.subtract, ALU.mult)
                    last = nc.vector.tensor_scalar(xn[:, q, t, :], X[:, b * NT + t, :], moments[:, q, t, 0:1], rstd[:, q, 1, t:t + 1],
                                                   ALU.subtract, ALU.mult)
                last.then_inc(xn_ready, 1)
                dve.drain()

            def times_gamma(i, p):
                if p == 3:
                    dve.wait_ge(au_taken, i + 1)
                    nc.vector.tensor_scalar(a_in[:, i, :], a_in[:, i, :], cols[:, 5:6], None, ALU.mult)

            pipeline(dve, 5, (2, normalise), (0, x_stats), (4, times_gamma), unroll=4)

        @block.gpsimd
        def _(pool):
            def invert(i, p):
                q = p % 2
                pool.wait_ge(var1, 4 * i + p + 1)
                nc.gpsimd.tensor_tensor(rstd[:, q, :, :], ve[:, q, :, :], minus_half[:, 0:2 * NT].rearrange("p (a t) -> p a t", a=2),
                                        ALU.pow).then_inc(rstd1, 1)

            pipeline(pool, 5, (0, invert), unroll=4)

        @block.scalar
        def _(act):
            act.wait_ge(loaded, LOADS)
            nc.scalar.activation(cols[:, 5:6], cols[:, 4:5], ACT.Sigmoid).then_inc(gamma_ready, 1)

            def copy_xnT(i, p):
                b = 4 * i + p
                act.wait_ge(turned, b + 1)
                act.wait_ge(au_ready, counted(b - 1))
                nc.scalar.activation(xnT[:, p % 2, :], xnT_bank[:, :], ACT.Identity, scale=cols[:, 0:1], bias=cols[:, 1:2]).then_inc(xnT_ready, 1)

            def take(i, p):
                if p == 3:
                    act.wait_ge(au_ready, 4 * i + 4)
                    nc.scalar.activation(u_in[:, i, :], u_bank[:, :], ACT.Identity, bias=cols[:, 3:4])
                    nc.scalar.activation(a_in[:, i, :], a_bank[:, :], ACT.Tanh, bias=cols[:, 2:3]).then_inc(au_taken, 1)

            pipeline(act, 5, (3, take), (2, copy_xnT), unroll=4)

        @block.tensor
        def _(pe):
            pe.wait_ge(loaded, LOADS)

            def turn(i, p):
                b = 4 * i + p
                pe.wait_ge(xn_ready, b + 1)
                pe.wait_ge(xnT_ready, b)
                for t in range(NT):
                    last = nc.tensor.transpose(xnT_bank[:, t * P:(t + 1) * P], xn[:, p % 2, t, :], ident)
                last.then_inc(turned, 1)

            def project(i, p):
                pe.wait_ge(xnT_ready, 4 * i + p + 1)
                pe.wait_ge(au_taken, i)
                rows = slice(STATE * p, STATE * (p + 1))
                nc.tensor.matmul(a_bank[rows, :], WaT[:, :], xnT[:, p % 2, :], start=True, stop=True)
                nc.tensor.matmul(u_bank[rows, :], WBT[:, :], xnT[:, p % 2, :], start=True, stop=True).then_inc(au_ready, 1)

            pipeline(pe, 5, (3, project), (2, turn), unroll=4)

    spec_ready, spec_taken, squared, mag2_ready = sem("s3_spec_ready"), sem("s3_spec_taken"), sem("s3_squared"), sem("s3_mag2")
    mag_ready, clamped, gate_ready = sem("s3_mag_ready"), sem("s3_clamped"), sem("s3_gate")
    re, im = const_part(const, "dft_re"), const_part(const, "dft_im")
    ny = const_part(const, "dft_ny")
    hp_h = HP[:, :, :, :].rearrange("p (c k) m s -> p c k (m s)", c=2)
    with nc.Block() as block:
        @block.tensor
        def _(pe):
            for n, (src, mat) in enumerate(((a_in, re), (a_in, im), (u_in, re), (u_in, im))):
                for s in range(SETS):
                    for half in range(2):
                        last = nc.tensor.matmul(bank[2 * n + s][:, :], mat[:, half * P:(half + 1) * P], src[:, 2 * s + half, :],
                                                start=(half == 0), stop=(half == 1))
                    last.then_inc(spec_ready, 1)
            for n, src in enumerate((a_in, u_in)):
                for s in range(SETS):
                    pe.wait_ge(spec_taken, 2 * n + s + 1)
                    for half in range(2):
                        last = nc.tensor.matmul(bank[2 * n + s][0:8, :], ny[:, half * 8:half * 8 + 8], src[:, 2 * s + half, :],
                                                start=(half == 0), stop=(half == 1))
                    last.then_inc(spec_ready, 1)

        @block.scalar
        def _(act):
            for n in range(4):
                for s in range(SETS):
                    act.wait_ge(spec_ready, 2 * n + s + 1)
                    dst = A[:, n % 2, s, :] if n < 2 else hp_h[:, n % 2, 0, s * T:(s + 1) * T]
                    nc.scalar.activation(dst, bank[2 * n + s][:, :], ACT.Copy).then_inc(spec_taken, 1)
                if n == 1:
                    act.drain()
                    nc.scalar.activation(squares[:, :, :, :], A[:, :, :, :], ACT.Square).then_inc(squared, 1)
            for n, dst in enumerate((An, Un)):
                for s in range(SETS):
                    act.wait_ge(spec_ready, 8 + 2 * n + s + 1)
                    nc.scalar.activation(dst[:, s, :], bank[2 * n + s][0:8, :], ACT.Copy)
            act.drain()
            nc.scalar.activation(gn[:, :, :], An[:, :, :], ACT.Abs)
            act.wait_ge(mag2_ready, 1)
            nc.scalar.activation(mag[:, :, :], squares[:, 0, :, :], ACT.Sqrt).then_inc(mag_ready, 1)
            act.wait_ge(clamped, 1)
            nc.scalar.activation(mag[:, :, :], mag[:, :, :], ACT.Sigmoid, scale=-2.0, bias=two[:, :])
            nc.scalar.activation(gn[:, :, :], gn[:, :, :], ACT.Sigmoid, scale=-2.0, bias=two[0:8, :]).then_inc(gate_ready, 1)


        @block.vector
        def _(dve):
            nc.vector.memset(two[:, :], 2.0)
            nc.vector.memset(ones[:, :], 1.0)
            nc.vector.memset(HP[:, :, :, :].rearrange("p (c k) m s -> p c k (m s)", c=2)[:, :, 1, :], 0.0)
            dve.wait_ge(squared, 1)
            nc.vector.tensor_tensor(squares[:, 0, :, :], squares[:, 0, :, :], squares[:, 1, :, :], ALU.add).then_inc(mag2_ready, 1)
            dve.wait_ge(mag_ready, 1)
            nc.vector.tensor_scalar(mag[:, :, :], mag[:, :, :], 1e-8, None, ALU.max)
            nc.vector.tensor_scalar(gn[:, :, :], gn[:, :, :], 1e-8, None, ALU.max).then_inc(clamped, 1)
            dve.wait_ge(gate_ready, 1)
            dve.wait_ge(spec_taken, 8)
            for c in range(2):
                nc.vector.tensor_tensor(A[:, c, :, :], A[:, c, :, :], mag[:, :, :], ALU.mult)
            nc.vector.tensor_tensor(An[:, :, :], An[:, :, :], gn[:, :, :], ALU.mult)
            dve.drain()
            for s in range(SETS):
                nc.vector.tensor_tensor_scan(Hn[:, s, :], An[:, s, :], Un[:, s, :], 0.0, ALU.mult, ALU.add)
            Am = A[:, :, :, :].rearrange("p c s (k t) -> p c (s k) t", t=CHUNK)
            M = SETS * CHUNKS
            by_re, by_im, step = by[:, 0, :, :], by[:, 1, :, :], by[:, 2, :, :]

            def times(dst, left_re, left_im, right):
                nc.vector.tensor_tensor(dst[0], left_re, right, ALU.mult)
                nc.vector.tensor_tensor(dst[1], left_im, right, ALU.mult)
                dve.drain()
                nc.vector.tensor_tensor(dst[2][:, 0:2], dst[0][:, 0:2], dst[1][:, 2:4], ALU.subtract)
                nc.vector.tensor_tensor(dst[2][:, 2:4], dst[0][:, 2:4], dst[1][:, 0:2], ALU.add)
                dve.drain()

            for c in range(2):
                nc.vector.tensor_copy(HP[:, 2 * c + 1, :, 0], Am[:, c, :, 0])
            dve.drain()
            for s in range(1, CHUNK):
                times((by_re, by_im, step), Am[:, 0, :, s].unsqueeze(1).to_broadcast([P, 4, M]),
                      Am[:, 1, :, s].unsqueeze(1).to_broadcast([P, 4, M]), HP[:, :, :, s - 1])
                nc.vector.tensor_tensor(HP[:, :, :, s], HP[:, :, :, s], step, ALU.add)
                dve.drain()
            nc.vector.tensor_copy(ends[:, 0, :, :], HP[:, :, :, CHUNK - 1])
            dve.drain()
            now, d = 0, 1
            while d < CHUNKS:
                cur, new = (ends[:, n, :, :].rearrange("p q (s k) -> p q s k", s=SETS) for n in (now, 1 - now))
                n = CHUNKS - d
                v = [by[:, m, :, :].rearrange("p q (s k) -> p q s k", s=SETS)[:, :, :, 0:n] for m in range(3)]
                for s in range(SETS):
                    w = [x[:, :, s, :] for x in v]
                    times(w, cur[:, 1, s, d:].unsqueeze(1).to_broadcast([P, 4, n]),
                          cur[:, 3, s, d:].unsqueeze(1).to_broadcast([P, 4, n]), cur[:, :, s, 0:n])
                for c in range(2):
                    nc.vector.tensor_tensor(new[:, 2 * c, :, d:], cur[:, 2 * c, :, d:], v[2][:, 2 * c], ALU.add)
                    nc.vector.tensor_copy(new[:, 2 * c + 1, :, d:], v[2][:, 2 * c + 1])
                nc.vector.tensor_copy(new[:, :, :, 0:d], cur[:, :, :, 0:d])
                dve.drain()
                now, d = 1 - now, 2 * d
            flat = squares[:, :, :, :].rearrange("p c s (k t) -> p c s k t", t=CHUNK)
            hp5 = HP[:, :, :, :].rearrange("p q (s k) t -> p q s k t", s=SETS)
            carry = ends[:, now, :, :].rearrange("p q (s k) -> p q s k", s=SETS)
            n = CHUNKS - 1
            for c in range(2):
                for half, (x, y) in enumerate(((1, 2 * c), (3, 2 - 2 * c))):
                    nc.vector.tensor_tensor(flat[:, half, :, 1:, :], hp5[:, x, :, 1:, :],
                                            carry[:, y, :, 0:n].unsqueeze(3).to_broadcast([P, SETS, n, CHUNK]), ALU.mult)
                dve.drain()
                nc.vector.tensor_tensor(flat[:, 0, :, 1:, :], flat[:, 0, :, 1:, :], flat[:, 1, :, 1:, :],
                                        ALU.subtract if c == 0 else ALU.add)
                dve.drain()
                nc.vector.tensor_tensor(hp5[:, 2 * c, :, 1:, :], hp5[:, 2 * c, :, 1:, :], flat[:, 0, :, 1:, :], ALU.add)
                dve.drain()


    hT = sb("s3_hT", [P, 2, T])
    y, z, skip = (sb(f"s3_{x}", [P, 2, NT, D]) for x in ("y", "z", "skip"))
    stats2, moments2 = sb("s3_stats2", [P, NT, 6]), sb("s3_moments2", [P, 2, NT, 2])
    h_ready, h_taken, y_ready, y_taken = (sem(f"s3_{x}") for x in ("h_ready", "h_taken", "y_ready", "y_taken"))
    skip_ready, var2, rstd2, z_ready, added = (sem(f"s3_{x}") for x in ("skip_ready", "var2", "rstd2", "z_ready", "added"))
    ire, iim, iny = const_part(const, "inv_re"), const_part(const, "inv_im"), const_part(const, "inv_ny", 8)
    h_bank, y_bank = bank[0:2], bank[2:4]
    with nc.Block() as block:
        @block.tensor
        def _(pe):
            def states(i, p):
                half = p // 4
                if p % 4 == 0:
                    lhs = slice(half * P, (half + 1) * P)
                    pe.wait_ge(h_taken, counted(2 * i + half - 1))
                    nc.tensor.matmul(h_bank[half][:, :], ire[:, lhs], hp_h[:, 0, 0, bass.ds(i * T, T)], start=True, stop=False)
                    nc.tensor.matmul(h_bank[half][:, :], iim[:, lhs], hp_h[:, 1, 0, bass.ds(i * T, T)], start=False, stop=False)
                    nc.tensor.matmul(h_bank[half][:, :], iny[:, lhs], Hn[:, i, :], start=False, stop=True).then_inc(h_ready, 1)

            def output(i, p):
                b, j, half = 8 * i + p, p % 4, p // 4
                pe.wait_ge(h_taken, 2 * i + half + 1)
                pe.wait_ge(y_taken, counted(b - 1))
                rows = slice(STATE * j, STATE * (j + 1))
                row = slice(STATE * j, STATE * j + 1)
                nc.tensor.matmul(y_bank[p % 2][:, :], ones[row, :], out_b[row, :], start=True, stop=False)
                for t in range(NT):
                    last = nc.tensor.matmul(y_bank[p % 2][:, t * P:(t + 1) * P], hT[rows, half, t * P:(t + 1) * P], WCT[rows, :],
                                            start=False, stop=(t == NT - 1))
                last.then_inc(y_ready, 1)

            pipeline(pe, 4, (1, output), (0, states), unroll=8)

        @block.scalar
        def _(act):
            def take(i, p):
                half = p // 4
                if p % 4 == 0:
                    act.wait_ge(h_ready, 2 * i + half + 1)
                    act.wait_ge(y_ready, counted(8 * i + 4 * half - 4))
                    nc.scalar.activation(hT[:, half, :], h_bank[half][:, :], ACT.Copy).then_inc(h_taken, 1)

            pipeline(act, 4, (0, take), unroll=8)

        @block.gpsimd
        def _(pool):
            def skips(i, p):
                b = 8 * i + p
                pool.wait_ge(y_taken, counted(b - 1))
                nc.gpsimd.tensor_tensor(skip[:, p % 2, :, :], tiles(XL, b), skip_w[:, :].unsqueeze(1).to_broadcast([P, NT, D]),
                                        ALU.mult).then_inc(skip_ready, 1)

            def invert(i, p):
                pool.wait_ge(var2, 8 * i + p + 1)
                nc.gpsimd.tensor_tensor(rstd[:, p % 2, 1, :], ve[:, p % 2, 1, :], minus_half[:, 0:NT], ALU.pow).then_inc(rstd2, 1)

            def add(i, p):
                b = 8 * i + p
                pool.wait_ge(z_ready, b + 1)
                nc.gpsimd.tensor_tensor(tiles(X, b), tiles(X, b), z[:, p % 2, :, :], ALU.add).then_inc(added, 1)

            pipeline(pool, 4, (0, skips), (2, invert), (3, add), unroll=8)

        @block.vector
        def _(dve):
            def add_skip(i, p):
                b, q = 8 * i + p, p % 2
                dve.wait_ge(y_ready, b + 1)
                dve.wait_ge(skip_ready, b + 1)
                nc.vector.tensor_tensor(y[:, q, :, :], y_bank[q][:, :].rearrange("p (t f) -> p t f", t=NT), skip[:, q, :, :],
                                        ALU.add).then_inc(y_taken, 1)
                dve.drain()
                layer_stats(nc, dve, y[:, q, :, :], stats2, moments2[:, q, :, :])
                nc.vector.tensor_scalar(ve[:, q, 1, :], moments2[:, q, :, 1], LN_EPS, None, ALU.add).then_inc(var2, 1)
                dve.drain()

            def normalise_y(i, p):
                b, q = 8 * i + p, p % 2
                dve.wait_ge(rstd2, b + 1)
                dve.wait_ge(added, counted(b - 1))
                for t in range(NT):
                    last = nc.vector.tensor_scalar(z[:, q, t, :], y[:, q, t, :], moments2[:, q, t, 0:1], rstd[:, q, 1, t:t + 1],
                                                   ALU.subtract, ALU.mult)
                last.then_inc(z_ready, 1)
                dve.drain()

            pipeline(dve, 4, (2, add_skip), (3, normalise_y), unroll=8)


def swiglu_layer(nc, io, X, XL, const, ident, minus_half, bank, ctx, sb, sem, scratch):
    HC = HIDDEN // P
    STAGES = 6
    raw = sb("s4_raw", [P, 3, HIDDEN], I32)
    wg, wu, wd = sb("s4_wg", [P, HIDDEN]), sb("s4_wu", [P, HIDDEN]), sb("s4_wd", [P, HC, D])
    stats, moments = sb("s4_stats", [P, NT, 6]), sb("s4_moments", [P, 2, 2, NT, 2])
    stats2 = sb("s4_stats2", [P, NT, 6])
    ve, rstd = sb("s4_ve", [P, 2, 2, NT]), sb("s4_rstd", [P, 2, 2, NT])
    xl, z = sb("s4_xl", [P, 2, NT, D]), sb("s4_z", [P, 2, NT, D])
    xT, yT = sb("s4_xT", [P, 2, T]), sb("s4_yT", [P, 2, T])
    silu, hid = sb("s4_silu", [P, 2, T]), sb("s4_hid", [P, 2, HC, T])
    loaded, scaled = sem("s4_loaded"), sem("s4_scaled")
    var1, rstd1, var2, rstd2 = sem("s4_var1"), sem("s4_rstd1"), sem("s4_var2"), sem("s4_rstd2")
    xl_ready, turned, xT_ready = sem("s4_xl_ready"), sem("s4_turned"), sem("s4_xT_ready")
    gate_ready, up_ready, silu_ready = sem("s4_gate_ready"), sem("s4_up_ready"), sem("s4_silu_ready")
    hid_ready, yT_ready, yT_copied, y_ready = sem("s4_hid_ready"), sem("s4_yT_ready"), sem("s4_yT_copied"), sem("s4_y_ready")
    z_ready, added, stored = sem("s4_z_ready"), sem("s4_added"), sem("s4_stored")
    xT_bank, yT_bank, y_bank, gate_bank, up_bank = bank[0], bank[1], bank[2:4], bank[4:6], bank[6:8]
    out_dram = io["out"].rearrange("b (t p) f -> p (b t) f", p=P)

    with nc.Block() as block:
        @block.sync
        def _(sp):
            sp.dma_start(raw[:, 0, :], io["w_gateT"][:, :]).then_inc(loaded, 16)
            sp.dma_start(raw[:, 1, :], io["w_upT"][:, :]).then_inc(loaded, 16)
            sp.dma_start(raw[:, 2, :].rearrange("p (c f) -> p c f", c=HC),
                         io["w_downT"].rearrange("(c p) f -> p c f", p=P)).then_inc(loaded, 16)
            with sp.Fori(0, B) as b:
                sp.wait_ge(added, b + 1)
                sp.dma_start(out_dram[:, bass.ds(b * NT, NT), :], tiles(X, b)).then_inc(stored, 16)
            sp.wait_ge(stored, 16 * B)

        @block.vector
        def _(dve):
            dve.wait_ge(loaded, 48)
            scale = float(np.float32(1.0 / 127.0))
            nc.vector.tensor_scalar(wg[:, :], raw[:, 0, :], scale, None, ALU.mult)
            nc.vector.tensor_scalar(wu[:, :], raw[:, 1, :], scale, None, ALU.mult)
            nc.vector.tensor_scalar(wd[:, :, :], raw[:, 2, :].rearrange("p (c f) -> p c f", c=HC), scale, None,
                                    ALU.mult).then_inc(scaled, 1)

            def x_stats(i, p):
                b = 2 * i + p
                layer_stats(nc, dve, tiles(X, b), stats, moments[:, p, 0, :, :])
                nc.vector.tensor_scalar(ve[:, p, 0, :], moments[:, p, 0, :, 1], LN_EPS, None, ALU.add).then_inc(var1, 1)
                dve.drain()

            def normalise(i, p):
                b = 2 * i + p
                dve.wait_ge(rstd1, b + 1)
                dve.wait_ge(turned, counted(b - 1))
                for t in range(NT):
                    last = nc.vector.tensor_scalar(xl[:, p, t, :], X[:, b * NT + t, :], moments[:, p, 0, t, 0:1],
                                                   rstd[:, p, 0, t:t + 1], ALU.subtract, ALU.mult)
                last.then_inc(xl_ready, 1)
                dve.drain()

            def gate(i, p):
                b = 2 * i + p
                dve.wait_ge(yT_ready, counted(b - 1))
                for c in range(HC):
                    dve.wait_ge(silu_ready, HC * b + c + 1)
                    dve.wait_ge(up_ready, HC * b + c + 1)
                    nc.vector.tensor_tensor(hid[:, p, c, :], silu[:, (p + c) % 2, :], up_bank[(p + c) % 2][:, :], ALU.mult).then_inc(hid_ready, 1)

            def y_stats(i, p):
                b = 2 * i + p
                dve.wait_ge(y_ready, b + 1)
                layer_stats(nc, dve, y_bank[p][:, :].rearrange("p (t f) -> p t f", t=NT), stats2, moments[:, p, 1, :, :])
                nc.vector.tensor_scalar(ve[:, p, 1, :], moments[:, p, 1, :, 1], LN_EPS, None, ALU.add).then_inc(var2, 1)
                dve.drain()

            def normalise_y(i, p):
                b = 2 * i + p
                dve.wait_ge(rstd2, b + 1)
                dve.wait_ge(added, counted(b - 1))
                for t in range(NT):
                    last = nc.vector.tensor_scalar(z[:, p, t, :], y_bank[p][:, t * P:(t + 1) * P], moments[:, p, 1, t, 0:1],
                                                   rstd[:, p, 1, t:t + 1], ALU.subtract, ALU.mult)
                last.then_inc(z_ready, 1)
                dve.drain()

            pipeline(dve, STAGES, (5, normalise_y), (0, x_stats), (1, normalise), (4, y_stats), (2, gate))

        @block.gpsimd
        def _(pool):
            def invert_x(i, p):
                pool.wait_ge(var1, 2 * i + p + 1)
                nc.gpsimd.tensor_tensor(rstd[:, p, 0, :], ve[:, p, 0, :], minus_half[:, 0:NT], ALU.pow).then_inc(rstd1, 1)

            def invert_y(i, p):
                pool.wait_ge(var2, 2 * i + p + 1)
                nc.gpsimd.tensor_tensor(rstd[:, p, 1, :], ve[:, p, 1, :], minus_half[:, 0:NT], ALU.pow).then_inc(rstd2, 1)

            def add(i, p):
                b = 2 * i + p
                pool.wait_ge(z_ready, b + 1)
                nc.gpsimd.tensor_tensor(tiles(X, b), tiles(X, b), z[:, p, :, :], ALU.add).then_inc(added, 1)

            pipeline(pool, STAGES, (5, add), (0, invert_x), (4, invert_y))

        @block.scalar
        def _(act):
            def copy_xT(i, p):
                b = 2 * i + p
                act.wait_ge(turned, b + 1)
                act.wait_ge(up_ready, counted(HC * (b - 1)))
                nc.scalar.activation(xT[:, p, :], xT_bank[:, :], ACT.Copy).then_inc(xT_ready, 1)

            def silus(i, p):
                b = 2 * i + p
                for c in range(HC):
                    act.wait_ge(gate_ready, HC * b + c + 1)
                    act.wait_ge(hid_ready, counted(HC * b + c - 1))
                    nc.scalar.activation(silu[:, (p + c) % 2, :], gate_bank[(p + c) % 2][:, :], ACT.Silu).then_inc(silu_ready, 1)

            def copy_yT(i, p):
                b = 2 * i + p
                act.wait_ge(yT_ready, b + 1)
                act.wait_ge(y_ready, counted(b - 1))
                nc.scalar.activation(yT[:, p, :], yT_bank[:, :], ACT.Copy).then_inc(yT_copied, 1)

            pipeline(act, STAGES, (3, copy_yT), (2, silus), (1, copy_xT))

        @block.tensor
        def _(pe):
            pe.wait_ge(scaled, 1)

            def turn(i, p):
                b = 2 * i + p
                pe.wait_ge(xl_ready, b + 1)
                pe.wait_ge(xT_ready, b)
                for t in range(NT):
                    last = nc.tensor.transpose(xT_bank[:, t * P:(t + 1) * P], xl[:, p, t, :], ident)
                last.then_inc(turned, 1)

            def gate_and_up(i, p):
                b = 2 * i + p
                pe.wait_ge(xT_ready, b + 1)
                for c in range(HC):
                    pe.wait_ge(silu_ready, counted(HC * b + c - 1))
                    nc.tensor.matmul(gate_bank[(p + c) % 2][:, :], wg[:, c * P:(c + 1) * P], xT[:, p, :], start=True,
                                     stop=True).then_inc(gate_ready, 1)
                    pe.wait_ge(hid_ready, counted(HC * b + c - 1))
                    nc.tensor.matmul(up_bank[(p + c) % 2][:, :], wu[:, c * P:(c + 1) * P], xT[:, p, :], start=True,
                                     stop=True).then_inc(up_ready, 1)

            def down(i, p):
                b = 2 * i + p
                pe.wait_ge(hid_ready, HC * (b + 1))
                pe.wait_ge(yT_copied, b)
                for c in range(HC):
                    last = nc.tensor.matmul(yT_bank[:, :], wd[:, c, :], hid[:, p, c, :], start=(c == 0), stop=(c == HC - 1))
                last.then_inc(yT_ready, 1)

            def turn_y(i, p):
                b = 2 * i + p
                pe.wait_ge(yT_copied, b + 1)
                pe.wait_ge(z_ready, counted(b - 1))
                for t in range(NT):
                    last = nc.tensor.transpose(y_bank[p][:, t * P:(t + 1) * P], yT[:, p, t * P:(t + 1) * P], ident)
                last.then_inc(y_ready, 1)

            pipeline(pe, STAGES, (4, turn_y), (3, down), (2, gate_and_up), (1, turn))


def load_only(nc, io, X, XL, const, ident, minus_half, bank, ctx, sb, sem, scratch):
    l = sem("lo_in")
    with nc.Block() as block:
        @block.sync
        def _(sp):
            sp.dma_start(const[:, :], io["consts"][:, :]).then_inc(l, 16)
            sp.dma_start(X[:, :, :], io["x"].rearrange("b (t p) f -> p (b t) f", p=P)).then_inc(l, 16)
            sp.wait_ge(l, 32)
        @block.vector
        def _(dve):
            nc.vector.memset(minus_half[:, :], -0.5)


def store_only(nc, io, X, XL, const, ident, minus_half, bank, ctx, sb, sem, scratch):
    out_done = sem("so_out")
    with nc.Block() as block:
        @block.sync
        def _(sp):
            sp.dma_start(io["out"].rearrange("b (t p) f -> p (b t) f", p=P), X[:, :, :]).then_inc(out_done, 16)
            sp.wait_ge(out_done, 16)


PHASES = [first_layer, qkv_layer, attention_layer, expert_layer, spectral_layer, swiglu_layer]


def laid_out(v):
    col = np.ascontiguousarray
    t = lambda a: col(np.asarray(a).T)
    a = {k: np.asarray(x) for k, x in v.items()}
    perm = np.array([(2 * pair + par) * HD + d for par in range(2) for d in range(HD) for pair in range(PAIRS)])
    dims = np.array([d for par in range(2) for d in range(HD) for pair in range(PAIRS)])
    return {
        "WqT": t(a["L0_ffn_wq"])[:, perm], "WkT": t(a["L0_ffn_wk"])[:, perm], "WvT": t(a["L0_ffn_wv"]),
        "WoT": t(a["L0_ffn_wo"])[:, MASKED:], "n1_w": a["L0_ffn_n1_w"], "qn_w": a["L0_ffn_qn_w"][dims],
        "kn_w": a["L0_ffn_kn_w"][dims], "n2_w": a["L0_ffn_n2_w"], "gateT": t(a["L0_ffn_gate_w"]),
        "e0uT": t(a["L0_ffn_e0_up"]), "e1aT": t(a["L0_ffn_e1_w1"]), "e1bT": t(a["L0_ffn_e1_w2"]),
        "e2aT": t(a["L0_ffn_e2_l1"]), "e2bT": t(a["L0_ffn_e2_l2"]), "e2cT": t(a["L0_ffn_e2_l3"]),
        "e3aT": t(a["L0_ffn_e3_down"]), "e3bT": t(a["L0_ffn_e3_up"]),
        "d0T": t(a["L0_ffn_e0_down"])[:, MASKED:], "d1T": t(a["L0_ffn_e1_down"])[:, MASKED:],
        "d2T": t(a["L0_ffn_e2_l4"])[:, MASKED:], "d3T": t(a["L0_ffn_e3_out"])[:, MASKED:],
        "x": a["L0_attn_x"], "A": a["L0_attn_A"], "BT": t(a["L0_attn_B"]), "WT": t(a["L0_attn_W"]), "b": a["L0_attn_b"],
        "WaT": t(a["L1_attn_Wa_w"]), "WBT": t(a["L1_attn_WB_w"]), "WCT4": np.tile(t(a["L1_attn_WC_w"]), (4, 1)),
        "ln_w": a["L1_attn_ln_w"], "ln_b": a["L1_attn_ln_b"], "Wa_b4": np.tile(a["L1_attn_Wa_b"], 4),
        "WB_b4": np.tile(a["L1_attn_WB_b"], 4), "log_gamma": a["L1_attn_log_gamma"].reshape(1),
        "D_skip": a["L1_attn_D_skip"], "WC_b": a["L1_attn_WC_b"],
        "w_gateT": t(a["L1_ffn_w_gate"]), "w_upT": t(a["L1_ffn_w_up"]), "w_downT": t(a["L1_ffn_w_down"]),
    }


def kernel(**inputs):
    import numpy as _np
    import concourse.bacc as _bacc
    from concourse import mybir as _mybir
    from concourse.bass_utils import run_bass_kernel_spmd as _run

    nc = _bacc.Bacc("TRN2", target_bir_lowering=False, num_devices=1)
    arrays, io = {}, {}
    for name, a in {**laid_out(inputs), "consts": constant_table()}.items():
        a = _np.ascontiguousarray(a)
        arrays[f"in_{name}"] = a
        io[name] = nc.dram_tensor(f"in_{name}", a.shape, _mybir.dt.from_np(a.dtype), kind="ExternalInput").ap()
    io["out"] = nc.dram_tensor("out_0", (B, T, D), _mybir.dt.float32, kind="ExternalOutput").ap()
    build(nc, io)
    r = _run(nc, [arrays], core_ids=[0])
    return r.results[0]["out_0"]
```

```python
import math
from contextlib import ExitStack

import numpy as np

import concourse.bass as bass
from concourse import mybir

F32 = mybir.dt.float32
BF16 = mybir.dt.bfloat16
I32 = mybir.dt.int32
F32R = mybir.dt.float32r
ALU = mybir.AluOpType
ACT = mybir.ActivationFunctionType
AX = mybir.AxisListType

P = 128
B, T, D = 16, 512, 128
NT = T // P
TILES = B * NT
LN_EPS = 1e-5
RMS_EPS = 1.1920929e-07
HEADS, HD = 16, 8
PAIRS = HEADS // 2
GROUP = 4
MASKED = 32
WIDE = D - MASKED
STATE = 32
FREQS = STATE // 2
SLOTS = 6
HIDDEN = 384
NEG = -1.0e30
FMAX = 3.4028234663852886e38

_WIDTHS = [("ident", P), ("mask", P), ("headmean", P), ("dft_re", 2 * P), ("dft_im", 2 * P), ("dft_ny", 16),
           ("inv_re", 2 * P), ("inv_im", 2 * P), ("inv_ny", 2 * P), ("earlier", 16)]
COLS, _at = {}, 0
for _name, _w in _WIDTHS:
    COLS[_name] = (_at, _at + _w)
    _at += _w
NCONST = _at


def constant_table():
    c = np.zeros((P, NCONST), np.float64)

    def put(name, a):
        c[:a.shape[0], COLS[name][0]:COLS[name][1]] = a

    put("ident", np.eye(P))
    put("mask", np.where(np.arange(P)[None, :] > np.arange(P)[:, None], NEG, 0.0))
    row = np.arange(P)
    same = (row[:, None] // 64 == row[None, :] // 64) & (row[:, None] % PAIRS == row[None, :] % PAIRS)
    put("headmean", same / HD)
    n, f = np.arange(STATE)[:, None], np.arange(FREQS)[None, :]
    turn = 2 * np.pi * ((n * f) % STATE) / STATE
    alt = (-1.0) ** np.arange(STATE)
    re, im = np.cos(turn), -np.sin(turn)
    twice = np.where(f == 0, 1.0, 2.0) / STATE
    dre, dim = np.zeros((P, 2, P)), np.zeros((P, 2, P))
    ire, iim = np.zeros((P, 2, P)), np.zeros((P, 2, P))
    dny, iny = np.zeros((P, 2, 8)), np.zeros((8, 2, P))
    for half in range(2):
        for j in range(4):
            rows, cols = slice(STATE * j, STATE * (j + 1)), slice(FREQS * (4 * half + j), FREQS * (4 * half + j + 1))
            dre[rows, half, cols], dim[rows, half, cols] = re, im
            ire[cols, half, rows], iim[cols, half, rows] = (re * twice).T, (im * twice).T
            dny[rows, half, 4 * half + j] = alt
            iny[4 * half + j, half, rows] = alt / STATE
    put("dft_re", dre.reshape(P, -1)), put("dft_im", dim.reshape(P, -1)), put("dft_ny", dny.reshape(P, -1))
    put("inv_re", ire.reshape(P, -1)), put("inv_im", iim.reshape(P, -1)), put("inv_ny", iny.reshape(8, -1))
    e = np.arange(4)
    put("earlier", np.tile((e[None, :] < e[:, None]).astype(float).reshape(1, 16), (P, 1)))
    return c.astype(np.float32)


def pipeline(eng, depth, *stages, unroll=2):
    lead = -(-(depth + 1) // unroll) * unroll

    def peeled(step):
        for s, work in stages:
            if 0 <= step - s < B:
                work((step - s) // unroll, (step - s) % unroll)
    for step in range(lead):
        peeled(step)
    with eng.Fori(0, (B - lead) // unroll) as i:
        for n in range(unroll):
            for s, work in stages:
                p = (n - s) % unroll
                work(i + (lead + n - s - p) // unroll, p)
    for step in range(B, B + depth - 1):
        peeled(step)


class Linear:
    def __init__(self, i, per, start, rest=0):
        self.i, self.per, self.start, self.rest = i, per, start, rest

    def __add__(self, n):
        return Linear(self.i, self.per, self.start, self.rest + n)

    def __sub__(self, n):
        return self + -n

    def __mul__(self, n):
        return Linear(self.i, self.per * n, self.start * n, self.rest * n)

    def __rmul__(self, n):
        return self * n

    __radd__ = __add__


def counted(n):
    if isinstance(n, Linear):
        base = n.i * n.per + n.start if n.start else n.i * n.per
        return base + n.rest
    return max(n, 0) if isinstance(n, int) else n


def tiles(buf, b):
    return buf[:, bass.ds(b * NT, NT), :]


def layer_stats(nc, dve, src, stats, moments):
    for t in range(NT):
        nc.vector.bn_stats(stats[:, t, :], src[:, t, :])
    dve.drain()
    for t in range(NT):
        nc.vector.bn_aggr(moments[:, t, :], stats[:, t, :])
    dve.drain()


def keep_high(ops, dst, src):
    return ops.tensor_copy(dst, src)


def keep_low(ops, dst, src, high):
    return ops.tensor_tensor(dst, src, high.bitcast(F32), ALU.subtract)


def const_part(const, name, rows=P):
    return const[0:rows, COLS[name][0]:COLS[name][1]]


def bcast_rows(ap, n=P):
    return ap.rearrange("(a n) -> a n", a=1).to_broadcast([n, ap.shape[0]])


def column(ap):
    return ap.rearrange("(n a) -> n a", a=1)


EXPERT_WEIGHTS = {"e0u": (1, 256), "e1a": (1, 256), "e1b": (1, 256), "e2a": (1, 256), "e2b": (2, 256), "e2c": (2, 256),
                  "e3a": (1, 128), "e3b": (1, 256)}


SPLIT_WEIGHTS = ("e0u", "e1a", "e1b", "e2a", "e2c", "e3a", "wg", "wu")


def weight_tiles(sb):
    w = {name: sb(name, [P, D]) for name in ("Wq", "Wk", "Wv")}
    w["qkv_cols"] = sb("qkv_cols", [P, 4])
    w["Wo"] = sb("Wo", [P, WIDE])
    w.update({name: sb(name, [P, n, width]) for name, (n, width) in EXPERT_WEIGHTS.items()})
    w["down"], w["gate"], w["n2w"] = sb("down", [P, EXPERTS, HC2, WIDE]), sb("gate", [P, EXPERTS]), sb("n2w", [P, 1])
    w["WaT"], w["WBT"], w["WCT"] = sb("WaT", [P, STATE]), sb("WBT", [P, STATE]), sb("WCT", [P, D])
    w["ssm_cols"] = sb("ssm_cols", [P, 6])
    w["skip_w"], w["out_b"] = sb("skip_w", [P, D]), sb("out_b", [P, NT * D])
    w["swiglu"] = sb("swiglu", [P, 3, HIDDEN], I32)
    w["wg"], w["wu"], w["wd"] = sb("wg", [P, HIDDEN]), sb("wu", [P, HIDDEN]), sb("wd", [P, HIDDEN // P, D])
    w["parts"] = {name: [sb(f"{name}_part{n}", [P] + list(w[name].shape[1:]), F32R) for n in range(2)] for name in SPLIT_WEIGHTS}
    return w


def prepare_weights(nc, dve, w):
    scale = float(np.float32(1.0 / 127.0))
    raw = w["swiglu"]
    nc.vector.tensor_scalar(w["wg"][:, :], raw[:, 0, :], scale, None, ALU.mult)
    nc.vector.tensor_scalar(w["wu"][:, :], raw[:, 1, :], scale, None, ALU.mult)
    nc.vector.tensor_scalar(w["wd"][:, :, :], raw[:, 2, :].rearrange("p (c f) -> p c f", c=HIDDEN // P), scale, None, ALU.mult)
    dve.drain()

    def all_of(name, tile):
        return tile[:, :, :] if name in EXPERT_WEIGHTS else tile[:, :]

    for name in SPLIT_WEIGHTS:
        keep_high(nc.vector, all_of(name, w["parts"][name][0]), all_of(name, w[name]))
    dve.drain()
    for name in SPLIT_WEIGHTS:
        high, low = (all_of(name, part) for part in w["parts"][name])
        keep_low(nc.vector, low, all_of(name, w[name]), high)
    dve.drain()


def weight_loads(w, io):
    for name in ("Wq", "Wk", "Wv"):
        yield w[name][:, :], io[name + "T"][:, :]
    for n, name in enumerate(("n1_w", "qn_w", "kn_w")):
        yield w["qkv_cols"][:, n:n + 1], column(io[name])
    yield w["Wo"][:, :], io["WoT"][:, :]
    for name in EXPERT_WEIGHTS:
        yield w[name][:, :, :], io[name + "T"].rearrange("(c p) f -> p c f", p=P)
    for e in range(EXPERTS):
        n = io[f"d{e}T"].shape[0] // P
        yield w["down"][:, e, 0:n, :], io[f"d{e}T"].rearrange("(c p) f -> p c f", p=P)
    yield w["gate"][:, :], io["gateT"][:, :]
    yield w["n2w"][:, :], column(io["n2_w"])
    yield w["WaT"][:, :], io["WaT"][:, :]
    yield w["WBT"][:, :], io["WBT"][:, :]
    yield w["WCT"][:, :], io["WCT4"][:, :]
    for n, name in enumerate(("ln_w", "ln_b", "Wa_b4", "WB_b4")):
        yield w["ssm_cols"][:, n:n + 1], column(io[name])
    yield w["ssm_cols"][:, 4:5], io["log_gamma"].rearrange("(a n) -> a n", a=1).to_broadcast([P, 1])
    yield w["skip_w"][:, :], bcast_rows(io["D_skip"])
    for t in range(NT):
        yield w["out_b"][:, t * D:(t + 1) * D], bcast_rows(io["WC_b"])
    yield w["swiglu"][:, 0, :], io["w_gateT"][:, :]
    yield w["swiglu"][:, 1, :], io["w_upT"][:, :]
    yield w["swiglu"][:, 2, :].rearrange("p (c f) -> p c f", c=HIDDEN // P), io["w_downT"].rearrange("(c p) f -> p c f", p=P)


def first_layer(nc, io, X, XL, const, ident, minus_half, bank, sb, sem, scratch, w):
    BT, WT = sb("s1_BT", [P, P]), sb("s1_WT", [P, P])
    Acol, Arow = sb("s1_A", [P, 1]), sb("s1_Abc", [P, T])
    bias, ones = sb("s1_bias", [1, NT * D]), sb("s1_ones", [1, P])
    stats, moments = sb("s1_stats", [P, NT, 6]), sb("s1_moments", [P, 2, 2, NT, 2])
    minus_mean = sb("s1_minus_mean", [P, 2, NT])
    ve, rstd = sb("s1_ve", [P, 2, 2, NT]), sb("s1_rstd", [P, 2, 2, NT])
    xl, z = sb("s1_xl", [P, 2, NT, D]), sb("s1_z", [P, 2, NT, D])
    stats2 = sb("s1_stats2", [P, NT, 6])
    xT, h = sb("s1_xT", [P, 2, T]), sb("s1_h", [P, 2, T])
    loaded, x_in = sem("s1_loaded"), [sem(f"s1_x{n}") for n in range(4)]
    filled, weights_in = sem("s1_filled"), sem("s1_weights_in")
    var1, rstd1, var2, rstd2 = sem("s1_var1"), sem("s1_rstd1"), sem("s1_var2"), sem("s1_rstd2")
    xl_ready, turned, xT_ready, u_ready = sem("s1_xl_ready"), sem("s1_turned"), sem("s1_xT_ready"), sem("s1_u_ready")
    h_ready, y_ready, z_ready, added = sem("s1_h_ready"), sem("s1_y_ready"), sem("s1_z_ready"), sem("s1_added")
    xT_bank, u_bank, y_bank = bank[0:2], bank[2:4], bank[4:6]
    x_dram = io["x"].rearrange("b (t p) f -> p (b t) f", p=P)
    PIECE, LOADS = TILES // 4, 8 * 16
    STAGES, PEELED = 5, 6

    with nc.Block() as block:
        @block.sync
        def _(sp):
            sp.dma_start(const[:, :], io["consts"][:, :]).then_inc(loaded, 16)
            for n in range(4):
                sp.dma_start(X[:, n * PIECE:(n + 1) * PIECE, :], x_dram[:, n * PIECE:(n + 1) * PIECE, :]).then_inc(x_in[n], 16)
                if n == 0:
                    sp.dma_start(BT[:, :], io["BT"][:, :]).then_inc(loaded, 16)
                    sp.dma_start(WT[:, :], io["WT"][:, :]).then_inc(loaded, 16)
                    sp.dma_start(Acol[:, :], column(io["A"])).then_inc(loaded, 16)
                    for t in range(NT):
                        sp.dma_start(bias[:, t * D:(t + 1) * D], io["b"].rearrange("(a f) -> a f", a=1)).then_inc(loaded, 16)
            loads = list(weight_loads(w, io))
            for dst, src in loads:
                sp.dma_start(dst, src).then_inc(weights_in, 16)
            sp.wait_ge(weights_in, 16 * len(loads))

        @block.vector
        def _(dve):
            nc.vector.memset(ones[:, :], 1.0)
            nc.vector.memset(minus_half[:, :], -0.5).then_inc(filled, 1)
            dve.wait_ge(loaded, LOADS)
            nc.vector.tensor_copy(Arow[:, :], Acol[:, :].to_broadcast([P, T]))

            def x_stats(i, p):
                b = 2 * i + p
                if isinstance(b, int):
                    dve.wait_ge(x_in[b * NT // PIECE], 16)
                    if b == PEELED - 1:
                        for n in range(4):
                            dve.wait_ge(x_in[n], 16)
                layer_stats(nc, dve, tiles(X, b), stats, moments[:, p, 0, :, :])
                nc.vector.tensor_scalar(ve[:, p, 0, :], moments[:, p, 0, :, 1], LN_EPS, None, ALU.add).then_inc(var1, 1)
                dve.drain()

            def normalise(i, p):
                b = 2 * i + p
                dve.wait_ge(rstd1, b + 1)
                dve.wait_ge(turned, counted(b - 1))
                for t in range(NT):
                    last = nc.vector.tensor_scalar(xl[:, p, t, :], X[:, b * NT + t, :], moments[:, p, 0, t, 0:1],
                                                   rstd[:, p, 0, t:t + 1], ALU.subtract, ALU.mult)
                last.then_inc(xl_ready, 1)
                dve.drain()

            def scan(i, p):
                b = 2 * i + p
                dve.wait_ge(u_ready, b + 1)
                dve.wait_ge(y_ready, counted(b - 1))
                nc.vector.tensor_tensor_scan(h[:, p, :], Arow[:, :], u_bank[p][:, :], 0.0, ALU.mult, ALU.add).then_inc(h_ready, 1)

            def y_stats(i, p):
                b = 2 * i + p
                dve.wait_ge(y_ready, b + 1)
                layer_stats(nc, dve, y_bank[p][:, :].rearrange("p (t f) -> p t f", t=NT), stats2, moments[:, p, 1, :, :])
                nc.vector.tensor_scalar(ve[:, p, 1, :], moments[:, p, 1, :, 1], LN_EPS, None, ALU.add).then_inc(var2, 1)
                dve.drain()

            pipeline(dve, STAGES, (0, x_stats), (1, normalise), (3, y_stats), (2, scan))

        @block.gpsimd
        def _(pool):
            nc.gpsimd.memset(w["K"][:, :, :, :, :].bitcast(F32), 0.0)
            pool.wait_ge(filled, 1)

            def invert_x(i, p):
                pool.wait_ge(var1, 2 * i + p + 1)
                nc.gpsimd.tensor_tensor(rstd[:, p, 0, :], ve[:, p, 0, :], minus_half[:, 0:NT], ALU.pow).then_inc(rstd1, 1)

            def invert_y(i, p):
                pool.wait_ge(var2, 2 * i + p + 1)
                nc.gpsimd.tensor_tensor(rstd[:, p, 1, :], ve[:, p, 1, :], minus_half[:, 0:NT], ALU.pow)
                nc.gpsimd.tensor_scalar(minus_mean[:, p, :], moments[:, p, 1, :, 0], -1.0, None, ALU.mult).then_inc(rstd2, 1)

            def add(i, p):
                b = 2 * i + p
                pool.wait_ge(z_ready, b + 1)
                nc.gpsimd.tensor_tensor(tiles(X, b), tiles(X, b), z[:, p, :, :], ALU.add).then_inc(added, 1)

            pipeline(pool, STAGES, (4, add), (0, invert_x), (3, invert_y))

        @block.scalar
        def _(act):
            def copy_xT(i, p):
                b = 2 * i + p
                act.wait_ge(turned, b + 1)
                act.wait_ge(u_ready, counted(b - 1))
                nc.scalar.activation(xT[:, p, :], xT_bank[p][:, :], ACT.Copy).then_inc(xT_ready, 1)

            def normalise_y(i, p):
                b = 2 * i + p
                act.wait_ge(rstd2, b + 1)
                act.wait_ge(added, counted(b - 1))
                for t in range(NT):
                    nc.scalar.activation(z[:, p, t, :], y_bank[p][:, t * P:(t + 1) * P], ACT.Identity, bias=minus_mean[:, p, t:t + 1])
                act.drain()
                for t in range(NT):
                    last = nc.scalar.activation(z[:, p, t, :], z[:, p, t, :], ACT.Copy, scale=rstd[:, p, 1, t:t + 1])
                last.then_inc(z_ready, 1)

            pipeline(act, STAGES, (4, normalise_y), (1, copy_xT))

        @block.tensor
        def _(pe):
            pe.wait_ge(loaded, LOADS)
            pe.wait_ge(filled, 1)

            def turn(i, p):
                b = 2 * i + p
                pe.wait_ge(xl_ready, b + 1)
                pe.wait_ge(xT_ready, counted(b - 1))
                for t in range(NT):
                    last = nc.tensor.transpose(xT_bank[p][:, t * P:(t + 1) * P], xl[:, p, t, :], ident)
                last.then_inc(turned, 1)

            def project(i, p):
                b = 2 * i + p
                pe.wait_ge(xT_ready, b + 1)
                pe.wait_ge(h_ready, counted(b - 1))
                nc.tensor.matmul(u_bank[p][:, :], BT[:, :], xT[:, p, :], start=True, stop=True).then_inc(u_ready, 1)

            def output(i, p):
                b = 2 * i + p
                pe.wait_ge(h_ready, b + 1)
                pe.wait_ge(z_ready, counted(b - 1))
                nc.tensor.matmul(y_bank[p][:, :], ones[:, :], bias[:, :], start=True, stop=False)
                for t in range(NT):
                    last = nc.tensor.matmul(y_bank[p][:, t * P:(t + 1) * P], h[:, p, t * P:(t + 1) * P], WT[:, :],
                                            start=False, stop=(t == NT - 1))
                last.then_inc(y_ready, 1)

            pipeline(pe, STAGES, (3, output), (2, project), (1, turn))


ROWS = SLOTS * HD * 2
SHIFTED = ROWS + 6


def qkv_layer(nc, io, X, XL, const, ident, minus_half, bank, sb, sem, scratch, w):
    STAGES = 7
    Wq, Wk, Wv, cols = w["Wq"], w["Wk"], w["Wv"], w["qkv_cols"]
    stats, moments = sb("q_stats", [P, NT, 6]), sb("q_moments", [P, 2, NT, 2])
    ve, rstd = sb("q_ve", [P, 2, 2, NT]), sb("q_rstd", [P, 2, 2, NT])
    h, hT = sb("q_h", [P, 2, NT, D]), sb("q_hT", [P, 2, T])
    sq, rroot, qn, rest = sb("q_sq", [P, 2, 2, T]), sb("q_rroot", [P, 2, 2, T]), sb("q_qn", [P, 2, 2, T]), sb("q_rest", [P, 2, 2, T])
    parts = sb("q_parts", [P, 2, 3, 2, T], BF16)
    v1 = sb("q_v1", [P, 2, NT, HEADS, HD + 1])
    filled = sem("q_filled")
    var1, rstd1, h_ready, turned, hT_ready = sem("q_var"), sem("q_rstd"), sem("q_h_ready"), sem("q_turned"), sem("q_hT_ready")
    qk_ready, v_ready, sq_ready, mean_ready = sem("q_qk_ready"), sem("q_v_ready"), sem("q_sq_ready"), sem("q_mean_ready")
    rroot_ready, qn_ready, v1_ready = sem("q_rroot_ready"), sem("q_qn_ready"), sem("q_v1_ready")
    high_ready, rest_ready, mid_ready, low_ready = sem("q_high_ready"), sem("q_rest_ready"), sem("q_mid_ready"), sem("q_low_ready")
    stored, v_stored = [sem("q_stored0"), sem("q_stored1")], [sem("q_v_stored0"), sem("q_v_stored1")]
    q_bank, k_bank, mean_bank, hT_bank, v_bank = bank[0:2], bank[2:4], bank[4:6], bank[6], bank[7]
    headmean = const_part(const, "headmean")
    stack, values = scratch

    with nc.Block() as block:
        @block.sync
        def _(sp):
            def store_v(i, p):
                b = 2 * i + p
                sp.wait_ge(v1_ready, b + 1)
                sp.dma_start(values[bass.ds(b, 1), :, :].rearrange("a p n -> (a p) n"),
                             v1[:, p, :, :, :].rearrange("p t h d -> p (t h d)")).then_inc(v_stored[p], 16)

            def store(i, p):
                b = 2 * i + p
                sp.wait_ge(low_ready, b + 1)
                sp.dma_start(stack[bass.ds(b, 1), :, :, :, :].rearrange("a c k r n -> (a r) c k n"),
                             parts[:, p, :, :, :]).then_inc(stored[p], 16)

            pipeline(sp, STAGES, (6, store), (4, store_v))
            for s in stored + v_stored:
                sp.wait_ge(s, B // 2 * 16)

        @block.vector
        def _(dve):
            nc.vector.memset(cols[:, 3:4], RMS_EPS)
            nc.vector.memset(v1[:, :, :, :, HD:HD + 1].rearrange("p a t h d -> p (a t h) d"), 1.0).then_inc(filled, 1)

            def x_stats(i, p):
                layer_stats(nc, dve, tiles(X, 2 * i + p), stats, moments[:, p, :, :])
                nc.vector.tensor_scalar(ve[:, p, 0, :], moments[:, p, :, 1], LN_EPS, None, ALU.add)
                nc.vector.tensor_scalar(ve[:, p, 1, :], moments[:, p, :, 1], 1.0 + RMS_EPS, LN_EPS * RMS_EPS, ALU.mult,
                                        ALU.add).then_inc(var1, 1)
                dve.drain()

            def normalise(i, p):
                b = 2 * i + p
                dve.wait_ge(rstd1, b + 1)
                dve.wait_ge(turned, counted(b - 1))
                for t in range(NT):
                    nc.vector.tensor_scalar(XL[:, b * NT + t, :], X[:, b * NT + t, :], moments[:, p, t, 0:1], rstd[:, p, 0, t:t + 1],
                                            ALU.subtract, ALU.mult)
                    last = nc.vector.tensor_scalar(h[:, p, t, :], X[:, b * NT + t, :], moments[:, p, t, 0:1], rstd[:, p, 1, t:t + 1],
                                                   ALU.subtract, ALU.mult)
                last.then_inc(h_ready, 1)
                dve.drain()

            def take_v(i, p):
                dve.wait_ge(v_ready, 2 * i + p + 1)
                dve.wait_ge(v_stored[p], 16 * i)
                nc.vector.tensor_copy(v1[:, p, :, :, 0:HD],
                                      v_bank[:, :].rearrange("p (t h d) -> p t h d", t=NT, h=HEADS)).then_inc(v1_ready, 1)

            def norm(i, p):
                b = 2 * i + p
                dve.wait_ge(rroot_ready, b + 1)
                nc.vector.scalar_tensor_tensor(qn[:, p, 0, :], q_bank[p][:, :], cols[:, 1:2], rroot[:, p, 0, :], ALU.mult, ALU.mult)
                nc.vector.scalar_tensor_tensor(qn[:, p, 1, :], k_bank[p][:, :], cols[:, 2:3], rroot[:, p, 1, :], ALU.mult,
                                               ALU.mult).then_inc(qn_ready, 1)

            def leave(i, p):
                b = 2 * i + p
                dve.wait_ge(high_ready, b + 1)
                dve.wait_ge(low_ready, counted(b - 1))
                nc.vector.tensor_tensor(rest[:, p, :, :], qn[:, p, :, :], parts[:, p, 0, :, :], ALU.subtract).then_inc(rest_ready, 1)

            pipeline(dve, STAGES, (2, normalise), (5, leave), (4, norm), (3, take_v), (0, x_stats))

        @block.gpsimd
        def _(pool):
            def invert(i, p):
                pool.wait_ge(var1, 2 * i + p + 1)
                nc.gpsimd.tensor_tensor(rstd[:, p, :, :], ve[:, p, :, :], minus_half[:, 0:2 * NT].rearrange("p (a t) -> p a t", a=2),
                                        ALU.pow).then_inc(rstd1, 1)

            def low(i, p):
                b = 2 * i + p
                pool.wait_ge(mid_ready, b + 1)
                nc.gpsimd.tensor_tensor(parts[:, p, 2, :, :], rest[:, p, :, :], parts[:, p, 1, :, :], ALU.subtract).then_inc(low_ready, 1)

            pipeline(pool, STAGES, (6, low), (0, invert))

        @block.scalar
        def _(act):
            act.wait_ge(filled, 1)

            def copy_hT(i, p):
                b = 2 * i + p
                act.wait_ge(turned, b + 1)
                act.wait_ge(v_ready, counted(b - 1))
                nc.scalar.activation(hT[:, p, :], hT_bank[:, :], ACT.Copy, scale=cols[:, 0:1]).then_inc(hT_ready, 1)

            def squares(i, p):
                b = 2 * i + p
                act.wait_ge(qk_ready, b + 1)
                act.wait_ge(mean_ready, counted(b - 1))
                nc.scalar.activation(sq[:, p, 0, :], q_bank[p][:, :], ACT.Square)
                nc.scalar.activation(sq[:, p, 1, :], k_bank[p][:, :], ACT.Square).then_inc(sq_ready, 1)

            def roots(i, p):
                b = 2 * i + p
                act.wait_ge(mean_ready, b + 1)
                act.wait_ge(qn_ready, counted(b - 1))
                nc.scalar.activation(rroot[:, p, 0, :], mean_bank[0][:, :], ACT.Ln, bias=cols[:, 3:4])
                nc.scalar.activation(rroot[:, p, 1, :], mean_bank[1][:, :], ACT.Ln, bias=cols[:, 3:4])
                act.drain()
                nc.scalar.activation(rroot[:, p, :, :], rroot[:, p, :, :], ACT.Exp, scale=-0.5).then_inc(rroot_ready, 1)

            def high(i, p):
                act.wait_ge(qn_ready, 2 * i + p + 1)
                act.wait_ge(stored[p], 16 * i)
                nc.scalar.activation(parts[:, p, 0, :, :], qn[:, p, :, :], ACT.Copy).then_inc(high_ready, 1)

            def mid(i, p):
                act.wait_ge(rest_ready, 2 * i + p + 1)
                nc.scalar.activation(parts[:, p, 1, :, :], rest[:, p, :, :], ACT.Copy).then_inc(mid_ready, 1)

            pipeline(act, STAGES, (6, mid), (4, roots), (5, high), (3, squares), (2, copy_hT))

        @block.tensor
        def _(pe):

            def turn(i, p):
                b = 2 * i + p
                pe.wait_ge(h_ready, b + 1)
                pe.wait_ge(hT_ready, b)
                for t in range(NT):
                    last = nc.tensor.transpose(hT_bank[:, t * P:(t + 1) * P], h[:, p, t, :], ident)
                last.then_inc(turned, 1)

            def project(i, p):
                b = 2 * i + p
                pe.wait_ge(hT_ready, b + 1)
                pe.wait_ge(qn_ready, counted(b - 1))
                nc.tensor.matmul(q_bank[p][:, :], Wq[:, :], hT[:, p, :], start=True, stop=True)
                nc.tensor.matmul(k_bank[p][:, :], Wk[:, :], hT[:, p, :], start=True, stop=True).then_inc(qk_ready, 1)
                pe.wait_ge(v1_ready, b)
                for t in range(NT):
                    last = nc.tensor.matmul(v_bank[:, t * P:(t + 1) * P], hT[:, p, t * P:(t + 1) * P], Wv[:, :], start=True, stop=True)
                last.then_inc(v_ready, 1)

            def means(i, p):
                b = 2 * i + p
                pe.wait_ge(sq_ready, b + 1)
                pe.wait_ge(rroot_ready, b)
                for n in range(2):
                    last = nc.tensor.matmul(mean_bank[n][:, :], headmean, sq[:, p, n, :], start=True, stop=True)
                last.then_inc(mean_ready, 1)

            pipeline(pe, STAGES, (4, means), (3, project), (2, turn))


SCORE_UNITS = [(0, (h,)) for h in range(4)] + [(1, (h,)) for h in range(4)] + [(2, (0, 1)), (2, (2, 3)), (3, (0, 1, 2, 3))]
MAX_UNITS = [(0, (0, 1, 2, 3)), (1, (0, 1)), (1, (2, 3))] + [(2, (h,)) for h in range(4)] + [(3, (h,)) for h in range(4)]
UNITS = len(SCORE_UNITS)
GROUPS = HEADS // GROUP
SCORES = UNITS * GROUPS
LAST_OF_TILE = {max(k for k, u in enumerate(SCORE_UNITS) if u[0] == kt): kt for kt in range(NT)}


def order_of_work():
    for g in range(GROUPS):
        before, back = (g - 1) % GROUPS, int(g == 0)
        for k in range(UNITS):
            yield "score", g, k, 0
            yield "max", g, k, 0
            if k == 1:
                yield "values", before, 2, back
            if k == 4:
                yield "values", before, 3, back
            if k == 8:
                yield "turn", before, 0, back
            if k == 7:
                yield "values", g, 0, 0
            if k == 10:
                yield "values", g, 1, 0
            if g == 0 and k == 10:
                yield "turn_all", 0, 0, 1
            if g == 1 and k == 1:
                yield "project", 0, 0, 1
            if g == 1 and k == 3:
                yield "shift", 1, 0, 1
            if g == 2 and k == 6:
                yield "shift", 0, 0, 0


def attention_layer(nc, io, X, XL, const, ident, minus_half, bank, sb, sem, scratch, w):
    stack, values = scratch
    Q, K = sb("a_Q", [P, 2, PAIRS, T], BF16), w["K"]
    V = sb("a_V", [P, 2, NT, HEADS, HD + 1])
    Wo = w["Wo"]
    identb, maskb = sb("a_identb", [P, P], BF16), sb("a_maskb", [P, P], BF16)
    E = [sb(f"a_E{kt}", [P, GROUP, T - P * kt]) for kt in range(NT)]
    neg = sb("a_neg", [P, NT, 2, PAIRS])
    nb, nr = sb("a_nb", [P, 2, NT, 2, 4], BF16), sb("a_nr", [P, NT, 2, 4])
    nparts = sb("a_nparts", [P, NT, 2, 3, 4])
    shiftT = sb("a_shiftT", [24, T], BF16)
    outT, inv = sb("a_outT", [P, T]), sb("a_inv", [P, NT * GROUP])
    ao, aoT = sb("a_ao", [P, NT, D]), sb("a_aoT", [P, T])
    prepared, ones_ready = sem("a_prepared"), sem("a_ones_ready")
    stacked = [[sem(f"a_stacked{p}{hf}") for hf in range(2)] for p in range(2)]
    v_in = [sem("a_v_in0"), sem("a_v_in1")]
    score_ready, exp_done, kept = sem("a_score_ready"), sem("a_exp_done"), sem("a_kept")
    max_ready, nparts_ready, shift_turned = sem("a_max_ready"), sem("a_nparts"), sem("a_shift_turned")
    max_taken = [sem("a_max_taken0"), sem("a_max_taken1")]
    shift_copied, shift_in = sem("a_shift_copied"), [sem("a_shift_in0"), sem("a_shift_in1")]
    pv_done, outT_ready, turned, ao_ready = sem("a_pv_done"), sem("a_outT_ready"), sem("a_turned"), sem("a_ao_ready")
    ao_turned, aoT_ready, wo_ready, wo_taken = sem("a_ao_turned"), sem("a_aoT_ready"), sem("a_wo_ready"), sem("a_wo_taken")
    pool_tick = sem("a_pool_tick")
    score_bank, max_bank, pv_bank, turn_bank = bank[0:3], bank[3:6], bank[6], bank[7]
    SCALE = float(HD) ** -0.5
    n_pv = GROUPS * NT

    def last_use(n, banks):
        return n - len(banks) if n >= len(banks) else (SCORES - 1 - n) // len(banks) * len(banks) + n - SCORES

    def stack_count(b, p):
        return ((b + p) // 2 + 1) * 192 if isinstance(b, int) else (b - p) * 96 + 192 * (p + 1)

    def v_count(b, p):
        return (b // 2 + 1) * 16 if isinstance(b, int) else (b - p) * 8 + 16

    def run(eng, step):
        def around(b, p):
            for kind, g, k, back in order_of_work():
                if isinstance(b, int) and (b == B - 1 or b == B) and kind in ("max", "shift") and b + 1 - back >= B:
                    continue
                if isinstance(b, int) and (b == 0 and back and kind != "shift" or b == B and not back):
                    continue
                step(kind, g, k, b - back, (p + back) % 2)

        for g in range(GROUPS):
            for k in range(UNITS):
                step("max", g, k, -1, 1)
            if g == 1:
                step("shift", 0, 0, -1, 1)
        around(0, 0)
        around(1, 1)
        with eng.Fori(1, B // 2 - 1) as i:
            for p in range(2):
                around(Linear(i, 2, p), p)
        for b in range(B - 2, B + 1):
            around(b, b % 2)

    def shift_rows(ops, eng, p):
        eng.drain()
        ops.memset(K[ROWS:ROWS + 3, p, 0, :, :], 1.0)
        ops.memset(K[ROWS:SHIFTED, p, 1, :, :], 1.0)
        eng.drain()
        return ops.memset(K[ROWS:ROWS + 3, p, 1, :, :], 0.0)

    with nc.Block() as block:
        @block.sync
        def _(sp):
            def load(b, p, hf):
                pairs = slice(4 * hf, 4 * hf + 4)
                if not (isinstance(b, int) and b < 2):
                    sp.wait_ge(score_ready, (b - 2) * SCORES + (hf + 1) * SCORES // 2)
                for par in range(2):
                    src = stack[bass.ds(b, 1), :, :, par * 64:par * 64 + 64, :].rearrange("a c k (d r) n -> (a c) k d r n", r=PAIRS)
                    slot = 0
                    for c in range(3):
                        rows = slice((par * SLOTS + slot) * HD, (par * SLOTS + slot + 3 - c) * HD)
                        sp.dma_start(Q[rows, p, pairs, :],
                                     src[c:c + 1, 0, :, pairs, :].to_broadcast([3 - c, HD, 4, T])).then_inc(stacked[p][hf], 16)
                        sp.dma_start(K[rows, p, par, pairs, :],
                                     src[0:3 - c, 1, :, pairs, :]).then_inc(stacked[p][hf], 16)
                        slot += 3 - c

            def load_v(b, p):
                if not (isinstance(b, int) and b < 2):
                    sp.wait_ge(pv_done, (b - 1) * n_pv)
                sp.dma_start(V[:, p, :, :, :].rearrange("p t h d -> p (t h d)"),
                             values[bass.ds(b, 1), :, :].rearrange("a p n -> (a p) n")).then_inc(v_in[p], 16)

            def shift(m, p, hf):
                sp.wait_ge(shift_copied, 2 * m + hf + 1)
                sp.dma_start(Q[ROWS:SHIFTED, p, 4 * hf:4 * hf + 4, :], shiftT[:, :]).then_inc(shift_in[hf], 16)

            load(0, 0, 0)
            load(0, 0, 1)
            load_v(0, 0)
            load(1, 1, 0)
            shift(0, 0, 0)
            load(1, 1, 1)
            load_v(1, 1)
            shift(0, 0, 1)
            with sp.Fori(0, B // 2 - 1) as i:
                for p in range(2):
                    load(2 * i + p + 2, p, 0)
                    shift(2 * i + p + 1, 1 - p, 0)
                    load(2 * i + p + 2, p, 1)
                    shift(2 * i + p + 1, 1 - p, 1)
                    load_v(2 * i + p + 2, p)
            shift(B - 1, 1, 0)
            shift(B - 1, 1, 1)

        @block.tensor
        def _(pe):
            pe.wait_ge(prepared, 1)

            def step(kind, g, k, b, p):
                m, mp = b + 1, 1 - p
                im = (m - mp) // 2 if isinstance(m, int) else None
                if kind == "score":
                    n = g * UNITS + k
                    kt, heads = SCORE_UNITS[k]
                    if k == 0 and g % 2 == 0:
                        pe.wait_ge(shift_in[g // 2], counted(16 * (b + 1)))
                    pe.wait_ge(exp_done, counted(b * SCORES + last_use(n, score_bank) + 1))
                    wide = T - P * kt
                    for x, j in enumerate(heads):
                        h = GROUP * g + j
                        last = nc.tensor.matmul(score_bank[n % len(score_bank)][:, x * wide:(x + 1) * wide], K[0:SHIFTED, p, h % 2, h // 2, kt * P:(kt + 1) * P],
                                                Q[0:SHIFTED, p, h // 2, kt * P:T], start=True, stop=True)
                    last.then_inc(score_ready, 1)
                if kind == "max":
                    n = g * UNITS + k
                    qt, heads = MAX_UNITS[k]
                    if k == 0 and g % 2 == 0:
                        pe.wait_ge(stacked[mp][g // 2], counted(stack_count(b, p)))
                    if n < len(max_bank):
                        pe.wait_ge(max_taken[1 - mp], counted((m + mp) * (SCORES // 2) + last_use(n, max_bank) + 1))
                    else:
                        pe.wait_ge(max_taken[mp], counted((m - mp) * (SCORES // 2) + last_use(n, max_bank) + 1))
                    wide = P * (qt + 1)
                    for x, j in enumerate(heads):
                        h = GROUP * g + j
                        at = x * wide
                        nc.tensor.matmul(max_bank[n % len(max_bank)][:, at:at + wide], Q[0:ROWS, mp, h // 2, qt * P:(qt + 1) * P],
                                         K[0:ROWS, mp, h % 2, h // 2, 0:wide], start=True, stop=False)
                        last = nc.tensor.matmul(max_bank[n % len(max_bank)][:, at + wide - P:at + wide], identb[:, :], maskb[:, :],
                                                start=False, stop=True)
                    last.then_inc(max_ready, 1)
                if kind == "values":
                    kt = k
                    pe.wait_ge(kept, counted(b * n_pv + g * NT + kt + 1))
                    if kt == 0:
                        pe.wait_ge(outT_ready, counted(b * GROUPS + g))
                        if g == 0:
                            pe.wait_ge(v_in[p], counted(v_count(b, p)))
                    for j in range(GROUP):
                        last = nc.tensor.matmul(pv_bank[32 * j:32 * j + HD + 1, kt * P:T], V[:, p, kt, GROUP * g + j, :], E[kt][:, j, :],
                                                start=(kt == 0), stop=(kt == NT - 1))
                    last.then_inc(pv_done, 1)
                if kind == "turn":
                    pe.wait_ge(outT_ready, counted(b * GROUPS + g + 1))
                    if g == 0:
                        pe.wait_ge(shift_copied, counted(2 * b + 2))
                    if g == 1:
                        pe.wait_ge(shift_copied, counted(2 * b + (2 if isinstance(b, int) and b == B - 1 else 3)))
                    if g:
                        pe.wait_ge(ao_ready, counted(b * GROUPS + g))
                    for t in range(NT):
                        last = nc.tensor.transpose(turn_bank[:, t * P:(t + 1) * P], outT[:, t * P:(t + 1) * P], ident)
                    last.then_inc(turned, 1)
                if kind == "turn_all":
                    pe.wait_ge(ao_ready, counted((b + 1) * GROUPS))
                    for t in range(NT):
                        last = nc.tensor.transpose(turn_bank[:, t * P:(t + 1) * P], ao[:, t, :], ident)
                    last.then_inc(ao_turned, 1)
                if kind == "project":
                    pe.wait_ge(aoT_ready, counted(b + 1))
                    for t in range(NT):
                        last = nc.tensor.matmul(turn_bank[:, t * WIDE:(t + 1) * WIDE], aoT[:, t * P:(t + 1) * P], Wo[:, :],
                                                start=True, stop=True)
                    last.then_inc(wo_ready, 1)
                if kind == "shift":
                    pe.wait_ge(nparts_ready, counted(2 * m + g + 1))
                    if g == 0:
                        pe.wait_ge(ao_ready, counted(b * GROUPS + 1))
                    elif isinstance(b, int) and b < 0:
                        pe.wait_ge(shift_copied, 1)
                    else:
                        pe.wait_ge(wo_taken, counted(b + 1))
                    for t in range(NT):
                        last = nc.tensor.transpose(turn_bank[0:24, t * P:(t + 1) * P], nparts[:, t, :, :, :].rearrange("p a r c -> p (a r c)"), ident)
                    last.then_inc(shift_turned, 1)
                    if isinstance(b, int) and b < 0 and g == 1:
                        pe.wait_ge(ones_ready, 2)

            run(pe, step)

        @block.scalar
        def _(act):
            def step(kind, g, k, b, p):
                m, mp = b + 1, 1 - p
                if kind == "score":
                    n = g * UNITS + k
                    kt, heads = SCORE_UNITS[k]
                    act.wait_ge(score_ready, counted(b * SCORES + n + 1))
                    act.wait_ge(pv_done, counted(b * n_pv + (g - 1) * NT + kt + 1))
                    wide = T - P * kt
                    nc.scalar.activation(E[kt][:, heads[0]:heads[-1] + 1, :],
                                         score_bank[n % len(score_bank)][:, 0:len(heads) * wide].rearrange("p (h q) -> p h q", q=wide),
                                         ACT.Exp, scale=SCALE).then_inc(exp_done, 1)
                if kind == "values" and k == NT - 1:
                    act.wait_ge(pv_done, counted(b * n_pv + g * NT + NT))
                    act.wait_ge(turned, counted(b * GROUPS + g))
                    nc.scalar.activation(outT[:, :], pv_bank[:, :], ACT.Copy).then_inc(outT_ready, 1)
                if kind == "turn_all":
                    act.wait_ge(ao_turned, counted(b + 1))
                    nc.scalar.activation(aoT[:, :], turn_bank[:, :], ACT.Copy).then_inc(aoT_ready, 1)
                if kind == "shift":
                    act.wait_ge(shift_turned, counted(2 * m + g + 1))
                    act.wait_ge(shift_in[1 - g], counted(16 * m if g == 0 else 16 * (m + 1)))
                    nc.scalar.activation(shiftT[:, :], turn_bank[0:24, :], ACT.Copy).then_inc(shift_copied, 1)

            run(act, step)

        @block.vector
        def _(dve):
            nc.vector.memset(pv_bank[:, :], 0.0)
            nc.vector.tensor_copy(identb[:, :], ident)
            nc.vector.tensor_copy(maskb[:, :], const_part(const, "mask")).then_inc(prepared, 1)
            shift_rows(nc.vector, dve, 0).then_inc(ones_ready, 1)
            dve.drain()
            prepare_weights(nc, dve, w)

            def step(kind, g, k, b, p):
                m = b + 1
                if kind == "max":
                    n = g * UNITS + k
                    qt, heads = MAX_UNITS[k]
                    dve.wait_ge(max_ready, counted(m * SCORES + n + 1))
                    if k == 0:
                        dve.wait_ge(nparts_ready, counted(2 * m))
                    wide, h0, nh = P * (qt + 1), GROUP * g + heads[0], len(heads)
                    src = max_bank[n % len(max_bank)][:, 0:nh * wide].rearrange("p (h q) -> p h q", q=wide)
                    if nh == 1:
                        dst = neg[:, qt, h0 % 2, h0 // 2:h0 // 2 + 1]
                    elif nh == 2:
                        dst = neg[:, qt, 0:2, h0 // 2]
                    else:
                        dst = neg[:, qt, :, h0 // 2:h0 // 2 + 2].rearrange("p r a -> p a r")
                        src = src.rearrange("p (a r) q -> p a r q", r=2)
                    nc.vector.tensor_reduce(out=dst, in_=src, axis=AX.X, op=ALU.max, negate=True).then_inc(max_taken[(p + 1) % 2], 1)
                if kind == "turn":
                    dve.wait_ge(turned, counted(b * GROUPS + g + 1))
                    o = turn_bank[:, :].rearrange("p (n c) -> p n c", c=32)
                    nc.vector.reciprocal(inv[:, :], o[:, :, HD])
                    dve.drain()
                    nc.vector.tensor_tensor(ao[:, :, 32 * g:32 * g + 32].rearrange("p t (j d) -> p t j d", d=HD),
                                            o[:, :, 0:HD].rearrange("p (t j) d -> p t j d", t=NT),
                                            inv[:, :].rearrange("p (t j) -> p t j", t=NT).unsqueeze(3).to_broadcast([P, NT, GROUP, HD]),
                                            ALU.mult).then_inc(ao_ready, 1)
                    dve.drain()
                if kind == "project":
                    dve.wait_ge(wo_ready, counted(b + 1))
                    dst = XL[:, bass.ds(counted(b * NT), NT), MASKED:D]
                    nc.vector.tensor_tensor(dst, turn_bank[:, 0:NT * WIDE].rearrange("p (t f) -> p t f", t=NT), dst, ALU.add).then_inc(wo_taken, 1)

            run(dve, step)

        @block.gpsimd
        def _(pool):
            shift_rows(nc.gpsimd, pool, 1).then_inc(ones_ready, 1)
            pool.drain()

            def step(kind, g, k, b, p):
                m = b + 1
                if kind == "score" and k in LAST_OF_TILE:
                    kt = LAST_OF_TILE[k]
                    pool.wait_ge(exp_done, counted(b * SCORES + g * UNITS + k + 1))
                    pool.sem_inc(pool_tick, 1)
                    nc.gpsimd.affine_select(out=E[kt][:, :, 0:P], in_=E[kt][:, :, 0:P], compare_op=ALU.is_ge, fill=0.0, base=0,
                                            pattern=[[0, GROUP], [1, P]], channel_multiplier=-1).then_inc(kept, 1)
                if kind == "max" and g % 2 == 1 and k == UNITS - 1:
                    hf = g // 2
                    pool.wait_ge(max_taken[1 - p], counted((m - (1 - p)) * (SCORES // 2) + (g + 1) * UNITS))
                    pool.wait_ge(shift_turned, counted(2 * m + hf))
                    pool.sem_inc(pool_tick, 1)
                    src = neg[:, :, :, 4 * hf:4 * hf + 4]
                    nc.gpsimd.tensor_copy(nb[:, 0, :, :, :], src)
                    pool.drain()
                    nc.gpsimd.tensor_copy(nparts[:, :, :, 0, :], nb[:, 0, :, :, :])
                    nc.gpsimd.tensor_tensor(nr[:, :, :, :], src, nb[:, 0, :, :, :], ALU.subtract)
                    pool.drain()
                    nc.gpsimd.tensor_copy(nb[:, 1, :, :, :], nr[:, :, :, :])
                    pool.drain()
                    nc.gpsimd.tensor_copy(nparts[:, :, :, 1, :], nb[:, 1, :, :, :])
                    nc.gpsimd.tensor_tensor(nparts[:, :, :, 2, :], nr[:, :, :, :], nb[:, 1, :, :, :], ALU.subtract).then_inc(nparts_ready, 1)
                    pool.drain()

            run(pool, step)


EXPERTS = 4
HC2 = 2
MOE_ORDER = [("up", "e1a", "x", 1, 2), ("up", "e1b", "x", 1, 2), ("up", "e0u", "x", 1, 2), ("up", "e2a", "x", 1, 2),
             ("out", 1), ("up", "e3a", "x", 1, 1), ("up", "e2b", "G1", 2, 2), ("out", 0), ("up", "e3b", "G3", 1, 2),
             ("up", "e2c", "G2", 2, 2), ("out", 3), ("out", 2)]
MOE_FIRST, MOE_SECOND = MOE_ORDER[:2], MOE_ORDER[2:]
MOE_UPS = [s for s in MOE_ORDER if s[0] == "up"]
MOE_OUTS = [s[1] for s in MOE_ORDER if s[0] == "out"]
MOE_TO = {"e0u": "H0", "e1a": "S1", "e1b": "H1", "e2a": "G1", "e3a": "G3", "e2b": "G2", "e3b": "H3", "e2c": "G4"}
MOE_LAST = {0: "H0", 1: "H1", 2: "G4", 3: "H3"}


def expert_layer(nc, io, X, XL, const, ident, minus_half, bank, sb, sem, scratch, w):
    STAGES = 6
    down, gate, n2w = w["down"], w["gate"], w["n2w"]
    stats, moments = sb("e_stats", [P, NT, 6]), sb("e_moments", [P, NT, 2])
    stats2, moments2 = sb("e_stats2", [P, NT, 6]), sb("e_moments2", [P, 2, NT, 2])
    ve, rstd = sb("e_ve", [P, 2, 2, NT]), sb("e_rstd", [P, 2, 2, NT])
    xf, z = sb("e_xf", [P, 2, NT, D]), sb("e_z", [P, 2, NT, D])
    xfT = sb("e_xfT", [P, 2, T])
    xf_parts = [sb(f"e_xf_part{n}", [P, 2, T], F32R) for n in range(2)]
    g2_parts = [sb(f"e_g2_part{n}", [P, HC2, T], F32R) for n in range(2)]
    w_parts, x_split, g2_split = w["parts"], sem("e_x_split"), sem("e_g2_split")
    hid = {name: sb(f"e_{name}", [P, 1 if name == "G3" else HC2, T]) for name in ("H0", "S1", "H1", "G1", "G2", "G3", "G4", "H3")}
    euler = sb("e_euler", [P, NT * EXPERTS])
    lg, part, pr, tv = (sb(f"e_{x}", [P, NT, EXPERTS]) for x in ("lg", "part", "pr", "tv"))
    top, cmp1, cmp2 = sb("e_top", [P, NT]), sb("e_cmp1", [P, NT, EXPERTS, EXPERTS]), sb("e_cmp2", [P, NT, EXPERTS, EXPERTS])
    wts = sb("e_wts", [P, NT, EXPERTS])
    var1, rstd1, var2, rstd2 = sem("e_var1"), sem("e_rstd1"), sem("e_var2"), sem("e_rstd2")
    xf_ready, turned, xfT_ready = sem("e_xf_ready"), sem("e_turned"), sem("e_xfT_ready")
    logits_ready, logits_taken, diff_ready, exp_ready = sem("e_logits_ready"), sem("e_logits_taken"), sem("e_diff_ready"), sem("e_exp_ready")
    up_ready, hidden_ready, h1_ready = sem("e_up_ready"), sem("e_hidden_ready"), sem("e_h1_ready")
    out_ready, out_taken, z_ready, added = sem("e_out_ready"), sem("e_out_taken"), sem("e_z_ready"), sem("e_added")
    xT_bank, logit_bank, out_bank = bank[0], bank[1], bank[6:8]
    up_banks = (bank[2:4], bank[4:6])
    n_up, n_act = len(MOE_UPS), len(MOE_UPS) - 1
    up_at = {s[1]: n for n, s in enumerate(MOE_UPS)}
    act_at = {s[1]: n for n, s in enumerate(s for s in MOE_UPS if s[1] != "e1b")}

    def banks_free(eng, n, b):
        if n < 2:
            return
        name = MOE_UPS[n - 2][1]
        if name == "e1b":
            eng.wait_ge(h1_ready, b + 1)
        else:
            eng.wait_ge(hidden_ready, b * n_act + act_at[name] + 1)

    def made(eng, name, b):
        if name == "H1":
            eng.wait_ge(h1_ready, b + 1)
        elif name == "G2":
            eng.wait_ge(g2_split, b + 1)
        elif name != "x":
            src = [k for k, v in MOE_TO.items() if v == name][0]
            eng.wait_ge(hidden_ready, b * n_act + act_at[src] + 1)

    with nc.Block() as block:
        @block.tensor
        def _(pe):
            def turn(i, p):
                b = 2 * i + p
                pe.wait_ge(xf_ready, b + 1)
                pe.wait_ge(xfT_ready, b)
                for t in range(NT):
                    last = nc.tensor.transpose(xT_bank[:, t * P:(t + 1) * P], xf[:, p, t, :], ident)
                last.then_inc(turned, 1)

            def score(i, p):
                b = 2 * i + p
                pe.wait_ge(xfT_ready, b + 1)
                pe.wait_ge(logits_taken, b)
                for t in range(NT):
                    last = nc.tensor.matmul(logit_bank[:, t * EXPERTS:(t + 1) * EXPERTS], xfT[:, p, t * P:(t + 1) * P], gate[:, :],
                                            start=True, stop=True)
                last.then_inc(logits_ready, 1)

            def experts(i, p, steps):
                b = 2 * i + p
                if steps is MOE_FIRST:
                    pe.wait_ge(x_split, b + 1)
                for step in steps:
                    if step[0] == "up":
                        _, name, src, n_in, n_chunks = step
                        n = up_at[name]
                        banks_free(pe, n, b)
                        made(pe, src, b)
                        for c in range(n_chunks):
                            cols = slice(c * P, (c + 1) * P)
                            if src in ("x", "G2"):
                                products = [(k, *parts) for k in range(n_in) for parts in ((0, 0), (0, 1), (1, 0))]
                                for n_product, (k, wp, xp) in enumerate(products):
                                    rhs = xf_parts[xp][:, p, :] if src == "x" else g2_parts[xp][:, k, :]
                                    last = nc.tensor.matmul(up_banks[n % 2][c][:, :], w_parts[name][wp][:, k, cols], rhs,
                                                            start=(n_product == 0), stop=(n_product == len(products) - 1))
                                continue
                            for k in range(n_in):
                                last = nc.tensor.matmul(up_banks[n % 2][c][:, :], w[name][:, k, cols], hid[src][:, k, :],
                                                        start=(k == 0), stop=(k == n_in - 1))
                        last.then_inc(up_ready, 1)
                    else:
                        e = step[1]
                        n_out = MOE_OUTS.index(e)
                        made(pe, MOE_LAST[e], b)
                        pe.wait_ge(out_taken, b * EXPERTS + max(n_out - 1, 0))
                        for t in range(NT):
                            for k in range(HC2):
                                last = nc.tensor.matmul(out_bank[n_out % 2][:, t * WIDE:(t + 1) * WIDE],
                                                        hid[MOE_LAST[e]][:, k, t * P:(t + 1) * P], down[:, e, k, :],
                                                        start=(k == 0), stop=(k == HC2 - 1))
                        last.then_inc(out_ready, 1)

            pipeline(pe, STAGES, (3, lambda i, p: experts(i, p, MOE_FIRST)), (2, score),
                     (3, lambda i, p: experts(i, p, MOE_SECOND)), (1, turn))

        @block.scalar
        def _(act):
            def copy_xfT(i, p):
                b = 2 * i + p
                act.wait_ge(turned, b + 1)
                act.wait_ge(x_split, counted(b - 1))
                nc.scalar.activation(xfT[:, p, :], xT_bank[:, :], ACT.Copy, scale=n2w[:, 0:1]).then_inc(xfT_ready, 1)

            def functions(i, p):
                b = 2 * i + p
                for n, (_, name, _, _, n_chunks) in enumerate(MOE_UPS):
                    if name == "e1b":
                        continue
                    act.wait_ge(up_ready, b * n_up + n + 1)
                    dst = hid[MOE_TO[name]]
                    if n == 0:
                        act.wait_ge(out_ready, b * EXPERTS)
                    if name == "e1a":
                        act.wait_ge(h1_ready, b)
                    for c in range(n_chunks):
                        last = nc.scalar.activation(dst[:, c, :], up_banks[n % 2][c][:, :], ACT.Silu if name == "e1a" else ACT.Gelu)
                    last.then_inc(hidden_ready, 1)

            pipeline(act, STAGES, (3, functions), (1, copy_xfT))

        @block.gpsimd
        def _(pool):
            nc.gpsimd.memset(euler[:, :], math.e)
            pool.drain()

            def invert_x(i, p):
                pool.wait_ge(var1, 2 * i + p + 1)
                nc.gpsimd.tensor_tensor(rstd[:, p, 0, :], ve[:, p, 0, :], minus_half[:, 0:NT], ALU.pow).then_inc(rstd1, 1)

            def exponentials(i, p):
                pool.wait_ge(diff_ready, 2 * i + p + 1)
                nc.gpsimd.tensor_tensor(pr[:, :, :].rearrange("p t e -> p (t e)"), euler[:, :],
                                        part[:, :, :].rearrange("p t e -> p (t e)"), ALU.pow).then_inc(exp_ready, 1)

            def invert_y(i, p):
                pool.wait_ge(var2, 2 * i + p + 1)
                nc.gpsimd.tensor_tensor(rstd[:, p, 1, :], ve[:, p, 1, :], minus_half[:, 0:NT], ALU.pow).then_inc(rstd2, 1)

            def add(i, p):
                b = 2 * i + p
                pool.wait_ge(z_ready, b + 1)
                nc.gpsimd.tensor_tensor(tiles(X, b), tiles(X, b), z[:, p, :, :], ALU.add).then_inc(added, 1)

            pipeline(pool, STAGES, (5, add), (0, invert_x), (2, exponentials), (4, invert_y))

        @block.vector
        def _(dve):
            earlier = const_part(const, "earlier").rearrange("p (i j) -> p i j", i=EXPERTS)

            def split_g2(i, p):
                b = 2 * i + p
                dve.wait_ge(hidden_ready, b * n_act + act_at["e2b"] + 1)
                keep_high(nc.vector, g2_parts[0][:, :, :], hid["G2"][:, :, :])
                dve.drain()
                keep_low(nc.vector, g2_parts[1][:, :, :], hid["G2"][:, :, :], g2_parts[0][:, :, :]).then_inc(g2_split, 1)

            def split_x(i, p):
                b = 2 * i + p
                dve.wait_ge(xfT_ready, b + 1)
                dve.wait_ge(up_ready, counted((b - 1) * n_up))
                keep_high(nc.vector, xf_parts[0][:, p, :], xfT[:, p, :])
                dve.drain()
                keep_low(nc.vector, xf_parts[1][:, p, :], xfT[:, p, :], xf_parts[0][:, p, :]).then_inc(x_split, 1)

            def f_stats(i, p):
                layer_stats(nc, dve, tiles(XL, 2 * i + p), stats, moments)
                nc.vector.tensor_tensor(top[:, :], moments[:, :, 0], moments[:, :, 0], ALU.mult)
                dve.drain()
                nc.vector.scalar_tensor_tensor(ve[:, p, 0, :], moments[:, :, 1], RMS_EPS, top[:, :], ALU.add, ALU.add).then_inc(var1, 1)
                dve.drain()

            def scale(i, p):
                b = 2 * i + p
                dve.wait_ge(rstd1, b + 1)
                dve.wait_ge(turned, counted(b - 1))
                for t in range(NT):
                    last = nc.vector.tensor_scalar(xf[:, p, t, :], XL[:, b * NT + t, :], rstd[:, p, 0, t:t + 1], None, ALU.mult)
                last.then_inc(xf_ready, 1)
                dve.drain()

            def differences(i, p):
                b = 2 * i + p
                dve.wait_ge(logits_ready, b + 1)
                raw = logit_bank[:, 0:NT * EXPERTS].rearrange("p (t e) -> p t e", e=EXPERTS)
                nc.vector.tensor_scalar(lg[:, :, :], raw, 0.0, FMAX, ALU.max, ALU.min)
                nc.vector.tensor_scalar(part[:, :, :], raw, 0.0, -FMAX, ALU.min, ALU.max).then_inc(logits_taken, 1)
                dve.drain()
                nc.vector.tensor_tensor(lg[:, :, :], lg[:, :, :], part[:, :, :], ALU.add)
                dve.drain()
                nc.vector.tensor_reduce(out=top[:, :], in_=lg[:, :, :], axis=AX.X, op=ALU.max)
                dve.drain()
                nc.vector.tensor_tensor(part[:, :, :], lg[:, :, :], top[:, :].unsqueeze(2).to_broadcast([P, NT, EXPERTS]),
                                        ALU.subtract).then_inc(diff_ready, 1)
                dve.drain()

            def weights(i, p):
                dve.wait_ge(exp_ready, 2 * i + p + 1)
                nc.vector.tensor_reduce(out=top[:, :], in_=pr[:, :, :], axis=AX.X, op=ALU.add)
                dve.drain()
                nc.vector.reciprocal(top[:, :], top[:, :])
                dve.drain()
                nc.vector.tensor_tensor(pr[:, :, :], pr[:, :, :], top[:, :].unsqueeze(2).to_broadcast([P, NT, EXPERTS]), ALU.mult)
                dve.drain()
                full = [P, NT, EXPERTS, EXPERTS]
                mine, other = pr[:, :, :].unsqueeze(3).to_broadcast(full), pr[:, :, :].unsqueeze(2).to_broadcast(full)
                nc.vector.tensor_tensor(cmp1[:, :, :, :], other, mine, ALU.is_equal)
                nc.vector.tensor_tensor(cmp2[:, :, :, :], other, mine, ALU.is_gt)
                dve.drain()
                nc.vector.tensor_tensor(cmp1[:, :, :, :], cmp1[:, :, :, :], earlier.unsqueeze(1).to_broadcast(full), ALU.mult)
                dve.drain()
                nc.vector.tensor_tensor(cmp1[:, :, :, :], cmp1[:, :, :, :], cmp2[:, :, :, :], ALU.add)
                dve.drain()
                nc.vector.tensor_reduce(out=tv[:, :, :], in_=cmp1[:, :, :, :], axis=AX.X, op=ALU.add)
                dve.drain()
                nc.vector.scalar_tensor_tensor(tv[:, :, :], tv[:, :, :], 1.5, pr[:, :, :], ALU.is_lt, ALU.mult)
                dve.drain()
                nc.vector.tensor_reduce(out=top[:, :], in_=tv[:, :, :], axis=AX.X, op=ALU.add)
                dve.drain()
                nc.vector.tensor_scalar(top[:, :], top[:, :], 1e-8, None, ALU.add)
                dve.drain()
                nc.vector.reciprocal(top[:, :], top[:, :])
                dve.drain()
                nc.vector.tensor_tensor(wts[:, :, :], tv[:, :, :], top[:, :].unsqueeze(2).to_broadcast([P, NT, EXPERTS]), ALU.mult)
                dve.drain()

            def multiply(i, p):
                b = 2 * i + p
                dve.wait_ge(up_ready, b * n_up + up_at["e1b"] + 1)
                dve.wait_ge(hidden_ready, b * n_act + act_at["e1a"] + 1)
                for c in range(HC2):
                    last = nc.vector.tensor_tensor(hid["H1"][:, c, :], hid["S1"][:, c, :], up_banks[up_at["e1b"] % 2][c][:, :], ALU.mult)
                last.then_inc(h1_ready, 1)

            def combine(i, p, n_out):
                b, e = 2 * i + p, MOE_OUTS[n_out]
                dve.wait_ge(out_ready, b * EXPERTS + n_out + 1)
                for t in range(NT):
                    acc = XL[:, b * NT + t, MASKED:D]
                    last = nc.vector.scalar_tensor_tensor(acc, out_bank[n_out % 2][:, t * WIDE:(t + 1) * WIDE],
                                                          wts[:, t, e:e + 1], acc, ALU.mult, ALU.add)
                last.then_inc(out_taken, 1)
                dve.drain()

            def y_stats(i, p):
                layer_stats(nc, dve, tiles(XL, 2 * i + p), stats2, moments2[:, p, :, :])
                nc.vector.tensor_scalar(ve[:, p, 1, :], moments2[:, p, :, 1], LN_EPS, None, ALU.add).then_inc(var2, 1)
                dve.drain()

            def normalise_y(i, p):
                b = 2 * i + p
                dve.wait_ge(rstd2, b + 1)
                dve.wait_ge(added, counted(b - 1))
                for t in range(NT):
                    last = nc.vector.tensor_scalar(z[:, p, t, :], XL[:, b * NT + t, :], moments2[:, p, t, 0:1], rstd[:, p, 1, t:t + 1],
                                                   ALU.subtract, ALU.mult)
                last.then_inc(z_ready, 1)
                dve.drain()

            pipeline(dve, STAGES, (3, multiply), (3, weights), (3, lambda i, p: combine(i, p, 0)), (2, split_x), (5, normalise_y), (0, f_stats),
                     (1, scale), (3, split_g2), (3, lambda i, p: combine(i, p, 1)), (2, differences), (4, y_stats),
                     (3, lambda i, p: combine(i, p, 2)), (3, lambda i, p: combine(i, p, 3)))


CHUNK = 16
CHUNKS = T // CHUNK
SETS = 2


def spectral_layer(nc, io, X, XL, const, ident, minus_half, bank, sb, sem, scratch, w):
    WaT, WBT, WCT, cols, skip_w, out_b = w["WaT"], w["WBT"], w["WCT"], w["ssm_cols"], w["skip_w"], w["out_b"]
    ones = sb("s3_ones", [P, P])
    stats, moments = sb("s3_stats", [P, NT, 6]), sb("s3_moments", [P, 2, NT, 2])
    ve, rstd = sb("s3_ve", [P, 2, 2, NT]), sb("s3_rstd", [P, 2, 2, NT])
    xn, xnT = sb("s3_xn", [P, 2, NT, D]), sb("s3_xnT", [P, 2, T])
    a_in, u_in = sb("s3_a", [P, 4, T]), sb("s3_u", [P, 4, T])
    A = sb("s3_A", [P, 2, SETS, T])
    HP = sb("s3_HP", [P, 4, SETS * CHUNKS, CHUNK])
    squares, mag = sb("s3_squares", [P, 2, SETS, T]), sb("s3_mag", [P, SETS, T])
    An, Un, Hn, gn = (sb(f"s3_{x}", [8, SETS, T]) for x in ("An", "Un", "Hn", "gn"))
    two = sb("s3_two", [P, 1])
    by, ends = sb("s3_by", [P, 3, 4, SETS * CHUNKS]), sb("s3_ends", [P, 2, 4, SETS * CHUNKS])
    gamma_ready = sem("s3_gamma")
    var1, rstd1 = sem("s3_var1"), sem("s3_rstd1")
    xn_ready, turned, xnT_ready, au_ready, au_taken = (sem(f"s3_{x}") for x in ("xn_ready", "turned", "xnT_ready", "au_ready", "au_taken"))
    xnT_bank, a_bank, u_bank = bank[0], bank[1], bank[2]

    with nc.Block() as block:
        @block.vector
        def _(dve):
            dve.wait_ge(gamma_ready, 1)

            def x_stats(i, p):
                q = p % 2
                layer_stats(nc, dve, tiles(X, 4 * i + p), stats, moments[:, q, :, :])
                nc.vector.tensor_scalar(ve[:, q, 0, :], moments[:, q, :, 1], LN_EPS, None, ALU.add)
                nc.vector.tensor_scalar(ve[:, q, 1, :], moments[:, q, :, 1], 1.0 + LN_EPS, LN_EPS * LN_EPS, ALU.mult,
                                        ALU.add).then_inc(var1, 1)
                dve.drain()

            def normalise(i, p):
                b, q = 4 * i + p, p % 2
                dve.wait_ge(rstd1, b + 1)
                dve.wait_ge(turned, counted(b - 1))
                for t in range(NT):
                    nc.vector.tensor_scalar(XL[:, b * NT + t, :], X[:, b * NT + t, :], moments[:, q, t, 0:1], rstd[:, q, 0, t:t + 1],
                                            ALU.subtract, ALU.mult)
                    last = nc.vector.tensor_scalar(xn[:, q, t, :], X[:, b * NT + t, :], moments[:, q, t, 0:1], rstd[:, q, 1, t:t + 1],
                                                   ALU.subtract, ALU.mult)
                last.then_inc(xn_ready, 1)
                dve.drain()

            def times_gamma(i, p):
                if p == 3:
                    dve.wait_ge(au_taken, i + 1)
                    nc.vector.tensor_scalar(a_in[:, i, :], a_in[:, i, :], cols[:, 5:6], None, ALU.mult)

            pipeline(dve, 5, (2, normalise), (0, x_stats), (4, times_gamma), unroll=4)

        @block.gpsimd
        def _(pool):
            def invert(i, p):
                q = p % 2
                pool.wait_ge(var1, 4 * i + p + 1)
                nc.gpsimd.tensor_tensor(rstd[:, q, :, :], ve[:, q, :, :], minus_half[:, 0:2 * NT].rearrange("p (a t) -> p a t", a=2),
                                        ALU.pow).then_inc(rstd1, 1)

            pipeline(pool, 5, (0, invert), unroll=4)

        @block.scalar
        def _(act):
            nc.scalar.activation(cols[:, 5:6], cols[:, 4:5], ACT.Sigmoid).then_inc(gamma_ready, 1)

            def copy_xnT(i, p):
                b = 4 * i + p
                act.wait_ge(turned, b + 1)
                act.wait_ge(au_ready, counted(b - 1))
                nc.scalar.activation(xnT[:, p % 2, :], xnT_bank[:, :], ACT.Identity, scale=cols[:, 0:1], bias=cols[:, 1:2]).then_inc(xnT_ready, 1)

            def take(i, p):
                if p == 3:
                    act.wait_ge(au_ready, 4 * i + 4)
                    nc.scalar.activation(u_in[:, i, :], u_bank[:, :], ACT.Identity, bias=cols[:, 3:4])
                    nc.scalar.activation(a_in[:, i, :], a_bank[:, :], ACT.Tanh, bias=cols[:, 2:3]).then_inc(au_taken, 1)

            pipeline(act, 5, (3, take), (2, copy_xnT), unroll=4)

        @block.tensor
        def _(pe):
            def turn(i, p):
                b = 4 * i + p
                pe.wait_ge(xn_ready, b + 1)
                pe.wait_ge(xnT_ready, b)
                for t in range(NT):
                    last = nc.tensor.transpose(xnT_bank[:, t * P:(t + 1) * P], xn[:, p % 2, t, :], ident)
                last.then_inc(turned, 1)

            def project(i, p):
                pe.wait_ge(xnT_ready, 4 * i + p + 1)
                pe.wait_ge(au_taken, i)
                rows = slice(STATE * p, STATE * (p + 1))
                nc.tensor.matmul(a_bank[rows, :], WaT[:, :], xnT[:, p % 2, :], start=True, stop=True)
                nc.tensor.matmul(u_bank[rows, :], WBT[:, :], xnT[:, p % 2, :], start=True, stop=True).then_inc(au_ready, 1)

            pipeline(pe, 5, (3, project), (2, turn), unroll=4)

    spec_ready, spec_taken, squared, mag2_ready = sem("s3_spec_ready"), sem("s3_spec_taken"), sem("s3_squared"), sem("s3_mag2")
    mag_ready, clamped, gate_ready = sem("s3_mag_ready"), sem("s3_clamped"), sem("s3_gate")
    re, im = const_part(const, "dft_re"), const_part(const, "dft_im")
    ny = const_part(const, "dft_ny")
    hp_h = HP[:, :, :, :].rearrange("p (c k) m s -> p c k (m s)", c=2)
    with nc.Block() as block:
        @block.tensor
        def _(pe):
            for n, (src, mat) in enumerate(((a_in, re), (a_in, im), (u_in, re), (u_in, im))):
                for s in range(SETS):
                    for half in range(2):
                        last = nc.tensor.matmul(bank[2 * n + s][:, :], mat[:, half * P:(half + 1) * P], src[:, 2 * s + half, :],
                                                start=(half == 0), stop=(half == 1))
                    last.then_inc(spec_ready, 1)
            for n, src in enumerate((a_in, u_in)):
                for s in range(SETS):
                    pe.wait_ge(spec_taken, 2 * n + s + 1)
                    for half in range(2):
                        last = nc.tensor.matmul(bank[2 * n + s][0:8, :], ny[:, half * 8:half * 8 + 8], src[:, 2 * s + half, :],
                                                start=(half == 0), stop=(half == 1))
                    last.then_inc(spec_ready, 1)

        @block.scalar
        def _(act):
            for n in range(4):
                for s in range(SETS):
                    act.wait_ge(spec_ready, 2 * n + s + 1)
                    dst = A[:, n % 2, s, :] if n < 2 else hp_h[:, n % 2, 0, s * T:(s + 1) * T]
                    nc.scalar.activation(dst, bank[2 * n + s][:, :], ACT.Copy).then_inc(spec_taken, 1)
                if n == 1:
                    act.drain()
                    nc.scalar.activation(squares[:, :, :, :], A[:, :, :, :], ACT.Square).then_inc(squared, 1)
            for n, dst in enumerate((An, Un)):
                for s in range(SETS):
                    act.wait_ge(spec_ready, 8 + 2 * n + s + 1)
                    nc.scalar.activation(dst[:, s, :], bank[2 * n + s][0:8, :], ACT.Copy)
            act.drain()
            nc.scalar.activation(gn[:, :, :], An[:, :, :], ACT.Abs)
            act.wait_ge(mag2_ready, 1)
            nc.scalar.activation(mag[:, :, :], squares[:, 0, :, :], ACT.Sqrt).then_inc(mag_ready, 1)
            act.wait_ge(clamped, 1)
            nc.scalar.activation(mag[:, :, :], mag[:, :, :], ACT.Sigmoid, scale=-2.0, bias=two[:, :])
            nc.scalar.activation(gn[:, :, :], gn[:, :, :], ACT.Sigmoid, scale=-2.0, bias=two[0:8, :]).then_inc(gate_ready, 1)


        @block.vector
        def _(dve):
            nc.vector.memset(two[:, :], 2.0)
            nc.vector.memset(ones[:, :], 1.0)
            nc.vector.memset(HP[:, :, :, :].rearrange("p (c k) m s -> p c k (m s)", c=2)[:, :, 1, :], 0.0)
            dve.wait_ge(squared, 1)
            nc.vector.tensor_tensor(squares[:, 0, :, :], squares[:, 0, :, :], squares[:, 1, :, :], ALU.add).then_inc(mag2_ready, 1)
            dve.wait_ge(mag_ready, 1)
            nc.vector.tensor_scalar(mag[:, :, :], mag[:, :, :], 1e-8, None, ALU.max)
            nc.vector.tensor_scalar(gn[:, :, :], gn[:, :, :], 1e-8, None, ALU.max).then_inc(clamped, 1)
            dve.wait_ge(gate_ready, 1)
            dve.wait_ge(spec_taken, 8)
            for c in range(2):
                nc.vector.tensor_tensor(A[:, c, :, :], A[:, c, :, :], mag[:, :, :], ALU.mult)
            nc.vector.tensor_tensor(An[:, :, :], An[:, :, :], gn[:, :, :], ALU.mult)
            dve.drain()
            for s in range(SETS):
                nc.vector.tensor_tensor_scan(Hn[:, s, :], An[:, s, :], Un[:, s, :], 0.0, ALU.mult, ALU.add)
            Am = A[:, :, :, :].rearrange("p c s (k t) -> p c (s k) t", t=CHUNK)
            M = SETS * CHUNKS
            by_re, by_im, step = by[:, 0, :, :], by[:, 1, :, :], by[:, 2, :, :]

            def times(dst, left_re, left_im, right):
                nc.vector.tensor_tensor(dst[0], left_re, right, ALU.mult)
                nc.vector.tensor_tensor(dst[1], left_im, right, ALU.mult)
                dve.drain()
                nc.vector.tensor_tensor(dst[2][:, 0:2], dst[0][:, 0:2], dst[1][:, 2:4], ALU.subtract)
                nc.vector.tensor_tensor(dst[2][:, 2:4], dst[0][:, 2:4], dst[1][:, 0:2], ALU.add)
                dve.drain()

            for c in range(2):
                nc.vector.tensor_copy(HP[:, 2 * c + 1, :, 0], Am[:, c, :, 0])
            dve.drain()
            for s in range(1, CHUNK):
                times((by_re, by_im, step), Am[:, 0, :, s].unsqueeze(1).to_broadcast([P, 4, M]),
                      Am[:, 1, :, s].unsqueeze(1).to_broadcast([P, 4, M]), HP[:, :, :, s - 1])
                nc.vector.tensor_tensor(HP[:, :, :, s], HP[:, :, :, s], step, ALU.add)
                dve.drain()
            nc.vector.tensor_copy(ends[:, 0, :, :], HP[:, :, :, CHUNK - 1])
            dve.drain()
            now, d = 0, 1
            while d < CHUNKS:
                cur, new = (ends[:, n, :, :].rearrange("p q (s k) -> p q s k", s=SETS) for n in (now, 1 - now))
                n = CHUNKS - d
                v = [by[:, m, :, :].rearrange("p q (s k) -> p q s k", s=SETS)[:, :, :, 0:n] for m in range(3)]
                for s in range(SETS):
                    times([x[:, :, s, :] for x in v], cur[:, 1, s, d:].unsqueeze(1).to_broadcast([P, 4, n]),
                          cur[:, 3, s, d:].unsqueeze(1).to_broadcast([P, 4, n]), cur[:, :, s, 0:n])
                for c in range(2):
                    nc.vector.tensor_tensor(new[:, 2 * c, :, d:], cur[:, 2 * c, :, d:], v[2][:, 2 * c], ALU.add)
                    nc.vector.tensor_copy(new[:, 2 * c + 1, :, d:], v[2][:, 2 * c + 1])
                nc.vector.tensor_copy(new[:, :, :, 0:d], cur[:, :, :, 0:d])
                dve.drain()
                now, d = 1 - now, 2 * d
            flat = squares[:, :, :, :].rearrange("p c s (k t) -> p c s k t", t=CHUNK)
            hp5 = HP[:, :, :, :].rearrange("p q (s k) t -> p q s k t", s=SETS)
            carry = ends[:, now, :, :].rearrange("p q (s k) -> p q s k", s=SETS)
            n = CHUNKS - 1
            for c in range(2):
                for half, (x, y) in enumerate(((1, 2 * c), (3, 2 - 2 * c))):
                    nc.vector.tensor_tensor(flat[:, half, :, 1:, :], hp5[:, x, :, 1:, :],
                                            carry[:, y, :, 0:n].unsqueeze(3).to_broadcast([P, SETS, n, CHUNK]), ALU.mult)
                dve.drain()
                nc.vector.tensor_tensor(flat[:, 0, :, 1:, :], flat[:, 0, :, 1:, :], flat[:, 1, :, 1:, :],
                                        ALU.subtract if c == 0 else ALU.add)
                dve.drain()
                nc.vector.tensor_tensor(hp5[:, 2 * c, :, 1:, :], hp5[:, 2 * c, :, 1:, :], flat[:, 0, :, 1:, :], ALU.add)
                dve.drain()


    hT = sb("s3_hT", [P, 2, T])
    skip = xn
    y, z = (a_in[:, half:half + 2, :].rearrange("p q (t f) -> p q t f", t=NT) for half in (0, 2))
    stats2, moments2 = sb("s3_stats2", [P, NT, 6]), sb("s3_moments2", [P, 2, NT, 2])
    h_ready, h_taken, y_ready, y_taken = (sem(f"s3_{x}") for x in ("h_ready", "h_taken", "y_ready", "y_taken"))
    skip_ready, var2, rstd2, z_ready, added = (sem(f"s3_{x}") for x in ("skip_ready", "var2", "rstd2", "z_ready", "added"))
    ire, iim, iny = const_part(const, "inv_re"), const_part(const, "inv_im"), const_part(const, "inv_ny", 8)
    h_bank, y_bank = bank[0:2], bank[2:4]
    with nc.Block() as block:
        @block.tensor
        def _(pe):
            def states(i, p):
                half = p // 4
                if p % 4 == 0:
                    lhs = slice(half * P, (half + 1) * P)
                    pe.wait_ge(h_taken, counted(2 * i + half - 1))
                    nc.tensor.matmul(h_bank[half][:, :], ire[:, lhs], hp_h[:, 0, 0, bass.ds(i * T, T)], start=True, stop=False)
                    nc.tensor.matmul(h_bank[half][:, :], iim[:, lhs], hp_h[:, 1, 0, bass.ds(i * T, T)], start=False, stop=False)
                    nc.tensor.matmul(h_bank[half][:, :], iny[:, lhs], Hn[:, i, :], start=False, stop=True).then_inc(h_ready, 1)

            def output(i, p):
                b, j, half = 8 * i + p, p % 4, p // 4
                pe.wait_ge(h_taken, 2 * i + half + 1)
                pe.wait_ge(y_taken, counted(b - 1))
                rows = slice(STATE * j, STATE * (j + 1))
                row = slice(STATE * j, STATE * j + 1)
                nc.tensor.matmul(y_bank[p % 2][:, :], ones[row, :], out_b[row, :], start=True, stop=False)
                for t in range(NT):
                    last = nc.tensor.matmul(y_bank[p % 2][:, t * P:(t + 1) * P], hT[rows, half, t * P:(t + 1) * P], WCT[rows, :],
                                            start=False, stop=(t == NT - 1))
                last.then_inc(y_ready, 1)

            pipeline(pe, 4, (1, output), (0, states), unroll=8)

        @block.scalar
        def _(act):
            def take(i, p):
                half = p // 4
                if p % 4 == 0:
                    act.wait_ge(h_ready, 2 * i + half + 1)
                    act.wait_ge(y_ready, counted(8 * i + 4 * half - 4))
                    nc.scalar.activation(hT[:, half, :], h_bank[half][:, :], ACT.Copy).then_inc(h_taken, 1)

            pipeline(act, 4, (0, take), unroll=8)

        @block.gpsimd
        def _(pool):
            def skips(i, p):
                b = 8 * i + p
                pool.wait_ge(y_taken, counted(b - 1))
                nc.gpsimd.tensor_tensor(skip[:, p % 2, :, :], tiles(XL, b), skip_w[:, :].unsqueeze(1).to_broadcast([P, NT, D]),
                                        ALU.mult).then_inc(skip_ready, 1)

            def invert(i, p):
                pool.wait_ge(var2, 8 * i + p + 1)
                nc.gpsimd.tensor_tensor(rstd[:, p % 2, 1, :], ve[:, p % 2, 1, :], minus_half[:, 0:NT], ALU.pow).then_inc(rstd2, 1)

            def add(i, p):
                b = 8 * i + p
                pool.wait_ge(z_ready, b + 1)
                nc.gpsimd.tensor_tensor(tiles(X, b), tiles(X, b), z[:, p % 2, :, :], ALU.add).then_inc(added, 1)

            pipeline(pool, 4, (0, skips), (2, invert), (3, add), unroll=8)

        @block.vector
        def _(dve):
            def add_skip(i, p):
                b, q = 8 * i + p, p % 2
                dve.wait_ge(y_ready, b + 1)
                dve.wait_ge(skip_ready, b + 1)
                nc.vector.tensor_tensor(y[:, q, :, :], y_bank[q][:, :].rearrange("p (t f) -> p t f", t=NT), skip[:, q, :, :],
                                        ALU.add).then_inc(y_taken, 1)
                dve.drain()
                layer_stats(nc, dve, y[:, q, :, :], stats2, moments2[:, q, :, :])
                nc.vector.tensor_scalar(ve[:, q, 1, :], moments2[:, q, :, 1], LN_EPS, None, ALU.add).then_inc(var2, 1)
                dve.drain()

            def normalise_y(i, p):
                b, q = 8 * i + p, p % 2
                dve.wait_ge(rstd2, b + 1)
                dve.wait_ge(added, counted(b - 1))
                for t in range(NT):
                    last = nc.vector.tensor_scalar(z[:, q, t, :], y[:, q, t, :], moments2[:, q, t, 0:1], rstd[:, q, 1, t:t + 1],
                                                   ALU.subtract, ALU.mult)
                last.then_inc(z_ready, 1)
                dve.drain()

            pipeline(dve, 4, (2, add_skip), (3, normalise_y), unroll=8)


def swiglu_layer(nc, io, X, XL, const, ident, minus_half, bank, sb, sem, scratch, w):
    HC = HIDDEN // P
    STAGES = 7
    wd, wg_parts, wu_parts = w["wd"], w["parts"]["wg"], w["parts"]["wu"]
    stats, moments = sb("s4_stats", [P, NT, 6]), sb("s4_moments", [P, 2, 2, NT, 2])
    stats2 = sb("s4_stats2", [P, NT, 6])
    ve, rstd = sb("s4_ve", [P, 2, 2, NT]), sb("s4_rstd", [P, 2, 2, NT])
    xl, z = sb("s4_xl", [P, 2, NT, D]), sb("s4_z", [P, 2, NT, D])
    xT, yT = sb("s4_xT", [P, 2, T]), sb("s4_yT", [P, 2, T])
    x_parts = [sb(f"s4_x_part{n}", [P, 2, T], F32R) for n in range(2)]
    x_high, x_split = sem("s4_x_high"), sem("s4_x_split")
    silu, hid = sb("s4_silu", [P, 2, T]), sb("s4_hid", [P, 2, HC, T])
    var1, rstd1, var2, rstd2 = sem("s4_var1"), sem("s4_rstd1"), sem("s4_var2"), sem("s4_rstd2")
    xl_ready, turned, xT_ready = sem("s4_xl_ready"), sem("s4_turned"), sem("s4_xT_ready")
    gate_ready, up_ready, silu_ready = sem("s4_gate_ready"), sem("s4_up_ready"), sem("s4_silu_ready")
    hid_ready, yT_ready, yT_copied, y_ready = sem("s4_hid_ready"), sem("s4_yT_ready"), sem("s4_yT_copied"), sem("s4_y_ready")
    z_ready, added, stored = sem("s4_z_ready"), sem("s4_added"), sem("s4_stored")
    xT_bank, yT_bank, y_bank, gate_bank, up_bank = bank[0], bank[1], bank[2:4], bank[4:6], bank[6:8]
    out_dram = io["out"].rearrange("b (t p) f -> p (b t) f", p=P)

    with nc.Block() as block:
        @block.sync
        def _(sp):
            with sp.Fori(0, B) as b:
                sp.wait_ge(added, b + 1)
                sp.dma_start(out_dram[:, bass.ds(b * NT, NT), :], tiles(X, b)).then_inc(stored, 16)
            sp.wait_ge(stored, 16 * B)

        @block.vector
        def _(dve):
            def split_high(i, p):
                b = 2 * i + p
                dve.wait_ge(xT_ready, b + 1)
                dve.wait_ge(up_ready, counted(HC * (b - 1)))
                keep_high(nc.vector, x_parts[0][:, p, :], xT[:, p, :]).then_inc(x_high, 1)

            def x_stats(i, p):
                b = 2 * i + p
                layer_stats(nc, dve, tiles(X, b), stats, moments[:, p, 0, :, :])
                nc.vector.tensor_scalar(ve[:, p, 0, :], moments[:, p, 0, :, 1], LN_EPS, None, ALU.add).then_inc(var1, 1)
                dve.drain()

            def normalise(i, p):
                b = 2 * i + p
                dve.wait_ge(rstd1, b + 1)
                dve.wait_ge(turned, counted(b - 1))
                for t in range(NT):
                    last = nc.vector.tensor_scalar(xl[:, p, t, :], X[:, b * NT + t, :], moments[:, p, 0, t, 0:1],
                                                   rstd[:, p, 0, t:t + 1], ALU.subtract, ALU.mult)
                last.then_inc(xl_ready, 1)
                dve.drain()

            def gate(i, p, c):
                b = 2 * i + p
                dve.wait_ge(yT_ready, counted(b - 1))
                dve.wait_ge(silu_ready, HC * b + c + 1)
                dve.wait_ge(up_ready, HC * b + c + 1)
                nc.vector.tensor_tensor(hid[:, p, c, :], silu[:, (p + c) % 2, :], up_bank[(p + c) % 2][:, :], ALU.mult).then_inc(hid_ready, 1)

            def y_stats(i, p):
                b = 2 * i + p
                dve.wait_ge(y_ready, b + 1)
                layer_stats(nc, dve, y_bank[p][:, :].rearrange("p (t f) -> p t f", t=NT), stats2, moments[:, p, 1, :, :])
                nc.vector.tensor_scalar(ve[:, p, 1, :], moments[:, p, 1, :, 1], LN_EPS, None, ALU.add).then_inc(var2, 1)
                dve.drain()

            def normalise_y(i, p):
                b = 2 * i + p
                dve.wait_ge(rstd2, b + 1)
                dve.wait_ge(added, counted(b - 1))
                for t in range(NT):
                    last = nc.vector.tensor_scalar(z[:, p, t, :], y_bank[p][:, t * P:(t + 1) * P], moments[:, p, 1, t, 0:1],
                                                   rstd[:, p, 1, t:t + 1], ALU.subtract, ALU.mult)
                last.then_inc(z_ready, 1)
                dve.drain()

            pipeline(dve, STAGES, (2, split_high), (3, lambda i, p: gate(i, p, 0)), (1, normalise),
                     (3, lambda i, p: gate(i, p, 1)), (6, normalise_y), (3, lambda i, p: gate(i, p, 2)), (0, x_stats), (5, y_stats))

        @block.gpsimd
        def _(pool):
            def split_low(i, p):
                pool.wait_ge(x_high, 2 * i + p + 1)
                keep_low(nc.gpsimd, x_parts[1][:, p, :], xT[:, p, :], x_parts[0][:, p, :]).then_inc(x_split, 1)

            def invert_x(i, p):
                pool.wait_ge(var1, 2 * i + p + 1)
                nc.gpsimd.tensor_tensor(rstd[:, p, 0, :], ve[:, p, 0, :], minus_half[:, 0:NT], ALU.pow).then_inc(rstd1, 1)

            def invert_y(i, p):
                pool.wait_ge(var2, 2 * i + p + 1)
                nc.gpsimd.tensor_tensor(rstd[:, p, 1, :], ve[:, p, 1, :], minus_half[:, 0:NT], ALU.pow).then_inc(rstd2, 1)

            def add(i, p):
                b = 2 * i + p
                pool.wait_ge(z_ready, b + 1)
                nc.gpsimd.tensor_tensor(tiles(X, b), tiles(X, b), z[:, p, :, :], ALU.add).then_inc(added, 1)

            pipeline(pool, STAGES, (2, split_low), (0, invert_x), (6, add), (5, invert_y))

        @block.scalar
        def _(act):
            def copy_xT(i, p):
                b = 2 * i + p
                act.wait_ge(turned, b + 1)
                act.wait_ge(x_split, counted(b - 1))
                nc.scalar.activation(xT[:, p, :], xT_bank[:, :], ACT.Copy).then_inc(xT_ready, 1)

            def silus(i, p):
                b = 2 * i + p
                for c in range(HC):
                    act.wait_ge(gate_ready, HC * b + c + 1)
                    act.wait_ge(hid_ready, counted(HC * b + c - 1))
                    nc.scalar.activation(silu[:, (p + c) % 2, :], gate_bank[(p + c) % 2][:, :], ACT.Silu).then_inc(silu_ready, 1)

            def copy_yT(i, p):
                b = 2 * i + p
                act.wait_ge(yT_ready, b + 1)
                act.wait_ge(y_ready, counted(b - 1))
                nc.scalar.activation(yT[:, p, :], yT_bank[:, :], ACT.Copy).then_inc(yT_copied, 1)

            pipeline(act, STAGES, (3, silus), (1, copy_xT), (4, copy_yT))

        @block.tensor
        def _(pe):

            def turn(i, p):
                b = 2 * i + p
                pe.wait_ge(xl_ready, b + 1)
                pe.wait_ge(xT_ready, b)
                for t in range(NT):
                    last = nc.tensor.transpose(xT_bank[:, t * P:(t + 1) * P], xl[:, p, t, :], ident)
                last.then_inc(turned, 1)

            def gate_and_up(i, p):
                b = 2 * i + p
                pe.wait_ge(x_split, b + 1)
                for c in range(HC):
                    cols = slice(c * P, (c + 1) * P)
                    pe.wait_ge(silu_ready, counted(HC * b + c - 1))
                    for n, (wp, xp) in enumerate(((0, 0), (0, 1), (1, 0))):
                        last = nc.tensor.matmul(gate_bank[(p + c) % 2][:, :], wg_parts[wp][:, cols],
                                                x_parts[xp][:, p, :], start=(n == 0), stop=(n == 2))
                    last.then_inc(gate_ready, 1)
                    pe.wait_ge(hid_ready, counted(HC * b + c - 1))
                    for n, (wp, xp) in enumerate(((0, 0), (0, 1), (1, 0))):
                        last = nc.tensor.matmul(up_bank[(p + c) % 2][:, :], wu_parts[wp][:, cols],
                                                x_parts[xp][:, p, :], start=(n == 0), stop=(n == 2))
                    last.then_inc(up_ready, 1)

            def down(i, p):
                b = 2 * i + p
                pe.wait_ge(hid_ready, HC * (b + 1))
                pe.wait_ge(yT_copied, b)
                for c in range(HC):
                    last = nc.tensor.matmul(yT_bank[:, :], wd[:, c, :], hid[:, p, c, :], start=(c == 0), stop=(c == HC - 1))
                last.then_inc(yT_ready, 1)

            def turn_y(i, p):
                b = 2 * i + p
                pe.wait_ge(yT_copied, b + 1)
                pe.wait_ge(z_ready, counted(b - 1))
                for t in range(NT):
                    last = nc.tensor.transpose(y_bank[p][:, t * P:(t + 1) * P], yT[:, p, t * P:(t + 1) * P], ident)
                last.then_inc(y_ready, 1)

            pipeline(pe, STAGES, (3, gate_and_up), (5, turn_y), (1, turn), (4, down))


PHASES = [first_layer, qkv_layer, attention_layer, expert_layer, spectral_layer, swiglu_layer]


def build(nc, io):
    with ExitStack() as whole:
        def sb(name, shape, dt=F32, ctx=whole):
            return ctx.enter_context(nc.sbuf_tensor(name, shape, dt))

        X = sb("X", [P, TILES, D])
        XL = sb("XL", [P, TILES, D])
        const = sb("const", [P, NCONST])
        ident = const[:, COLS["ident"][0]:COLS["ident"][1]]
        minus_half = sb("minus_half", [P, 16])
        bank = [whole.enter_context(nc.psum_tensor(f"bank{n}", [P, 512], F32)) for n in range(8)]
        stack = nc.dram_tensor("qk_parts", (B, 3, 2, P, T), BF16, kind="Internal").ap()
        values = nc.dram_tensor("v_ones", (B, P, NT * HEADS * (HD + 1)), F32, kind="Internal").ap()
        w = weight_tiles(sb)
        common = dict(w=w, scratch=(stack, values), nc=nc, io=io, X=X, XL=XL, const=const, ident=ident, minus_half=minus_half, bank=bank)
        keys = whole.enter_context(ExitStack())
        w["K"] = sb("K", [P, 2, 2, PAIRS, T], BF16, keys)
        for phase in PHASES:
            if phase is expert_layer:
                keys.close()
            with ExitStack() as ctx:
                phase(sb=lambda name, shape, dt=F32, ctx=ctx: sb(name, shape, dt, ctx),
                      sem=lambda name, ctx=ctx: ctx.enter_context(nc.semaphore(name)), **common)


def laid_out(v):
    col = np.ascontiguousarray
    t = lambda a: col(np.asarray(a).T)
    a = {k: np.asarray(x) for k, x in v.items()}
    perm = np.array([(2 * pair + par) * HD + d for par in range(2) for d in range(HD) for pair in range(PAIRS)])
    dims = np.array([d for par in range(2) for d in range(HD) for pair in range(PAIRS)])
    return {
        "WqT": t(a["L0_ffn_wq"])[:, perm], "WkT": t(a["L0_ffn_wk"])[:, perm], "WvT": t(a["L0_ffn_wv"]),
        "WoT": t(a["L0_ffn_wo"])[:, MASKED:], "n1_w": a["L0_ffn_n1_w"], "qn_w": a["L0_ffn_qn_w"][dims],
        "kn_w": a["L0_ffn_kn_w"][dims], "n2_w": a["L0_ffn_n2_w"], "gateT": t(a["L0_ffn_gate_w"]),
        "e0uT": t(a["L0_ffn_e0_up"]), "e1aT": t(a["L0_ffn_e1_w1"]), "e1bT": t(a["L0_ffn_e1_w2"]),
        "e2aT": t(a["L0_ffn_e2_l1"]), "e2bT": t(a["L0_ffn_e2_l2"]), "e2cT": t(a["L0_ffn_e2_l3"]),
        "e3aT": t(a["L0_ffn_e3_down"]), "e3bT": t(a["L0_ffn_e3_up"]),
        "d0T": t(a["L0_ffn_e0_down"])[:, MASKED:], "d1T": t(a["L0_ffn_e1_down"])[:, MASKED:],
        "d2T": t(a["L0_ffn_e2_l4"])[:, MASKED:], "d3T": t(a["L0_ffn_e3_out"])[:, MASKED:],
        "x": a["L0_attn_x"], "A": a["L0_attn_A"], "BT": t(a["L0_attn_B"]), "WT": t(a["L0_attn_W"]), "b": a["L0_attn_b"],
        "WaT": t(a["L1_attn_Wa_w"]), "WBT": t(a["L1_attn_WB_w"]), "WCT4": np.tile(t(a["L1_attn_WC_w"]), (4, 1)),
        "ln_w": a["L1_attn_ln_w"], "ln_b": a["L1_attn_ln_b"], "Wa_b4": np.tile(a["L1_attn_Wa_b"], 4),
        "WB_b4": np.tile(a["L1_attn_WB_b"], 4), "log_gamma": a["L1_attn_log_gamma"].reshape(1),
        "D_skip": a["L1_attn_D_skip"], "WC_b": a["L1_attn_WC_b"],
        "w_gateT": t(a["L1_ffn_w_gate"]), "w_upT": t(a["L1_ffn_w_up"]), "w_downT": t(a["L1_ffn_w_down"]),
    }


def kernel(**inputs):
    import numpy as _np
    import concourse.bacc as _bacc
    from concourse import mybir as _mybir
    from concourse.bass_utils import run_bass_kernel_spmd as _run

    nc = _bacc.Bacc("TRN2", target_bir_lowering=False, num_devices=1)
    arrays, io = {}, {}
    for name, a in {**laid_out(inputs), "consts": constant_table()}.items():
        a = _np.ascontiguousarray(a)
        arrays[f"in_{name}"] = a
        io[name] = nc.dram_tensor(f"in_{name}", a.shape, _mybir.dt.from_np(a.dtype), kind="ExternalInput").ap()
    io["out"] = nc.dram_tensor("out_0", (B, T, D), _mybir.dt.float32, kind="ExternalOutput").ap()
    build(nc, io)
    r = _run(nc, [arrays], core_ids=[0])
    return r.results[0]["out_0"]
```
